# Optimizing a Trainium2 kernel written in Bass

```python
import numpy as np
import jax
import jax.numpy as jnp

def _softmax(x, axis=-1):
    return jax.nn.softmax(x, axis=axis)

def _gelu(x):
    return jax.nn.gelu(x, approximate=True)

def _silu(x):
    return jax.nn.silu(x)

def _sigmoid(x):
    return jax.nn.sigmoid(x)

def _layernorm(x, axis=-1, eps=1e-05):
    m = jnp.mean(x, axis=axis, keepdims=True)
    v = jnp.var(x, axis=axis, keepdims=True)
    return (x - m) / jnp.sqrt(v + eps)

def _scatter_add(tgt, idx, src, axis=0):
    return tgt.at[idx].add(src)

def _segment_sum(src, seg, n):
    return jax.ops.segment_sum(src, seg, n)
kernel_name = 'mk_decoder_preln_d2_seqx_r4_2d8516'

def setup_inputs(seed: int=0):
    np.random.seed(seed)
    _w = jnp.asarray

    def _rec_inputs():
        import jax
        import jax.numpy as jnp
        _rk = jax.random.key(seed)
        x = -0.0002928 + 1 * jax.random.normal(jax.random.fold_in(_rk, 1), (32, 128, 256), jnp.float32)
        _lenS = 128 - jax.random.randint(jax.random.fold_in(_rk, 7), (32,), 0, max(1, 128 // 4) + 1, jnp.int32)
        _lenS2 = 128 - jax.random.randint(jax.random.fold_in(_rk, 8), (32,), 0, max(1, 128 // 4) + 1, jnp.int32)
        _ctx_1024P = jax.random.normal(jax.random.fold_in(_rk, 11), (32, 16, 256), jnp.float32)
        _ctx_1024c = jax.random.dirichlet(jax.random.fold_in(_rk, 511), 0.3 * jnp.ones((16,), jnp.float32), (32, 128))
        _ctx_1024t = jnp.einsum('bsk,bkd->bsd', _ctx_1024c, _ctx_1024P)
        _ctx_1024t = _ctx_1024t * jax.lax.rsqrt(jnp.mean(jnp.square(_ctx_1024t)) + 1e-12) * 0.953939
        ctx_1024 = 4.13588e-05 + 0.999923 * (_ctx_1024t + 0.3 * jax.random.normal(jax.random.fold_in(_rk, 611), (32, 128, 256), jnp.float32))
        itok_BxS_8_8191 = jax.random.randint(jax.random.fold_in(_rk, 12), (32, 128), 8, 2048, jnp.int32)
        itok_BxS2_1_8191 = jax.random.randint(jax.random.fold_in(_rk, 13), (32, 128), 1, 2048, jnp.int32)
        _validS = jnp.arange(128)[None, :] < _lenS[:, None]
        _validS2 = jnp.arange(128)[None, :] < _lenS2[:, None]
        _causal = jnp.tril(jnp.ones((128, 128), dtype=bool))
        mask_BxSxS2_if1 = jnp.where(jnp.ones((32, 128, 128), dtype=bool), 1, 0).astype(jnp.int32)
        return (x, ctx_1024, itok_BxS_8_8191, itok_BxS2_1_8191, mask_BxSxS2_if1)
    x, ctx_1024, itok_BxS_8_8191, itok_BxS2_1_8191, mask_BxSxS2_if1 = _rec_inputs()

    def _L0_attn_setup():
        import jax, jax.numpy as jnp
        import numpy as np
        DIM = 256
        HEADS = 16
        DIM_HEAD = DIM // HEADS
        LATENT = DIM // 4
        SCALE = DIM_HEAD ** (-0.5)
        key = jax.random.key(seed)
        ks = jax.random.split(key, 8)
        B, S = (2, 512)
        init = lambda k, shape, fan_in: jax.random.normal(k, shape, jnp.float32) * fan_in ** (-0.5)
        return {'x': jax.random.normal(ks[0], (B, S, DIM), jnp.float32), 'Wq': init(ks[1], (DIM, DIM), DIM), 'bq': jnp.zeros((DIM,), jnp.float32), 'Wl': init(ks[2], (DIM, LATENT), DIM), 'bl': jnp.zeros((LATENT,), jnp.float32), 'Wk': init(ks[3], (LATENT, DIM), LATENT), 'bk': jnp.zeros((DIM,), jnp.float32), 'Wv': init(ks[4], (LATENT, DIM), LATENT), 'bv': jnp.zeros((DIM,), jnp.float32), 'Wo': init(ks[5], (DIM, DIM), DIM), 'bo': jnp.zeros((DIM,), jnp.float32)}
    _L0_attn_all = _L0_attn_setup()
    _L0_attn_in = {k: v for k, v in _L0_attn_all.items() if k in ('Wq', 'bq', 'Wl', 'bl', 'Wk', 'bk', 'Wv', 'bv', 'Wo', 'bo')}
    del _L0_attn_all

    def _L0_xattn_setup():
        import jax, jax.numpy as jnp
        import numpy as np
        DIM = 256
        NUM_HEADS = 16
        HEAD_DIM = DIM // NUM_HEADS

        def _slopes(num_heads):
            ratio = 2.0 ** (-8.0 / num_heads)
            return jnp.asarray([ratio ** i for i in range(1, num_heads + 1)], dtype=jnp.float32)
        key = jax.random.key(seed)
        ks = jax.random.split(key, 10)
        b, q_len, k_len = (2, 512, 1024)
        query = jax.random.normal(ks[0], (b, q_len, DIM), dtype=jnp.float32)
        keys = jax.random.normal(ks[1], (b, k_len, DIM), dtype=jnp.float32)
        values = jax.random.normal(ks[2], (b, k_len, DIM), dtype=jnp.float32)
        query_pos = jnp.sort(jax.random.randint(ks[3], (b, q_len), 0, 2048), axis=-1)
        key_pos = jnp.sort(jax.random.randint(ks[4], (b, k_len), 0, 2048), axis=-1)
        mask = jnp.ones((b, q_len, k_len), dtype=jnp.int32)
        lim = float(np.sqrt(6.0 / (DIM + DIM)))
        W_q = jax.random.uniform(ks[5], (DIM, DIM), minval=-lim, maxval=lim, dtype=jnp.float32)
        W_k = jax.random.uniform(ks[6], (DIM, DIM), minval=-lim, maxval=lim, dtype=jnp.float32)
        W_v = jax.random.uniform(ks[7], (DIM, DIM), minval=-lim, maxval=lim, dtype=jnp.float32)
        W_o = jax.random.uniform(ks[8], (DIM, DIM), minval=-lim, maxval=lim, dtype=jnp.float32)
        return {'query': query, 'keys': keys, 'values': values, 'W_q': W_q, 'W_k': W_k, 'W_v': W_v, 'W_o': W_o, 'query_pos': query_pos, 'key_pos': key_pos, 'mask': mask}
    _L0_xattn_all = _L0_xattn_setup()
    _L0_xattn_in = {k: v for k, v in _L0_xattn_all.items() if k in ('W_q', 'W_k', 'W_v', 'W_o')}
    del _L0_xattn_all

    def _L0_ffn_setup():
        import jax, jax.numpy as jnp
        import numpy as np
        NEG_INF = jnp.float32(-1000000000.0)

        def _router(x, Wr, br, top_k=2):
            logits = jnp.einsum('bsd,de->bse', x, Wr) + br
            _, top_idx = jax.lax.top_k(logits, top_k)
            num_experts = logits.shape[-1]
            mask = jnp.any(top_idx[..., None] == jnp.arange(num_experts), axis=-2)
            sparse_logits = jnp.where(mask, logits, NEG_INF)
            weights = jax.nn.softmax(sparse_logits, axis=-1)
            return (weights, top_idx, mask)
        key = jax.random.key(seed)
        ks = jax.random.split(key, 8)
        B, S, D, E, H = (4, 512, 256, 8, 1024)
        sd = 1.0 / np.sqrt(D)
        sh = 1.0 / np.sqrt(H)
        x = jax.random.normal(ks[0], (B, S, D), dtype=jnp.float32)
        Wr = jax.random.normal(ks[1], (D, E), dtype=jnp.float32) * sd
        br = jnp.zeros((E,), dtype=jnp.float32)
        W1 = jax.random.normal(ks[2], (E, D, H), dtype=jnp.float32) * sd
        b1 = jnp.zeros((E, H), dtype=jnp.float32)
        W2 = jax.random.normal(ks[3], (E, H, D), dtype=jnp.float32) * sh
        b2 = jnp.zeros((E, D), dtype=jnp.float32)
        return {'x': x, 'Wr': Wr, 'br': br, 'W1': W1, 'b1': b1, 'W2': W2, 'b2': b2}
    _L0_ffn_all = _L0_ffn_setup()
    _L0_ffn_in = {k: v for k, v in _L0_ffn_all.items() if k in ('Wr', 'br', 'W1', 'b1', 'W2', 'b2')}
    del _L0_ffn_all

    def _L1_attn_setup():
        import jax, jax.numpy as jnp
        import numpy as np
        DIM = 256
        HEADS = 16
        HDIM = DIM // HEADS
        CHUNK = 64
        RES_SCALE = float(1.0 / np.sqrt(2.0))
        EPS_FP32 = float(np.finfo(np.float32).eps)

        def _rms(x, eps):
            return x * jax.lax.rsqrt(jnp.mean(x * x, axis=-1, keepdims=True) + eps)

        def _mixer(x, in_proj_w, out_proj_w):
            B, S, D = x.shape
            proj = x @ in_proj_w.T
            q, k, v, a, g = jnp.split(proj, 5, axis=-1)
            rs = lambda t: t.reshape(B, S, HEADS, HDIM)
            q, k, v, a, g = map(rs, (q, k, v, a, g))
            q = _rms(q, EPS_FP32)
            k = jnp.tanh(k)
            a = jnp.clip(jax.nn.sigmoid(a + 2.0), 0.6, 0.9995)
            u = k * v
            nC = S // CHUNK
            a_c = jnp.moveaxis(a.reshape(B, nC, CHUNK, HEADS, HDIM), 1, 0)
            u_c = jnp.moveaxis(u.reshape(B, nC, CHUNK, HEADS, HDIM), 1, 0)

            def step(state, inp):
                ac, uc = inp
                prefix = jnp.cumprod(ac, axis=1)
                acc = jnp.cumsum(uc / jnp.maximum(prefix, 1e-06), axis=1)
                states = prefix * (state[:, None] + acc)
                return (states[:, -1], states)
            state0 = jnp.zeros((B, HEADS, HDIM), jnp.float32)
            _, states = jax.lax.scan(step, state0, (a_c, u_c))
            memory = jnp.moveaxis(states, 0, 1).reshape(B, S, HEADS, HDIM)
            gate = jax.nn.sigmoid(g)
            y = gate * (q * memory) + (1.0 - gate) * v
            return y.reshape(B, S, D) @ out_proj_w.T
        key = jax.random.key(seed)
        ks = jax.random.split(key, 5)
        s = 0.02
        return {'x': jax.random.normal(ks[0], (2, 1024, DIM), jnp.float32), 'norm1_w': jnp.ones((DIM,), jnp.float32), 'norm2_w': jnp.ones((DIM,), jnp.float32), 'in_proj_w': jax.random.normal(ks[1], (5 * DIM, DIM), jnp.float32) * s, 'out_proj_w': jax.random.normal(ks[2], (DIM, DIM), jnp.float32) * s, 'fc_w': jax.random.normal(ks[3], (1024, DIM), jnp.float32) * s, 'proj_w': jax.random.normal(ks[4], (DIM, 1024), jnp.float32) * s}
    _L1_attn_all = _L1_attn_setup()
    _L1_attn_in = {k: v for k, v in _L1_attn_all.items() if k in ('norm1_w', 'norm2_w', 'in_proj_w', 'out_proj_w', 'fc_w', 'proj_w')}
    del _L1_attn_all

    def _L1_xattn_setup():
        import jax, jax.numpy as jnp
        import numpy as np
        C = 256
        B, HW, N = (8, 1024, 77)
        key = jax.random.key(seed)
        ks = jax.random.split(key, 14)
        s = 1.0 / np.sqrt(C)
        inp = {'vis_features': jax.random.normal(ks[0], (B, HW, C), jnp.float32), 'lang_features': jax.random.normal(ks[1], (B, N, C), jnp.float32), 'W_vk': jax.random.uniform(ks[2], (C, C), jnp.float32, -s, s), 'b_vk': jax.random.uniform(ks[3], (C,), jnp.float32, -s, s), 'W_lk': jax.random.uniform(ks[4], (C, C), jnp.float32, -s, s), 'b_lk': jax.random.uniform(ks[5], (C,), jnp.float32, -s, s), 'W_vv': jax.random.uniform(ks[6], (C, C), jnp.float32, -s, s), 'b_vv': jax.random.uniform(ks[7], (C,), jnp.float32, -s, s), 'W_lv': jax.random.uniform(ks[8], (C, C), jnp.float32, -s, s), 'b_lv': jax.random.uniform(ks[9], (C,), jnp.float32, -s, s)}
        return inp
    _L1_xattn_all = _L1_xattn_setup()
    _L1_xattn_in = {k: v for k, v in _L1_xattn_all.items() if k in ('W_vk', 'b_vk', 'W_lk', 'b_lk', 'W_vv', 'b_vv', 'W_lv', 'b_lv')}
    del _L1_xattn_all

    def _L1_ffn_setup():
        import jax, jax.numpy as jnp
        import numpy as np
        B, S, D_MODEL, D_HIDDEN = (4, 512, 256, 1024)

        def act_quant(x):
            scale = 127.0 / jnp.clip(jnp.max(jnp.abs(x), axis=-1, keepdims=True), 1e-05)
            return jnp.clip(jnp.round(x * scale), -128, 127) / scale

        def weight_quant(w):
            scale = 1.0 / jnp.clip(jnp.mean(jnp.abs(w)), 1e-05)
            return jnp.clip(jnp.round(w * scale), -1, 1) / scale

        def bit_linear(x, w):
            xq = x + jax.lax.stop_gradient(act_quant(x) - x)
            wq = w + jax.lax.stop_gradient(weight_quant(w) - w)
            return jnp.einsum('bsd,hd->bsh', xq, wq)

        def depthwise_conv1d(x_bcl, w, b):
            y = jax.lax.conv_general_dilated(x_bcl, w, window_strides=(1,), padding=[(1, 1)], dimension_numbers=('NCH', 'OIH', 'NCH'), feature_group_count=x_bcl.shape[1])
            return y + b[None, :, None]
        key = jax.random.key(seed)
        ks = jax.random.split(key, 5)
        lim1 = 1.0 / np.sqrt(D_MODEL)
        lim2 = 1.0 / np.sqrt(D_HIDDEN)
        limc = 1.0 / np.sqrt(3.0)
        return {'x': jax.random.normal(ks[0], (B, S, D_MODEL), dtype=jnp.float32), 'w1': jax.random.uniform(ks[1], (D_HIDDEN, D_MODEL), jnp.float32, -lim1, lim1), 'conv_w': jax.random.uniform(ks[2], (D_HIDDEN, 1, 3), jnp.float32, -limc, limc), 'conv_b': jax.random.uniform(ks[3], (D_HIDDEN,), jnp.float32, -limc, limc), 'w2': jax.random.uniform(ks[4], (D_MODEL, D_HIDDEN), jnp.float32, -lim2, lim2)}
    _L1_ffn_all = _L1_ffn_setup()
    _L1_ffn_in = {k: v for k, v in _L1_ffn_all.items() if k in ('w1', 'conv_w', 'conv_b', 'w2')}
    del _L1_ffn_all
    return {'x': x, 'ctx_1024': ctx_1024, 'itok_BxS_8_8191': itok_BxS_8_8191, 'itok_BxS2_1_8191': itok_BxS2_1_8191, 'mask_BxSxS2_if1': mask_BxSxS2_if1, 'L0_attn_Wq': _L0_attn_in['Wq'], 'L0_attn_bq': _L0_attn_in['bq'], 'L0_attn_Wl': _L0_attn_in['Wl'], 'L0_attn_bl': _L0_attn_in['bl'], 'L0_attn_Wk': _L0_attn_in['Wk'], 'L0_attn_bk': _L0_attn_in['bk'], 'L0_attn_Wv': _L0_attn_in['Wv'], 'L0_attn_bv': _L0_attn_in['bv'], 'L0_attn_Wo': _L0_attn_in['Wo'], 'L0_attn_bo': _L0_attn_in['bo'], 'L0_xattn_W_q': _L0_xattn_in['W_q'], 'L0_xattn_W_k': _L0_xattn_in['W_k'], 'L0_xattn_W_v': _L0_xattn_in['W_v'], 'L0_xattn_W_o': _L0_xattn_in['W_o'], 'L0_ffn_Wr': _L0_ffn_in['Wr'], 'L0_ffn_br': _L0_ffn_in['br'], 'L0_ffn_W1': _L0_ffn_in['W1'], 'L0_ffn_b1': _L0_ffn_in['b1'], 'L0_ffn_W2': _L0_ffn_in['W2'], 'L0_ffn_b2': _L0_ffn_in['b2'], 'L1_attn_norm1_w': _L1_attn_in['norm1_w'], 'L1_attn_norm2_w': _L1_attn_in['norm2_w'], 'L1_attn_in_proj_w': _L1_attn_in['in_proj_w'], 'L1_attn_out_proj_w': _L1_attn_in['out_proj_w'], 'L1_attn_fc_w': _L1_attn_in['fc_w'], 'L1_attn_proj_w': _L1_attn_in['proj_w'], 'L1_xattn_W_vk': _L1_xattn_in['W_vk'], 'L1_xattn_b_vk': _L1_xattn_in['b_vk'], 'L1_xattn_W_lk': _L1_xattn_in['W_lk'], 'L1_xattn_b_lk': _L1_xattn_in['b_lk'], 'L1_xattn_W_vv': _L1_xattn_in['W_vv'], 'L1_xattn_b_vv': _L1_xattn_in['b_vv'], 'L1_xattn_W_lv': _L1_xattn_in['W_lv'], 'L1_xattn_b_lv': _L1_xattn_in['b_lv'], 'L1_ffn_w1': _L1_ffn_in['w1'], 'L1_ffn_conv_w': _L1_ffn_in['conv_w'], 'L1_ffn_conv_b': _L1_ffn_in['conv_b'], 'L1_ffn_w2': _L1_ffn_in['w2']}

def reference(x, ctx_1024, itok_BxS_8_8191, itok_BxS2_1_8191, mask_BxSxS2_if1, L0_attn_Wq, L0_attn_bq, L0_attn_Wl, L0_attn_bl, L0_attn_Wk, L0_attn_bk, L0_attn_Wv, L0_attn_bv, L0_attn_Wo, L0_attn_bo, L0_xattn_W_q, L0_xattn_W_k, L0_xattn_W_v, L0_xattn_W_o, L0_ffn_Wr, L0_ffn_br, L0_ffn_W1, L0_ffn_b1, L0_ffn_W2, L0_ffn_b2, L1_attn_norm1_w, L1_attn_norm2_w, L1_attn_in_proj_w, L1_attn_out_proj_w, L1_attn_fc_w, L1_attn_proj_w, L1_xattn_W_vk, L1_xattn_b_vk, L1_xattn_W_lk, L1_xattn_b_lk, L1_xattn_W_vv, L1_xattn_b_vv, L1_xattn_W_lv, L1_xattn_b_lv, L1_ffn_w1, L1_ffn_conv_w, L1_ffn_conv_b, L1_ffn_w2):
    import jax
    import jax.numpy as jnp

    def _L0_attn_ref(x, Wq, bq, Wl, bl, Wk, bk, Wv, bv, Wo, bo):
        import jax, jax.numpy as jnp
        import numpy as np
        DIM = 256
        HEADS = 16
        DIM_HEAD = DIM // HEADS
        LATENT = DIM // 4
        SCALE = DIM_HEAD ** (-0.5)
        B, S, D = x.shape
        H, Dh = (HEADS, DIM_HEAD)
        q = (x @ Wq + bq).reshape(B, S, H, Dh)
        latent = x @ Wl + bl
        k = (latent @ Wk + bk).reshape(B, S, H, Dh)
        v = (latent @ Wv + bv).reshape(B, S, H, Dh)
        scores = jnp.einsum('bihd,bjhd->bhij', q, k) * SCALE
        attn = jax.nn.softmax(scores, axis=-1)
        out = jnp.einsum('bhij,bjhd->bihd', attn, v).reshape(B, S, D)
        out = out @ Wo + bo
        return out

    def _L0_xattn_ref(query, keys, values, W_q, W_k, W_v, W_o, query_pos, key_pos, mask):
        import jax, jax.numpy as jnp
        import numpy as np
        DIM = 256
        NUM_HEADS = 16
        HEAD_DIM = DIM // NUM_HEADS

        def _slopes(num_heads):
            ratio = 2.0 ** (-8.0 / num_heads)
            return jnp.asarray([ratio ** i for i in range(1, num_heads + 1)], dtype=jnp.float32)
        b, q_len, _ = query.shape
        k_len = keys.shape[1]
        scale = 1.0 / np.sqrt(HEAD_DIM)
        Q = (query @ W_q.T).reshape(b, q_len, NUM_HEADS, HEAD_DIM).transpose(0, 2, 1, 3)
        K = (keys @ W_k.T).reshape(b, k_len, NUM_HEADS, HEAD_DIM).transpose(0, 2, 1, 3)
        V = (values @ W_v.T).reshape(b, k_len, NUM_HEADS, HEAD_DIM).transpose(0, 2, 1, 3)
        scores = jnp.einsum('bhqd,bhkd->bhqk', Q, K) * scale
        dist = (query_pos[:, :, None] - key_pos[:, None, :]).astype(scores.dtype)
        bias = -_slopes(NUM_HEADS)[None, :, None, None] * dist[:, None, :, :]
        scores = scores + bias
        scores = jnp.where(mask[:, None, :, :] == 0, -jnp.inf, scores)
        m = jnp.max(scores, axis=-1, keepdims=True)
        e = jnp.exp(scores - m)
        attn = e / (1.0 + jnp.sum(e, axis=-1, keepdims=True))
        out = jnp.einsum('bhqk,bhkd->bhqd', attn, V)
        out = out.transpose(0, 2, 1, 3).reshape(b, q_len, DIM)
        return out @ W_o.T

    def _L0_ffn_ref(x, Wr, br, W1, b1, W2, b2):
        import jax, jax.numpy as jnp
        import numpy as np
        NEG_INF = jnp.float32(-1000000000.0)

        def _router(x, Wr, br, top_k=2):
            logits = jnp.einsum('bsd,de->bse', x, Wr) + br
            _, top_idx = jax.lax.top_k(logits, top_k)
            num_experts = logits.shape[-1]
            mask = jnp.any(top_idx[..., None] == jnp.arange(num_experts), axis=-2)
            sparse_logits = jnp.where(mask, logits, NEG_INF)
            weights = jax.nn.softmax(sparse_logits, axis=-1)
            return (weights, top_idx, mask)
        weights, top_idx, mask = _router(x, Wr, br, top_k=2)
        num_experts = W1.shape[0]
        out = jnp.zeros_like(x)
        for e in range(num_experts):
            h = jax.nn.relu(jnp.einsum('bsd,dh->bsh', x, W1[e]) + b1[e])
            y = jnp.einsum('bsh,hd->bsd', h, W2[e]) + b2[e]
            w = weights[:, :, e] * mask[:, :, e].astype(x.dtype)
            out = out + y * w[:, :, None]
        return out

    def _L1_attn_ref(x, norm1_w, norm2_w, in_proj_w, out_proj_w, fc_w, proj_w):
        import jax, jax.numpy as jnp
        import numpy as np
        DIM = 256
        HEADS = 16
        HDIM = DIM // HEADS
        CHUNK = 64
        RES_SCALE = float(1.0 / np.sqrt(2.0))
        EPS_FP32 = float(np.finfo(np.float32).eps)

        def _rms(x, eps):
            return x * jax.lax.rsqrt(jnp.mean(x * x, axis=-1, keepdims=True) + eps)

        def _mixer(x, in_proj_w, out_proj_w):
            B, S, D = x.shape
            proj = x @ in_proj_w.T
            q, k, v, a, g = jnp.split(proj, 5, axis=-1)
            rs = lambda t: t.reshape(B, S, HEADS, HDIM)
            q, k, v, a, g = map(rs, (q, k, v, a, g))
            q = _rms(q, EPS_FP32)
            k = jnp.tanh(k)
            a = jnp.clip(jax.nn.sigmoid(a + 2.0), 0.6, 0.9995)
            u = k * v
            nC = S // CHUNK
            a_c = jnp.moveaxis(a.reshape(B, nC, CHUNK, HEADS, HDIM), 1, 0)
            u_c = jnp.moveaxis(u.reshape(B, nC, CHUNK, HEADS, HDIM), 1, 0)

            def step(state, inp):
                ac, uc = inp
                prefix = jnp.cumprod(ac, axis=1)
                acc = jnp.cumsum(uc / jnp.maximum(prefix, 1e-06), axis=1)
                states = prefix * (state[:, None] + acc)
                return (states[:, -1], states)
            state0 = jnp.zeros((B, HEADS, HDIM), jnp.float32)
            _, states = jax.lax.scan(step, state0, (a_c, u_c))
            memory = jnp.moveaxis(states, 0, 1).reshape(B, S, HEADS, HDIM)
            gate = jax.nn.sigmoid(g)
            y = gate * (q * memory) + (1.0 - gate) * v
            return y.reshape(B, S, D) @ out_proj_w.T
        h1 = norm1_w * _rms(x, 1e-06)
        x = x + RES_SCALE * _mixer(h1, in_proj_w, out_proj_w)
        h2 = norm2_w * _rms(x, 1e-06)
        mlp = jax.nn.silu(h2 @ fc_w.T) @ proj_w.T
        return x + RES_SCALE * mlp

    def _L1_xattn_ref(vis_features, lang_features, W_vk, b_vk, W_lk, b_lk, W_vv, b_vv, W_lv, b_lv):
        import jax, jax.numpy as jnp
        import numpy as np
        C = 256
        B, HW, N = (8, 1024, 77)
        scale = jnp.asarray(C, vis_features.dtype) ** (-0.5)
        vis_key = jnp.einsum('bsc,dc->bsd', vis_features, W_vk) + b_vk
        lang_key = jnp.einsum('bnc,dc->bnd', lang_features, W_lk) + b_lk
        vis_value = jnp.einsum('bsc,dc->bsd', vis_features, W_vv) + b_vv
        lang_value = jnp.einsum('bnc,dc->bnd', lang_features, W_lv) + b_lv
        attn = jax.nn.softmax(jnp.einsum('bsd,bnd->bsn', vis_key, lang_key) * scale, axis=-1)
        lang_attended_vis = jnp.einsum('bsn,bnc->bsc', attn, lang_value)
        vision_attended_lang = jnp.einsum('bsn,bsc->bnc', attn, vis_value)
        projected = jnp.einsum('bsn,bnc->bsc', attn, vision_attended_lang)
        return lang_attended_vis + projected

    def _L1_ffn_ref(x, w1, conv_w, conv_b, w2):
        import jax, jax.numpy as jnp
        import numpy as np
        B, S, D_MODEL, D_HIDDEN = (4, 512, 256, 1024)

        def act_quant(x):
            scale = 127.0 / jnp.clip(jnp.max(jnp.abs(x), axis=-1, keepdims=True), 1e-05)
            return jnp.clip(jnp.round(x * scale), -128, 127) / scale

        def weight_quant(w):
            scale = 1.0 / jnp.clip(jnp.mean(jnp.abs(w)), 1e-05)
            return jnp.clip(jnp.round(w * scale), -1, 1) / scale

        def bit_linear(x, w):
            xq = x + jax.lax.stop_gradient(act_quant(x) - x)
            wq = w + jax.lax.stop_gradient(weight_quant(w) - w)
            return jnp.einsum('bsd,hd->bsh', xq, wq)

        def depthwise_conv1d(x_bcl, w, b):
            y = jax.lax.conv_general_dilated(x_bcl, w, window_strides=(1,), padding=[(1, 1)], dimension_numbers=('NCH', 'OIH', 'NCH'), feature_group_count=x_bcl.shape[1])
            return y + b[None, :, None]
        h = bit_linear(x, w1)
        h = depthwise_conv1d(h.transpose(0, 2, 1), conv_w, conv_b)
        h = h.transpose(0, 2, 1)
        h = jax.nn.silu(h)
        return bit_linear(h, w2)
    x = x + _L0_attn_ref(_layernorm(x, axis=-1), L0_attn_Wq, L0_attn_bq, L0_attn_Wl, L0_attn_bl, L0_attn_Wk, L0_attn_bk, L0_attn_Wv, L0_attn_bv, L0_attn_Wo, L0_attn_bo)
    x = x + _L0_xattn_ref(_layernorm(x, axis=-1), ctx_1024, ctx_1024, L0_xattn_W_q, L0_xattn_W_k, L0_xattn_W_v, L0_xattn_W_o, itok_BxS_8_8191, itok_BxS2_1_8191, mask_BxSxS2_if1)
    x = x + _L0_ffn_ref(_layernorm(x, axis=-1), L0_ffn_Wr, L0_ffn_br, L0_ffn_W1, L0_ffn_b1, L0_ffn_W2, L0_ffn_b2)
    x = x + _L1_attn_ref(_layernorm(x, axis=-1), L1_attn_norm1_w, L1_attn_norm2_w, L1_attn_in_proj_w, L1_attn_out_proj_w, L1_attn_fc_w, L1_attn_proj_w)
    x = x + _L1_xattn_ref(_layernorm(x, axis=-1), ctx_1024, L1_xattn_W_vk, L1_xattn_b_vk, L1_xattn_W_lk, L1_xattn_b_lk, L1_xattn_W_vv, L1_xattn_b_vv, L1_xattn_W_lv, L1_xattn_b_lv)
    x = x + _L1_ffn_ref(_layernorm(x, axis=-1), L1_ffn_w1, L1_ffn_conv_w, L1_ffn_conv_b, L1_ffn_w2)
    return x

_drawn_inputs = setup_inputs


def setup_inputs(seed=0):
    import zlib

    import numpy as np

    out = dict(_drawn_inputs(seed))
    spreads = {'L0_attn_bq': (0.0, 0.1),
     'L0_attn_bl': (0.0, 0.1),
     'L0_attn_bk': (0.0, 2.0),
     'L0_attn_bv': (0.0, 0.1),
     'L0_attn_bo': (0.0, 0.1),
     'L0_ffn_br': (0.0, 0.1),
     'L0_ffn_b1': (0.0, 0.1),
     'L0_ffn_b2': (0.0, 0.1),
     'L1_attn_norm1_w': (1.0, 0.6),
     'L1_attn_norm2_w': (1.0, 0.6)}
    factors = {'L1_xattn_W_vk': 3.487,
     'L1_xattn_b_vk': 8.0,
     'L1_xattn_W_lk': 3.448,
     'L1_xattn_b_lk': 64.0,
     'L1_xattn_b_vv': 3.47,
     'L1_xattn_b_lv': 3.478,
     'L1_ffn_w1': 2.867,
     'L1_ffn_conv_w': 2.83}
    for name, (base, spread) in spreads.items():
        noise = np.random.default_rng([zlib.crc32(name.encode()), seed]).standard_normal(out[name].shape)
        drawn = base * np.exp(spread * noise) if base else spread * noise
        out[name] = jnp.asarray(drawn.astype(out[name].dtype))
    for name, factor in factors.items():
        out[name] = (out[name] * factor).astype(out[name].dtype)
    return out
```

```python
from contextlib import ExitStack

import numpy as np

import concourse.bass as bass
from concourse import mybir

F32, BF16, I32, U32 = mybir.dt.float32, mybir.dt.bfloat16, mybir.dt.int32, mybir.dt.uint32
ALU = mybir.AluOpType
ACT = mybir.ActivationFunctionType
AX = mybir.AxisListType

P = 128
NB = 32
D = 256
DC = D // P
HEADS = 16
HD = D // HEADS
LATENT = D // 4
QUADS = HEADS // 4
LN_EPS = 1e-5


class Semaphores:

    def __init__(self, nc, ctx, name):
        self.nc, self.ctx, self.name, self.cleared = nc, ctx, name, []

    def __call__(self, n):
        s = self.ctx.enter_context(self.nc.semaphore(f"{self.name}_{n}"))
        self.cleared.append(s)
        return s

    def kept(self, n):
        return self.nc.alloc_semaphore(f"{self.name}_{n}")

    def clear(self):
        with self.nc.Block() as block:
            @block.gpsimd
            def _(pool):
                for s in self.cleared:
                    pool.sem_clear(s)


class Batch:

    def __init__(self, number, parity):
        self.n, self.par = number, parity

    def known(self):
        return isinstance(self.n, int)


def wait(eng, sem, batch, per_batch, done):
    value = batch.n * per_batch + done if per_batch != 1 else batch.n + done
    if batch.known() and value <= 0:
        return
    eng.wait_ge(sem, value)


def pipeline(eng, count, depth, step):
    lag = depth - 1
    start = (lag + 3) // 2 * 2

    def one(t, parity):
        def at(k):
            if isinstance(t, int):
                return Batch(t - k, (t - k) % 2) if 0 <= t - k < count else None
            return Batch(t - k if k else t, (parity - k) % 2)
        step(at)

    end = start + (count - start) // 2 * 2
    for t in range(start):
        one(t, t % 2)
    with eng.Fori(start, end - 1, 2) as i:
        one(i, 0)
        one(i + 1, 1)
    for t in range(end, count + lag):
        one(t, t % 2)


def chained(eng, sem):
    count = [0]

    def link(instruction):
        count[0] += 1
        instruction.then_inc(sem, 1)
        eng.wait_ge(sem, count[0])
    return link


def first_statistics(nc, x_in, stats, count=NB):
    per = 4
    with ExitStack() as ctx:
        x_a = ctx.enter_context(nc.sbuf_tensor("first_x", [P, 2, per, D], F32))
        loaded = [nc.alloc_semaphore(f"first_loaded{i}") for i in range(2)]
        done = nc.alloc_semaphore("first_done")
        block = ctx.enter_context(nc.Block())

        @block.sync
        def _(sp):
            for g in range(count // per):
                if g >= 2:
                    sp.wait_ge(done, per * (g - 1))
                sp.dma_start(x_a[:, g % 2, :, :], x_in[per * g:per * g + per].rearrange("b t d -> t b d"))\
                  .then_inc(loaded[g % 2], 16)

        @block.vector
        def _(dve):
            for g in range(count // per):
                dve.wait_ge(loaded[g % 2], 16 * (g // 2 + 1))
                for i in range(per):
                    dve.bn_stats(stats[:, per * g + i, :], x_a[:, g % 2, i, :]).then_inc(done, 1)


def norm_scales(nc, name, stats, mean, rstd, rms_scale=None, rms_eps=1e-6, count=NB):
    with ExitStack() as ctx:
        def sb(n):
            return ctx.enter_context(nc.sbuf_tensor(f"{name}_{n}", [P, count], F32))
        diff, var, root, tmp = sb("diff"), sb("var"), sb("root"), sb("tmp")
        dve_step = nc.alloc_semaphore(f"{name}_dve_step")
        var_ready = nc.alloc_semaphore(f"{name}_var_ready")
        root_ready = nc.alloc_semaphore(f"{name}_root_ready")
        block = ctx.enter_context(nc.Block())
        rounds = 1 if rms_scale is None else 2

        @block.vector
        def _(dve):
            link = chained(dve, dve_step)

            def tt(out, a, b, op):
                link(dve.tensor_tensor(out, a, b, op))

            def inverse_root(out, turn):
                link(dve.tensor_copy(tmp[:, :], var[:, :]))
                dve.sem_inc(var_ready, 1)
                dve.wait_ge(root_ready, turn)
                link(dve.reciprocal(out, root[:, :]))
                tt(tmp[:, :], out, out, ALU.mult)
                tt(tmp[:, :], tmp[:, :], var[:, :], ALU.mult)
                link(dve.tensor_scalar(tmp[:, :], tmp[:, :], -0.5, 1.5, ALU.mult, ALU.add))
                tt(out, out, tmp[:, :], ALU.mult)

            tt(mean[:, :], stats[:, :, 1], stats[:, :, 4], ALU.add)
            link(dve.tensor_scalar(mean[:, :], mean[:, :], 0.5, None, ALU.mult))
            tt(diff[:, :], stats[:, :, 1], stats[:, :, 4], ALU.subtract)
            tt(diff[:, :], diff[:, :], diff[:, :], ALU.mult)
            link(dve.tensor_scalar(diff[:, :], diff[:, :], 0.25, LN_EPS, ALU.mult, ALU.add))
            tt(var[:, :], stats[:, :, 2], stats[:, :, 5], ALU.add)
            link(dve.tensor_scalar(var[:, :], var[:, :], 1.0 / D, None, ALU.mult))
            if rms_scale is not None:
                tt(rms_scale[:, :], var[:, :], diff[:, :], ALU.add)
                link(dve.tensor_scalar(rms_scale[:, :], rms_scale[:, :], -LN_EPS, None, ALU.add))
            tt(var[:, :], var[:, :], diff[:, :], ALU.add)
            inverse_root(rstd[:, :], 1)
            if rms_scale is not None:
                tt(tmp[:, :], rstd[:, :], rstd[:, :], ALU.mult)
                tt(var[:, :], rms_scale[:, :], tmp[:, :], ALU.mult)
                link(dve.tensor_scalar(var[:, :], var[:, :], rms_eps, None, ALU.add))
                inverse_root(rms_scale[:, :], 2)
                tt(rms_scale[:, :], rms_scale[:, :], rstd[:, :], ALU.mult)

        @block.scalar
        def _(act):
            for turn in range(rounds):
                act.wait_ge(var_ready, turn + 1)
                act.activation(root[:, :], var[:, :], ACT.Sqrt).then_inc(root_ready, 1)


def alibi_rows(nc, q_pos, k_pos, slope_bc, q_rows, k_rows, count=NB):
    with ExitStack() as ctx:
        def sb(n, shape, dt):
            return ctx.enter_context(nc.sbuf_tensor(f"alibi_{n}", shape, dt))
        ints = sb("ints", [count, 2, P], I32)
        pos = sb("pos", [count, 2, P], F32)
        slope = sb("slope", [count, HEADS], F32)
        prod = sb("prod", [count, HEADS, P], F32)
        parts = sb("parts", [count, 3, HEADS, P], BF16)
        q_parts = sb("q_parts", [count, 4, P], BF16)
        loaded, step, stored = (nc.alloc_semaphore(f"alibi_{n}") for n in ("loaded", "step", "stored"))
        parts_ready = nc.alloc_semaphore("alibi_parts_ready")
        block = ctx.enter_context(nc.Block())

        @block.sync
        def _(sp):
            sp.dma_start(ints[:, 0, :], q_pos).then_inc(loaded, 16)
            sp.dma_start(ints[:, 1, :], k_pos).then_inc(loaded, 16)
            sp.dma_start(slope[:, :], slope_bc).then_inc(loaded, 16)
            sp.wait_ge(parts_ready, 1)
            for row in range(12):
                a = 3 if row < 3 else (row - 3) // 3
                sp.dma_start(q_rows[row], q_parts[:, a, :]).then_inc(stored, 16)
            sp.dma_start(k_rows.rearrange("b a n -> b (a n)"),
                         parts[:, :, :, :].rearrange("b a h t -> b (a h t)")).then_inc(stored, 16)
            sp.wait_ge(stored, 16 * 13)

        @block.vector
        def _(dve):
            link = chained(dve, step)
            dve.wait_ge(loaded, 48)
            link(dve.tensor_copy(pos[:, :, :], ints[:, :, :]))
            link(dve.memset(q_parts[:, 3, :], 1.0))
            link(dve.tensor_tensor(prod[:, :, :], pos[:, 1, :].unsqueeze(1).to_broadcast([count, HEADS, P]),
                                   slope[:, :].unsqueeze(2).to_broadcast([count, HEADS, P]), ALU.mult))
            for part in range(3):
                link(dve.tensor_copy(parts[:, part, :, :], prod[:, :, :]))
                link(dve.tensor_copy(q_parts[:, part, :], pos[:, 0, :]))
                if part < 2:
                    link(dve.tensor_tensor(prod[:, :, :], prod[:, :, :], parts[:, part, :, :], ALU.subtract))
                    link(dve.tensor_tensor(pos[:, 0, :], pos[:, 0, :], q_parts[:, part, :], ALU.subtract))
            dve.sem_inc(parts_ready, 1)


def latent_weights(nc, w_in, w_out):
    with ExitStack() as ctx:
        def sb(n, shape):
            return ctx.enter_context(nc.sbuf_tensor(f"latent_{n}", shape, F32))

        def sem(n):
            return nc.alloc_semaphore(f"latent_{n}")

        down, up = sb("down", [LATENT, D]), sb("up", [LATENT, 2 * D])
        bl, bl_rows = sb("bl", [LATENT, 1]), sb("bl_rows", [LATENT, P])
        bk, bv = sb("bk", [P, DC]), sb("bv", [P, D])
        both = sb("both", [P, DC, 2 * D])
        w_ps = ctx.enter_context(nc.psum_tensor("latent_w_ps", [P, DC, 2 * D], F32))
        v_ps = ctx.enter_context(nc.psum_tensor("latent_v_ps", [P, 2 * D], F32))
        k_ps = ctx.enter_context(nc.psum_tensor("latent_k_ps", [P, 2 * D], F32))
        loaded, rows_ready, done, ready, stored = (sem(n) for n in ("loaded", "rows_ready", "done", "ready", "stored"))
        block = ctx.enter_context(nc.Block())

        @block.sync
        def _(sp):
            for dst, key in ((down, "down"), (up, "up"), (bl, "bl"), (bk, "bk"), (bv, "bv")):
                sp.dma_start(dst[:, :], w_in[key]).then_inc(loaded, 16)
            sp.wait_ge(ready, 3)
            sp.dma_start(w_out["wk"], both[:, :, 0:D]).then_inc(stored, 16)
            sp.dma_start(w_out["wv"], both[:, :, D:2 * D]).then_inc(stored, 16)
            sp.dma_start(w_out["bk"], bk[:, :]).then_inc(stored, 16)
            sp.dma_start(w_out["bv"], bv[:, :]).then_inc(stored, 16)
            sp.wait_ge(stored, 64)

        @block.tensor
        def _(pe):
            pe.wait_ge(loaded, 80)
            for c in range(DC):
                pe.matmul(w_ps[:, c, :], down[:, P * c:P * c + P], up[:, :], start=True, stop=True)
            for c in range(DC):
                pe.matmul(k_ps[:, c:c + 1], up[:, P * c:P * c + P], bl[:, :], start=True, stop=True)
            pe.wait_ge(rows_ready, 1)
            pe.matmul(v_ps[:, 0:D], bl_rows[:, :], up[:, D:2 * D], start=True, stop=True).then_inc(done, 1)

        @block.vector
        def _(dve):
            dve.wait_ge(loaded, 80)
            dve.tensor_copy(bl_rows[:, :], bl[:, :].to_broadcast([LATENT, P])).then_inc(rows_ready, 1)
            dve.wait_ge(done, 1)
            dve.tensor_copy(both[:, :, :], w_ps[:, :, :]).then_inc(ready, 1)
            dve.tensor_tensor(bk[:, :], k_ps[:, 0:DC], bk[:, :], ALU.add).then_inc(ready, 1)
            dve.tensor_tensor(bv[:, :], v_ps[:, 0:D], bv[:, :], ALU.add).then_inc(ready, 1)


def attention(nc, name, cross, x_in, x_out, ctx_in, mask_in, alibi, stats, mean, rstd, ident,
              ident_b, w_dram, const, count=NB):
    with ExitStack() as ctx:
        def sb(n, shape, dt=F32):
            return ctx.enter_context(nc.sbuf_tensor(f"{name}_{n}", shape, dt))

        def ps(n, shape):
            return ctx.enter_context(nc.psum_tensor(f"{name}_{n}", shape, F32))

        sem = Semaphores(nc, ctx, name)

        wq, wk, wv, wo = (sb(n, [P, DC, D]) for n in ("wq", "wk", "wv", "wo"))
        bq, bk = sb("bq", [P, DC]), sb("bk", [P, DC])
        bv, bo = sb("bv", [P, D]), sb("bo", [P, D])
        head_mask = sb("head_mask", [P, 8])
        x_t, x_r, xn, o_n, x_o = (sb(n, [P, 2, D]) for n in ("x_t", "x_r", "xn", "o_n", "x_o"))
        xnT, o_nT, qT, kT = (sb(n, [P, 2, DC, P]) for n in ("xnT", "o_nT", "qT", "kT"))
        k_diag = sb("k_diag", [P, 2, HEADS, P])
        v_pad = sb("v_pad", [P, 2, HEADS, 32])
        probs = sb("probs", [P, QUADS, 4, P])
        probsT = sb("probsT", [P, 2, 4, P])
        oT = sb("oT", [P, QUADS, P])
        neg_max, sums, inv = (sb(n, [P, 2, HEADS]) for n in ("neg_max", "sums", "inv"))
        s_ps = ps("scores", [P, QUADS, 4, P])
        o_ps = ps("o_ps", [P, QUADS, P])
        b_ps = ps("b_ps", [P, 512])
        p_ps = [ps("p0", [P, 512]), ps("p1", [P, 512])]

        loaded_w, scaled = sem("loaded_w"), sem("scaled")
        x_loaded = [sem("x_loaded0"), sem("x_loaded1")]
        r_loaded = [sem("r_loaded0"), sem("r_loaded1")]
        xn_ready, xt_done, xnT_ready = sem("xn_ready"), sem("xt_done"), sem("xnT_ready")
        q_done, k_done, v_done = sem("q_done"), sem("k_done"), sem("v_done")
        q_ready, k_ready, v_ready, diag_ready = sem("q_ready"), sem("k_ready"), sem("v_ready"), sem("diag_ready")
        s_done, max_ready, exp_ready = sem("s_done"), sem("max_ready"), sem("exp_ready")
        pt_done, pt_ready, pv_done = sem("pt_done"), sem("pt_ready"), sem("pv_done")
        oT_ready, back_done, on_ready, inv_ready = sem("oT_ready"), sem("back_done"), sem("on_ready"), sem("inv_ready")
        ont_done, onT_ready, wo_done = sem("ont_done"), sem("onT_ready"), sem("wo_done")
        r_biased, xo_ready, stat_ready = sem("r_biased"), sem("xo_ready"), sem("stat_ready")
        stored = [sem.kept("stored0"), sem.kept("stored1")]
        if cross:
            c_t = sb("c_t", [P, 2, D])
            cT = sb("cT", [P, 2, DC, P])
            mask_t = sb("mask_t", [P, 2, P], I32)
            mask_b = sb("mask_b", [P, 2, P], BF16)
            rows_k = sb("rows_k", [12, 2, HEADS * P], BF16)
            rows_q = sb("rows_q", [12, NB, P], BF16)
            c_loaded = [sem("c_loaded0"), sem("c_loaded1")]
            m_loaded = [sem("m_loaded0"), sem("m_loaded1")]
            k_rows_loaded = [sem("k_rows0"), sem("k_rows1")]
            ct_done, cT_ready, mask_ready = sem("ct_done"), sem("cT_ready"), sem("mask_ready")
        ctx.callback(sem.clear)
        block = ctx.enter_context(nc.Block())
        n_w = 9 + (3 if cross else 0)

        @block.sync
        def _(sp):
            for dst, key in ((wq, "wq"), (wk, "wk"), (wv, "wv"), (wo, "wo")):
                sp.dma_start(dst[:, :, :], w_dram[key]).then_inc(loaded_w, 16)
            for dst, key in ((bq, "bq"), (bk, "bk"), (bv, "bv"), (bo, "bo"), (head_mask, "head_mask")):
                sp.dma_start(dst[:, :], w_dram[key]).then_inc(loaded_w, 16)
            if cross:
                sp.dma_start(rows_q[:, :, :], alibi["q"]).then_inc(loaded_w, 16)
                for par in range(2):
                    sp.dma_start(rows_k[3:12, par, :], alibi["slopes"]).then_inc(loaded_w, 16)

            def step(at):
                b = at(0)
                if b:
                    wait(sp, xn_ready, b, 1, -1)
                    sp.dma_start(x_t[:, b.par, :], x_in[b.n]).then_inc(x_loaded[b.par], 16)
                    if cross:
                        wait(sp, ct_done, b, 1, -1)
                        sp.dma_start(c_t[:, b.par, :], ctx_in[b.n]).then_inc(c_loaded[b.par], 16)
                        wait(sp, mask_ready, b, 1, -1)
                        sp.dma_start(mask_t[:, b.par, :], mask_in[b.n]).then_inc(m_loaded[b.par], 16)
                        wait(sp, s_done, b, QUADS, -QUADS)
                        sp.dma_start(rows_k[0:3, b.par, :], alibi["k"][b.n]).then_inc(k_rows_loaded[b.par], 16)
                    wait(sp, xo_ready, b, 1, -1)
                    sp.dma_start(x_r[:, b.par, :], x_in[b.n]).then_inc(r_loaded[b.par], 16)
            pipeline(sp, count, 1, step)
            for par in range(2):
                sp.wait_ge(stored[par], 16 * (count // 2))

        def loaded(eng, sems, b):
            eng.wait_ge(sems[b.par], (b.n + (2 - b.par)) * 8)

        @block.tensor
        def _(pe):
            pe.wait_ge(scaled, 1)

            def scores(b, j):
                if j == 0:
                    wait(pe, q_ready, b, 1, 1)
                    wait(pe, diag_ready, b, 1, 1)
                    if cross:
                        wait(pe, mask_ready, b, 1, 1)
                        loaded(pe, k_rows_loaded, b)
                wait(pe, pt_ready, b, QUADS, j - 3)
                last = pe.matmul(s_ps[:, j, :, :], qT[:, b.par, j // 2, :],
                                 k_diag[:, b.par, 4 * j:4 * j + 4, :], start=True, stop=not cross)
                if cross:
                    pe.matmul(s_ps[:, j, :, :], ident_b[:, :],
                              mask_b[:, b.par, :].unsqueeze(1).to_broadcast([P, 4, P]), start=False, stop=False)
                    last = pe.matmul(s_ps[:, j, :, :], rows_q[:, b.n, :],
                                     rows_k[:, b.par, 512 * j:512 * j + 512].rearrange("p (a c) -> p a c", a=4),
                                     start=False, stop=True)
                last.then_inc(s_done, 1)

            def back(b):
                wait(pe, oT_ready, b, 1, 1)
                wait(pe, xo_ready, b, 1, 0)
                for j in range(QUADS):
                    last = pe.transpose(b_ps[:, P * j:P * j + P], oT[:, j, :], ident[:, :])
                last.then_inc(back_done, 1)

            def x_transpose(b):
                wait(pe, xn_ready, b, 1, 1)
                wait(pe, v_ready, b, 1, 0)
                for c in range(DC):
                    last = pe.transpose(p_ps[0][:, P * c:P * c + P], xn[:, b.par, P * c:P * c + P], ident[:, :])
                last.then_inc(xt_done, 1)
                if cross:
                    loaded(pe, c_loaded, b)
                    wait(pe, k_ready, b, 1, 0)
                    for c in range(DC):
                        last = pe.transpose(p_ps[1][:, P * c:P * c + P], c_t[:, b.par, P * c:P * c + P], ident[:, :])
                    last.then_inc(ct_done, 1)

            def on_transpose(b):
                wait(pe, on_ready, b, 1, 1)
                for c in range(DC):
                    last = pe.transpose(b_ps[:, P * c:P * c + P], o_n[:, b.par, P * c:P * c + P], ident[:, :])
                last.then_inc(ont_done, 1)

            def probs_transpose(b, j):
                wait(pe, exp_ready, b, QUADS, j + 1)
                for i in range(4):
                    last = pe.transpose(s_ps[:, j, i, :], probs[:, j, i, :], ident[:, :])
                last.then_inc(pt_done, 1)

            def project(b, w, src, bank, done):
                for m in range(DC):
                    for c in range(DC):
                        last = pe.matmul(p_ps[bank][:, P * m:P * m + P], w[:, c, P * m:P * m + P],
                                         src[:, b.par, c, :], start=(c == 0), stop=(c == DC - 1))
                last.then_inc(done, 1)

            def values(b, j):
                if j == 0:
                    wait(pe, v_ready, b, 1, 1)
                    wait(pe, oT_ready, b, 1, 0)
                wait(pe, pt_ready, b, QUADS, j + 1)
                for i in range(4):
                    last = pe.matmul(o_ps[32 * i:32 * i + 32, j, :], v_pad[:, b.par, 4 * j + i, :],
                                     probsT[:, j % 2, i, :], start=True, stop=True)
                last.then_inc(pv_done, 1)

            def step(at):
                b0, b1, b2 = at(0), at(1), at(2)
                src = cT if cross else xnT
                if b1:
                    scores(b1, 0)
                    scores(b1, 1)
                if b2:
                    back(b2)
                if b1:
                    scores(b1, 2)
                if b0:
                    x_transpose(b0)
                if b1:
                    scores(b1, 3)
                if b2:
                    on_transpose(b2)
                if b1:
                    probs_transpose(b1, 0)
                if b0:
                    wait(pe, xnT_ready, b0, 1, 1)
                    project(b0, wq, xnT, 0, q_done)
                if b1:
                    values(b1, 0)
                if b2:
                    wait(pe, onT_ready, b2, 1, 1)
                    for c in range(DC):
                        last = pe.matmul(b_ps[:, 0:D], o_nT[:, b2.par, c, :], wo[:, c, :],
                                         start=(c == 0), stop=(c == DC - 1))
                    last.then_inc(wo_done, 1)
                if b1:
                    probs_transpose(b1, 1)
                if b0:
                    if cross:
                        wait(pe, cT_ready, b0, 1, 1)
                    else:
                        wait(pe, k_ready, b0, 1, 0)
                    project(b0, wk, src, 1, k_done)
                if b1:
                    values(b1, 1)
                    probs_transpose(b1, 2)
                if b0:
                    wait(pe, q_ready, b0, 1, 1)
                    for c in range(DC):
                        last = pe.matmul(p_ps[0][:, 0:D], src[:, b0.par, c, :], wv[:, c, :],
                                         start=(c == 0), stop=(c == DC - 1))
                    last.then_inc(v_done, 1)
                if b1:
                    values(b1, 2)
                    probs_transpose(b1, 3)
                    values(b1, 3)
            pipeline(pe, count, 3, step)

        @block.scalar
        def _(act):
            def exps(b, j):
                wait(act, max_ready, b, QUADS, j + 1)
                wait(act, pt_done, b, QUADS, j - 3)
                if j == 0:
                    wait(act, on_ready, b, 1, -1)
                for i in range(4):
                    h = 4 * j + i
                    last = act.activation(probs[:, j, i, :], s_ps[:, j, i, :], ACT.Exp,
                                          bias=neg_max[:, b.par, h:h + 1], scale=1.0,
                                          accum_out=sums[:, b.par, h:h + 1])
                last.then_inc(exp_ready, 1)

            def step(at):
                b0, b1, b2 = at(0), at(1), at(2)
                if b2:
                    wait(act, pv_done, b2, QUADS, QUADS)
                    act.copy(oT[:, :, :], o_ps[:, :, :]).then_inc(oT_ready, 1)
                if b1:
                    exps(b1, 0)
                if b0:
                    wait(act, xt_done, b0, 1, 1)
                    wait(act, v_done if not cross else q_done, b0, 1, -1)
                    act.copy(xnT[:, b0.par, :, :], p_ps[0][:, 0:D].rearrange("p (c t) -> p c t", c=DC))\
                       .then_inc(xnT_ready, 1)
                    if cross:
                        wait(act, ct_done, b0, 1, 1)
                        wait(act, v_done, b0, 1, -1)
                        act.copy(cT[:, b0.par, :, :], p_ps[1][:, 0:D].rearrange("p (c t) -> p c t", c=DC))\
                           .then_inc(cT_ready, 1)
                if b1:
                    exps(b1, 1)
                if b2:
                    wait(act, ont_done, b2, 1, 1)
                    wait(act, wo_done, b2, 1, -1)
                    act.copy(o_nT[:, b2.par, :, :], b_ps[:, 0:D].rearrange("p (c t) -> p c t", c=DC))\
                       .then_inc(onT_ready, 1)
                if b1:
                    exps(b1, 2)
                    exps(b1, 3)
            pipeline(act, count, 3, step)

        @block.vector
        def _(dve):
            dve.memset(v_pad[:, :, :, :], 0.0)
            dve.wait_ge(loaded_w, 16 * n_w)
            dve.tensor_scalar(wq[:, :, :], wq[:, :, :], HD ** -0.5, None, ALU.mult)
            dve.tensor_scalar(bq[:, :], bq[:, :], HD ** -0.5, None, ALU.mult).then_inc(scaled, 1)
            dve.wait_ge(scaled, 1)

            def maxima(b, j):
                wait(dve, s_done, b, QUADS, j + 1)
                if j == 0:
                    wait(dve, exp_ready, b, QUADS, -QUADS)
                dve.tensor_reduce(neg_max[:, b.par, 4 * j:4 * j + 4], s_ps[:, j, :, :], AX.X, ALU.max,
                                  negate=True).then_inc(max_ready, 1)

            def probsT_copy(b, j):
                wait(dve, pt_done, b, QUADS, j + 1)
                wait(dve, pv_done, b, QUADS, j - 1)
                dve.tensor_copy(probsT[:, j % 2, :, :], s_ps[:, j, :, :]).then_inc(pt_ready, 1)

            def step(at):
                b0, b1, b2 = at(0), at(1), at(2)
                if b0:
                    loaded(dve, x_loaded, b0)
                    wait(dve, xt_done, b0, 1, -1)
                    dve.tensor_scalar(xn[:, b0.par, :], x_t[:, b0.par, :], mean[:, bass.ds(b0.n, 1)],
                                      rstd[:, bass.ds(b0.n, 1)], ALU.subtract, ALU.mult).then_inc(xn_ready, 1)
                    if cross:
                        loaded(dve, m_loaded, b0)
                        wait(dve, s_done, b0, QUADS, -QUADS)
                        dve.tensor_scalar(mask_b[:, b0.par, :], mask_t[:, b0.par, :], 0.0, -3.0e38,
                                          ALU.is_equal, ALU.mult).then_inc(mask_ready, 1)
                if b1:
                    maxima(b1, 0)
                if b2:
                    src = sums
                    wait(dve, exp_ready, b2, QUADS, QUADS)
                    if cross:
                        dve.tensor_scalar(sums[:, b2.par, :], sums[:, b2.par, :], 1.0, None, ALU.add)\
                           .then_inc(inv_ready, 1)
                        wait(dve, inv_ready, b2, 2, 1)
                    dve.reciprocal(inv[:, b2.par, :], sums[:, b2.par, :]).then_inc(inv_ready, 1)
                    wait(dve, inv_ready, b2, 1 + cross, 1 + cross)
                    wait(dve, back_done, b2, 1, 1)
                    wait(dve, ont_done, b2, 1, -1)
                    dve.tensor_tensor(o_n[:, b2.par, :].rearrange("p (h d) -> p h d", h=HEADS),
                                      b_ps[:, :].rearrange("p (h d) -> p h d", h=HEADS)[:, :, 0:HD],
                                      inv[:, b2.par, :].unsqueeze(2).to_broadcast([P, HEADS, HD]),
                                      ALU.mult).then_inc(on_ready, 1)
                if b1:
                    maxima(b1, 1)
                    maxima(b1, 2)
                    maxima(b1, 3)
                    probsT_copy(b1, 0)
                if b0:
                    wait(dve, q_done, b0, 1, 1)
                    wait(dve, s_done, b0, QUADS, -QUADS)
                    dve.tensor_tensor(qT[:, b0.par, :, :], p_ps[0][:, 0:D].rearrange("p (c t) -> p c t", c=DC),
                                      bq[:, :].unsqueeze(2).to_broadcast([P, DC, P]), ALU.add)\
                       .then_inc(q_ready, 1)
                if b2:
                    wait(dve, wo_done, b2, 1, 1)
                    wait(dve, r_biased, b2, 1, 1)
                    if not b2.known() or b2.n >= 2:
                        dve.wait_ge(stored[b2.par], (b2.n - b2.par) * 8)
                    dve.tensor_tensor(x_o[:, b2.par, :], b_ps[:, 0:D], x_r[:, b2.par, :], ALU.add)\
                       .then_inc(xo_ready, 1)
                    wait(dve, xo_ready, b2, 1, 1)
                    dve.bn_stats(stats[:, b2.n, :], x_o[:, b2.par, :]).then_inc(stat_ready, 1)
                if b1:
                    probsT_copy(b1, 1)
                if b0:
                    wait(dve, k_done, b0, 1, 1)
                    wait(dve, diag_ready, b0, 1, -1)
                    dve.tensor_tensor(kT[:, b0.par, :, :], p_ps[1][:, 0:D].rearrange("p (c t) -> p c t", c=DC),
                                      bk[:, :].unsqueeze(2).to_broadcast([P, DC, P]), ALU.add)\
                       .then_inc(k_ready, 1)
                if b1:
                    probsT_copy(b1, 2)
                if b0:
                    wait(dve, v_done, b0, 1, 1)
                    wait(dve, pv_done, b0, QUADS, -QUADS)
                    dve.tensor_tensor(v_pad[:, b0.par, :, 0:HD], p_ps[0][:, 0:D].rearrange("p (h d) -> p h d", h=HEADS),
                                      bv[:, :].rearrange("p (h d) -> p h d", h=HEADS), ALU.add)\
                       .then_inc(v_ready, 1)
                if b1:
                    probsT_copy(b1, 3)
            pipeline(dve, count, 3, step)

        @block.gpsimd
        def _(pool):
            pool.wait_ge(loaded_w, 16 * n_w)

            def step(at):
                b0, b1, b2 = at(0), at(1), at(2)
                if b2:
                    loaded(pool, r_loaded, b2)
                    pool.tensor_tensor(x_r[:, b2.par, :], x_r[:, b2.par, :], bo[:, :], ALU.add)\
                        .then_inc(r_biased, 1)
                if b0:
                    wait(pool, k_ready, b0, 1, 1)
                    wait(pool, s_done, b0, QUADS, -QUADS)
                    for c in range(DC):
                        last = pool.tensor_tensor(
                            k_diag[:, b0.par, 8 * c:8 * c + 8, :],
                            kT[:, b0.par, c, :].unsqueeze(1).to_broadcast([P, 8, P]),
                            head_mask[:, :].unsqueeze(2).to_broadcast([P, 8, P]), ALU.mult)
                    last.then_inc(diag_ready, 1)
                if b2:
                    wait(pool, xo_ready, b2, 1, 1)
                    pool.dma_start(x_out[b2.n], x_o[:, b2.par, :]).then_inc(stored[b2.par], 16)
            pipeline(pool, count, 3, step)


HID = 1024
HC = HID // P
EXPERTS = 8
NEG_INF = -1.0e9
ROUNDER = 12582912.0


def expert_tiles(count):
    return 2 * count + EXPERTS - 1


def experts_ffn(nc, x_in, x_out, stats, mean, rstd, ident, w_dram, xg, yg, count=NB):
    name = "moe"
    tiles = expert_tiles(count)
    with ExitStack() as ctx:
        def sb(n, shape, dt=F32, where=None):
            return (where or ctx).enter_context(nc.sbuf_tensor(f"{name}_{n}", shape, dt))

        def ps(n, shape, where):
            return where.enter_context(nc.psum_tensor(f"{name}_ps_{n}", shape, F32))

        sem = Semaphores(nc, ctx, name)

        w1, w2 = sb("w1", [P, EXPERTS, DC, HID]), sb("w2", [P, EXPERTS, HC, D])
        b1, b2 = sb("b1", [P, EXPERTS * HC]), sb("b2", [P, EXPERTS * D])
        slots = sb("slots", [P, 2, count], I32)
        zero_rows = sb("zero_rows", [P, 2], I32)
        share = sb("share", [P, 2, count])
        tile_expert = sb("tile_expert", [1, tiles], I32)
        w1_loaded, w2_loaded, b_loaded = sem("w1_loaded"), sem("w2_loaded"), sem("b_loaded")

        def take_rows(pool, index, b):
            column = slots[:, :, bass.ds(b.n, 1)].rearrange("p a b -> p (a b)")
            return pool.tensor_tensor(index[:, b.par, :], column, zero_rows[:, :], ALU.add)

        with ExitStack() as route:
            wr, br = sb("wr", [P, DC, EXPERTS], where=route), sb("br", [P, EXPERTS], where=route)
            zeros = sb("zeros", [P, D], where=route)
            x_t, xn = sb("x_t", [P, 2, D], where=route), sb("xn", [P, 2, D], where=route)
            xnT = sb("xnT", [P, 2, DC, P], where=route)
            logits = sb("logits", [P, count, EXPERTS], where=route)
            xt_ps, l_ps = ps("xt", [P, 2, 512], route), ps("l", [P, 2, 512], route)
            r_loaded, zero_ready, zero_stored = sem("r_loaded"), sem("zero_ready"), sem.kept("zero_stored")
            x_loaded = [sem("x_loaded0"), sem("x_loaded1")]
            xn_ready, xt_done, xnT_ready, l_done, l_ready = (
                sem(n) for n in ("xn_ready", "xt_done", "xnT_ready", "l_done", "l_ready"))

            with nc.Block() as block:
                @block.sync
                def _(sp):
                    sp.dma_start(wr[:, :, :], w_dram["wr"]).then_inc(r_loaded, 16)
                    sp.dma_start(br[:, :], w_dram["br"]).then_inc(r_loaded, 16)

                    def step(at):
                        b = at(0)
                        if b:
                            wait(sp, xn_ready, b, 1, -1)
                            sp.dma_start(x_t[:, b.par, :], x_in[b.n]).then_inc(x_loaded[b.par], 16)
                    pipeline(sp, count, 1, step)

                @block.gpsimd
                def _(pool):
                    pool.memset(zero_rows[:, :], 0)
                    pool.memset(zeros[:, :], 0.0).then_inc(zero_ready, 1)
                    pool.wait_ge(zero_ready, 1)
                    pool.dma_start(xg.rearrange("(t p) d -> p t d", p=P),
                                   zeros[:, :].unsqueeze(1).to_broadcast([P, tiles, D])).then_inc(zero_stored, 16)
                    pool.wait_ge(zero_stored, 16)

                @block.tensor
                def _(pe):
                    pe.wait_ge(r_loaded, 32)

                    def step(at):
                        b0, b1_ = at(0), at(1)
                        if b0:
                            wait(pe, xn_ready, b0, 1, 1)
                            wait(pe, xnT_ready, b0, 1, -1)
                            for c in range(DC):
                                last = pe.transpose(xt_ps[:, b0.par, P * c:P * c + P], xn[:, b0.par, P * c:P * c + P],
                                                    ident[:, :])
                            last.then_inc(xt_done, 1)
                        if b1_:
                            wait(pe, xnT_ready, b1_, 1, 1)
                            wait(pe, l_ready, b1_, 1, -1)
                            for c in range(DC):
                                last = pe.matmul(l_ps[:, b1_.par, 0:EXPERTS], xnT[:, b1_.par, c, :], wr[:, c, :],
                                                 start=(c == 0), stop=(c == DC - 1))
                            last.then_inc(l_done, 1)
                    pipeline(pe, count, 2, step)

                @block.scalar
                def _(act):
                    act.dma_start(b1[:, :], w_dram["b1"]).then_inc(b_loaded, 16)
                    act.dma_start(b2[:, :], w_dram["b2"]).then_inc(b_loaded, 16)
                    act.dma_start(w1[:, :, :, :], w_dram["w1"]).then_inc(w1_loaded, 16)
                    act.dma_start(w2[:, :, :, :], w_dram["w2"]).then_inc(w2_loaded, 16)

                    def step(at):
                        b = at(0)
                        if b:
                            wait(act, xt_done, b, 1, 1)
                            wait(act, l_done, b, 1, -1)
                            act.copy(xnT[:, b.par, :, :], xt_ps[:, b.par, 0:D].rearrange("p (c t) -> p c t", c=DC))\
                               .then_inc(xnT_ready, 1)
                    pipeline(act, count, 1, step)

                @block.vector
                def _(dve):
                    dve.wait_ge(r_loaded, 32)

                    def step(at):
                        b0, b1_ = at(0), at(1)
                        if b0:
                            dve.wait_ge(x_loaded[b0.par], (b0.n + (2 - b0.par)) * 8)
                            wait(dve, xt_done, b0, 1, -1)
                            dve.tensor_scalar(xn[:, b0.par, :], x_t[:, b0.par, :], mean[:, bass.ds(b0.n, 1)],
                                              rstd[:, bass.ds(b0.n, 1)], ALU.subtract, ALU.mult).then_inc(xn_ready, 1)
                        if b1_:
                            wait(dve, l_done, b1_, 1, 1)
                            dve.tensor_tensor(logits[:, b1_.n, :], l_ps[:, b1_.par, 0:EXPERTS], br[:, :], ALU.add)\
                                .then_inc(l_ready, 1)
                    pipeline(dve, count, 2, step)

            place_tokens(nc, name, route, sb, ps, sem, w_dram, logits, slots, share, tile_expert, tiles, count)

        with ExitStack() as sort:
            x_t, xn = sb("s_x_t", [P, 2, D], where=sort), sb("s_xn", [P, 2, D], where=sort)
            index = sb("s_index", [P, 2, 2], I32, where=sort)
            x_loaded = [sem("s_x_loaded0"), sem("s_x_loaded1")]
            scattered = [sem.kept("scattered0"), sem.kept("scattered1")]
            xn_ready, index_ready = sem("s_xn_ready"), sem("index_ready")
            with nc.Block() as block:
                @block.sync
                def _(sp):
                    def step(at):
                        b = at(0)
                        if b:
                            wait(sp, xn_ready, b, 1, -1)
                            sp.dma_start(x_t[:, b.par, :], x_in[b.n]).then_inc(x_loaded[b.par], 16)
                    pipeline(sp, count, 1, step)

                @block.vector
                def _(dve):
                    def step(at):
                        b = at(0)
                        if b:
                            dve.wait_ge(x_loaded[b.par], (b.n + (2 - b.par)) * 8)
                            if not b.known() or b.n >= 2:
                                dve.wait_ge(scattered[b.par], (b.n - b.par) * 16)
                            dve.tensor_scalar(xn[:, b.par, :], x_t[:, b.par, :], mean[:, bass.ds(b.n, 1)],
                                              rstd[:, bass.ds(b.n, 1)], ALU.subtract, ALU.mult).then_inc(xn_ready, 1)
                    pipeline(dve, count, 1, step)

                @block.gpsimd
                def _(pool):
                    def step(at):
                        b0, b1_ = at(0), at(1)
                        if b1_:
                            wait(pool, index_ready, b1_, 1, 1)
                            wait(pool, xn_ready, b1_, 1, 1)
                        if b0:
                            if not b0.known() or b0.n >= 2:
                                pool.wait_ge(scattered[b0.par], (b0.n - b0.par) * 16)
                            take_rows(pool, index, b0).then_inc(index_ready, 1)
                        if b1_:
                            for k in range(2):
                                pool.indirect_dma_start(
                                    xg, bass.IndirectOffsetOnAxis(ap=index[:, b1_.par, k:k + 1], axis=0),
                                    xn[:, b1_.par, :], None).then_inc(scattered[b1_.par], 16)
                    pipeline(pool, count, 2, step)
                    for par in range(2):
                        pool.wait_ge(scattered[par], 16 * count)

        with ExitStack() as work:
            x_t, y_o = sb("e_x_t", [P, 2, D], where=work), sb("e_y_o", [P, 2, D], where=work)
            xT = sb("e_xT", [P, 2, DC, P], where=work)
            h = sb("e_h", [P, HID], where=work)
            h_b, hT = sb("e_h_b", [P, HC, P], where=work), sb("e_hT", [P, HC, P], where=work)
            x_ps, y_ps = ps("e_x", [P, 512], work), ps("e_y", [P, 512], work)
            h_ps, ht_ps = ps("e_h", [P, 2, 512], work), ps("e_ht", [P, 2, 4, P], work)
            x_loaded = [sem("e_x_loaded0"), sem("e_x_loaded1")]
            stored = [sem.kept("e_stored0"), sem.kept("e_stored1")]
            xt_done, xT_ready, h_done, h_ready, ht_done, hb_ready, hT_ready, y_done, y_ready = (
                sem(f"e_{n}") for n in ("xt_done", "xT_ready", "h_done", "h_ready", "ht_done", "hb_ready",
                                        "hT_ready", "y_done", "y_ready"))

            def expert_of(eng, t):
                column = tile_expert[0:1, t.n:t.n + 1] if t.known() else tile_expert[0:1, bass.ds(t.n, 1)]
                return eng.value_load(column, min_val=0, max_val=EXPERTS - 1)

            with nc.Block() as block:
                @block.sync
                def _(sp):
                    def step(at):
                        t = at(0)
                        if t:
                            wait(sp, xt_done, t, 1, -1)
                            sp.dma_start(x_t[:, t.par, :], xg.rearrange("(t p) d -> t p d", p=P)[t.n])\
                              .then_inc(x_loaded[t.par], 16)
                    pipeline(sp, tiles, 1, step)

                @block.tensor
                def _(pe):
                    def h_transpose(t, j):
                        wait(pe, h_ready, t, 2, j + 1)
                        wait(pe, hb_ready, t, 2, j - 1)
                        for c in range(4):
                            col = P * (4 * j + c)
                            last = pe.transpose(ht_ps[:, j, c, :], h[:, col:col + P], ident[:, :])
                        last.then_inc(ht_done, 1)

                    pe.wait_ge(w1_loaded, 16)
                    pe.wait_ge(w2_loaded, 16)

                    def step(at):
                        t0, t1 = at(0), at(1)
                        if t1:
                            h_transpose(t1, 0)
                        if t0:
                            pe.wait_ge(x_loaded[t0.par], (t0.n + (2 - t0.par)) * 8)
                            wait(pe, xT_ready, t0, 1, 0)
                            for c in range(DC):
                                last = pe.transpose(x_ps[:, P * c:P * c + P], x_t[:, t0.par, P * c:P * c + P], ident[:, :])
                            last.then_inc(xt_done, 1)
                        if t1:
                            h_transpose(t1, 1)
                        if t0:
                            e0 = expert_of(pe, t0)
                            wait(pe, xT_ready, t0, 1, 1)
                            for j in range(2):
                                wait(pe, h_ready, t0, 2, j - 1)
                                for c in range(DC):
                                    last = pe.matmul(h_ps[:, j, :], xT[:, t0.par, c, :],
                                                     w1[:, bass.ds(e0, 1), c, 512 * j:512 * j + 512].rearrange("p a n -> p (a n)"),
                                                     start=(c == 0), stop=(c == DC - 1))
                                last.then_inc(h_done, 1)
                        if t1:
                            e1 = expert_of(pe, t1)
                            wait(pe, hT_ready, t1, 2, 2)
                            wait(pe, y_ready, t1, 1, 0)
                            for c in range(HC):
                                last = pe.matmul(y_ps[:, 0:D], hT[:, c, :],
                                                 w2[:, bass.ds(e1, 1), c, :].rearrange("p a n -> p (a n)"),
                                                 start=(c == 0), stop=(c == HC - 1))
                            last.then_inc(y_done, 1)
                    pipeline(pe, tiles, 2, step)

                @block.scalar
                def _(act):
                    def step(at):
                        t0, t1 = at(0), at(1)
                        if t0:
                            wait(act, xt_done, t0, 1, 1)
                            wait(act, h_done, t0, 2, -2)
                            act.copy(xT[:, t0.par, :, :], x_ps[:, 0:D].rearrange("p (c t) -> p c t", c=DC))\
                               .then_inc(xT_ready, 1)
                        if t1:
                            for j in range(2):
                                wait(act, hb_ready, t1, 2, j + 1)
                                wait(act, y_done, t1, 1, 0)
                                act.activation(hT[:, 4 * j:4 * j + 4, :], h_b[:, 4 * j:4 * j + 4, :], ACT.Relu)\
                                   .then_inc(hT_ready, 1)
                        if t0:
                            for j in range(2):
                                wait(act, h_done, t0, 2, j + 1)
                                wait(act, ht_done, t0, 2, 0)
                                act.copy(h[:, 512 * j:512 * j + 512], h_ps[:, j, :]).then_inc(h_ready, 1)
                    pipeline(act, tiles, 2, step)

                @block.vector
                def _(dve):
                    dve.wait_ge(b_loaded, 32)

                    def step(at):
                        t1, t2 = at(1), at(2)
                        if t1:
                            e1 = expert_of(dve, t1)
                            for j in range(2):
                                wait(dve, ht_done, t1, 2, j + 1)
                                wait(dve, hT_ready, t1, 2, j - 1)
                                dve.tensor_tensor(h_b[:, 4 * j:4 * j + 4, :], ht_ps[:, j, :, :],
                                                  b1[:, bass.ds(e1 * HC + 4 * j, 4)].unsqueeze(2).to_broadcast([P, 4, P]),
                                                  ALU.add).then_inc(hb_ready, 1)
                            if not t1.known() or t1.n >= 2:
                                dve.wait_ge(stored[t1.par], (t1.n - t1.par) * 8)
                            wait(dve, y_done, t1, 1, 1)
                            dve.tensor_tensor(y_o[:, t1.par, :], y_ps[:, 0:D], b2[:, bass.ds(e1 * D, D)], ALU.add)\
                                .then_inc(y_ready, 1)
                    pipeline(dve, tiles, 2, step)

                @block.gpsimd
                def _(pool):
                    def step(at):
                        t1 = at(1)
                        if t1:
                            wait(pool, y_ready, t1, 1, 1)
                            pool.dma_start(yg.rearrange("(t p) d -> t p d", p=P)[t1.n], y_o[:, t1.par, :])\
                                .then_inc(stored[t1.par], 16)
                    pipeline(pool, tiles, 2, step)
                    for par in range(2):
                        pool.wait_ge(stored[par], 16 * ((tiles + 1 - par) // 2))

        with ExitStack() as join:
            x_t, x_o, part = (sb(f"j_{n}", [P, 2, D], where=join) for n in ("x_t", "x_o", "part"))
            y = sb("j_y", [P, 2, 2, D], where=join)
            index = sb("j_index", [P, 2, 2], I32, where=join)
            x_loaded, stored = ([sem(f"j_{n}{i}") for i in range(2)] for n in ("x_loaded", "stored"))
            gathered = [sem.kept("gathered0"), sem.kept("gathered1")]
            index_ready, part_ready, xo_ready, stat_ready = (
                sem(f"j_{n}") for n in ("index_ready", "part_ready", "xo_ready", "stat_ready"))
            with nc.Block() as block:
                @block.sync
                def _(sp):
                    def step(at):
                        b, b1_ = at(0), at(1)
                        if b:
                            wait(sp, part_ready, b, 1, -1)
                            sp.dma_start(x_t[:, b.par, :], x_in[b.n]).then_inc(x_loaded[b.par], 16)
                        if b1_:
                            wait(sp, xo_ready, b1_, 1, 1)
                            sp.dma_start(x_out[b1_.n], x_o[:, b1_.par, :]).then_inc(stored[b1_.par], 16)
                    pipeline(sp, count, 2, step)
                    for par in range(2):
                        sp.wait_ge(stored[par], 16 * (count // 2))

                @block.gpsimd
                def _(pool):
                    def step(at):
                        b0, b1_ = at(0), at(1)
                        if b1_:
                            wait(pool, index_ready, b1_, 1, 1)
                            wait(pool, xo_ready, b1_, 1, -1)
                        if b0:
                            if not b0.known() or b0.n >= 2:
                                pool.wait_ge(gathered[b0.par], (b0.n - b0.par) * 16)
                            take_rows(pool, index, b0).then_inc(index_ready, 1)
                        if b1_:
                            for k in range(2):
                                pool.indirect_dma_start(
                                    y[:, b1_.par, k, :], None, yg,
                                    bass.IndirectOffsetOnAxis(ap=index[:, b1_.par, k:k + 1], axis=0))\
                                    .then_inc(gathered[b1_.par], 16)
                    pipeline(pool, count, 2, step)

                @block.vector
                def _(dve):
                    def step(at):
                        b1_ = at(0)
                        if b1_:
                            dve.wait_ge(x_loaded[b1_.par], (b1_.n + (2 - b1_.par)) * 8)
                            dve.wait_ge(gathered[b1_.par], (b1_.n + (2 - b1_.par)) * 16)
                            dve.scalar_tensor_tensor(out=part[:, b1_.par, :], in0=y[:, b1_.par, 0, :],
                                                     scalar=share[:, 0, bass.ds(b1_.n, 1)], in1=x_t[:, b1_.par, :],
                                                     op0=ALU.mult, op1=ALU.add).then_inc(part_ready, 1)
                            wait(dve, part_ready, b1_, 1, 1)
                            if not b1_.known() or b1_.n >= 2:
                                dve.wait_ge(stored[b1_.par], (b1_.n - b1_.par) * 8)
                            dve.scalar_tensor_tensor(out=x_o[:, b1_.par, :], in0=y[:, b1_.par, 1, :],
                                                     scalar=share[:, 1, bass.ds(b1_.n, 1)], in1=part[:, b1_.par, :],
                                                     op0=ALU.mult, op1=ALU.add).then_inc(xo_ready, 1)
                            wait(dve, xo_ready, b1_, 1, 1)
                            dve.bn_stats(stats[:, b1_.n, :], x_o[:, b1_.par, :]).then_inc(stat_ready, 1)
                    pipeline(dve, count, 1, step)

        sem.clear()


def place_tokens(nc, name, where, sb, ps, sem, w_dram, logits, slots, share, tile_expert, tiles, count):
    shape = [P, count, EXPERTS]
    falling = sb("falling", [P, EXPERTS], where=where)
    before, ones = sb("before", [P, P], where=where), sb("ones", [P, P], where=where)
    tile_no = sb("tile_no", [1, tiles], where=where)
    first, second, equal, rest = (sb(n, shape, where=where) for n in ("first", "second", "equal", "rest"))
    chosen, sums, run_a, run_b = (sb(n, shape, where=where) for n in ("chosen", "sums", "run_a", "run_b"))
    top1, top2, key, high, floor_, total = (sb(n, [P, count], where=where) for n in ("top1", "top2", "key", "high", "floor", "total"))
    n_tiles, end_a, end_b, base = (sb(n, [P, EXPERTS], where=where) for n in ("n_tiles", "end_a", "end_b", "base"))
    passed = sb("passed", [1, tiles, EXPERTS], where=where)
    number = sb("number", [1, tiles], where=where)
    rank_ps, sum_ps = ps("rank", [P, count * EXPERTS], where), ps("sum", [P, count * EXPERTS], where)
    loaded, dve_step, chosen_ready, counted, diffs_ready, exps_ready = (
        sem(f"p_{n}") for n in ("loaded", "dve_step", "chosen_ready", "counted", "diffs_ready", "exps_ready"))

    def flat(t):
        return t[:, :, :].rearrange("p b e -> p (b e)")

    with nc.Block() as block:
        @block.sync
        def _(sp):
            for dst, key_ in ((falling, "falling"), (before, "before"), (ones, "ones"), (tile_no, "tile_no")):
                sp.dma_start(dst[:, :], w_dram[key_]).then_inc(loaded, 16)

        @block.tensor
        def _(pe):
            pe.wait_ge(loaded, 64)
            pe.wait_ge(chosen_ready, 1)
            pe.matmul(rank_ps[:, :], before[:, :], flat(chosen), start=True, stop=True)
            pe.matmul(sum_ps[:, :], ones[:, :], flat(chosen), start=True, stop=True).then_inc(counted, 1)

        @block.scalar
        def _(act):
            act.wait_ge(diffs_ready, 1)
            for t in (top1, top2, floor_):
                last = act.activation(t[:, :], t[:, :], ACT.Exp)
            last.then_inc(exps_ready, 1)

        @block.vector
        def _(dve):
            link = chained(dve, dve_step)
            experts = falling[:, :].unsqueeze(1).to_broadcast(shape)

            def over_experts(t):
                return t[:, :].unsqueeze(2).to_broadcast(shape)

            def largest(scores, top, one_hot):
                link(dve.tensor_reduce(top[:, :], scores[:, :, :], AX.X, ALU.max))
                link(dve.tensor_tensor(equal[:, :, :], scores[:, :, :], over_experts(top), ALU.is_equal))
                link(dve.tensor_tensor(equal[:, :, :], equal[:, :, :], experts, ALU.mult))
                link(dve.tensor_reduce(key[:, :], equal[:, :, :], AX.X, ALU.max))
                link(dve.tensor_tensor(one_hot[:, :, :], experts, over_experts(key), ALU.is_equal))

            dve.wait_ge(loaded, 64)
            largest(logits, top1, first)
            link(dve.scalar_tensor_tensor(out=flat(rest), in0=flat(first), scalar=-3.0e38, in1=flat(logits),
                                          op0=ALU.mult, op1=ALU.add))
            largest(rest, top2, second)
            link(dve.tensor_tensor(flat(chosen), flat(first), flat(second), ALU.add))
            dve.sem_inc(chosen_ready, 1)

            link(dve.tensor_scalar(high[:, :], top1[:, :], NEG_INF, None, ALU.max))
            link(dve.tensor_tensor(top1[:, :], top1[:, :], high[:, :], ALU.subtract))
            link(dve.tensor_tensor(top2[:, :], top2[:, :], high[:, :], ALU.subtract))
            link(dve.tensor_scalar(floor_[:, :], high[:, :], -1.0, NEG_INF, ALU.mult, ALU.add))
            dve.sem_inc(diffs_ready, 1)
            dve.wait_ge(exps_ready, 1)
            link(dve.tensor_tensor(total[:, :], top1[:, :], top2[:, :], ALU.add))
            link(dve.scalar_tensor_tensor(out=total[:, :], in0=floor_[:, :], scalar=float(EXPERTS - 2), in1=total[:, :],
                                          op0=ALU.mult, op1=ALU.add))
            link(dve.reciprocal(total[:, :], total[:, :]))
            link(dve.tensor_tensor(share[:, 0, :], top1[:, :], total[:, :], ALU.mult))
            link(dve.tensor_tensor(share[:, 1, :], top2[:, :], total[:, :], ALU.mult))

            dve.wait_ge(counted, 1)
            link(dve.tensor_copy(flat(sums), sum_ps[:, :]))
            link(dve.tensor_copy(flat(run_a), flat(sums)))
            src, dst = run_a, run_b
            shift = 1
            while shift < count:
                link(dve.tensor_copy(dst[:, 0:shift, :], src[:, 0:shift, :]))
                link(dve.tensor_tensor(dst[:, shift:, :], src[:, shift:, :], src[:, :count - shift, :], ALU.add))
                src, dst, shift = dst, src, 2 * shift
            run = src
            link(dve.tensor_scalar(n_tiles[:, :], run[:, count - 1, :], 1.0 / P, (P - 1) / P - 0.5 + 0.5 / P, ALU.mult, ALU.add))
            link(dve.tensor_scalar(n_tiles[:, :], n_tiles[:, :], ROUNDER, ROUNDER, ALU.add, ALU.subtract))
            link(dve.tensor_copy(end_a[:, :], n_tiles[:, :]))
            end, other, shift = end_a, end_b, 1
            while shift < EXPERTS:
                link(dve.tensor_copy(other[:, 0:shift], end[:, 0:shift]))
                link(dve.tensor_tensor(other[:, shift:], end[:, shift:], end[:, :EXPERTS - shift], ALU.add))
                end, other, shift = other, end, 2 * shift
            link(dve.tensor_tensor(base[:, :], end[:, :], n_tiles[:, :], ALU.subtract))
            link(dve.tensor_scalar(base[:, :], base[:, :], float(P), None, ALU.mult))
            link(dve.tensor_tensor(flat(run), flat(run), flat(sums), ALU.subtract))
            link(dve.tensor_tensor(flat(run), rank_ps[:, :], flat(run), ALU.add))
            link(dve.tensor_tensor(run[:, :, :], run[:, :, :], base[:, :].unsqueeze(1).to_broadcast(shape), ALU.add))
            for k, one_hot in enumerate((first, second)):
                link(dve.tensor_tensor(flat(one_hot), flat(one_hot), flat(run), ALU.mult))
                link(dve.tensor_reduce(key[:, :], one_hot[:, :, :], AX.X, ALU.add))
                link(dve.tensor_copy(slots[:, k, :], key[:, :]))
            link(dve.tensor_tensor(passed[:, :, :], end[0:1, :].unsqueeze(1).to_broadcast([1, tiles, EXPERTS]),
                                   tile_no[:, :].unsqueeze(2).to_broadcast([1, tiles, EXPERTS]), ALU.is_le))
            link(dve.tensor_reduce(number[:, :], passed[:, :, :], AX.X, ALU.add))
            link(dve.tensor_scalar(number[:, :], number[:, :], float(EXPERTS - 1), None, ALU.min))
            link(dve.tensor_copy(tile_expert[:, :], number[:, :]))


RES = float(1.0 / np.sqrt(2.0))
CHUNK = 64
HC = HID // P
RMS_EPS = 1e-6
Q_EPS = float(np.finfo(np.float32).eps)


def mixer(nc, x_in, x_out, stats, mean, rstd, scale, ident, w_dram, count=NB):
    name = "mix"
    with ExitStack() as ctx:
        def sb(n, shape, dt=F32):
            return ctx.enter_context(nc.sbuf_tensor(f"{name}_{n}", shape, dt))

        def ps(n, shape):
            return ctx.enter_context(nc.psum_tensor(f"{name}_{n}", shape, F32))

        sem = Semaphores(nc, ctx, name)

        w_in = sb("w_in", [P, DC, 5 * D])
        w_out = sb("w_out", [P, DC, D])
        w_fc = sb("w_fc", [P, DC, HID])
        w_pr = sb("w_pr", [P, HC, D])
        norm1, norm2 = sb("norm1", [P, DC]), sb("norm2", [P, DC])
        x_t, x_again, x_ln, h_n, x_1, x_s, h2_n, x_o, junk = (
            sb(n, [P, 2, D]) for n in ("x_t", "x_again", "x_ln", "h_n", "x_1", "x_s", "h2_n", "x_o", "junk"))
        hT, h2T, vT, kT, uT, aT, gT, prefix, inv_prefix, accT, memT, zT, yT = (
            sb(n, [P, 2, DC, P]) for n in ("hT", "h2T", "vT", "kT", "uT", "aT", "gT", "prefix", "inv_prefix",
                                           "accT", "memT", "zT", "yT"))
        q_t, q_sq, q_n = (sb(n, [P, 2, D]) for n in ("q_t", "q_sq", "q_n"))
        q_ms, q_r = sb("q_ms", [P, 2, HEADS]), sb("q_r", [P, 2, HEADS])
        x_ms, x_r = sb("x_ms", [P, 2]), sb("x_r", [P, 2])
        ones, consts = sb("ones", [P, CHUNK]), sb("consts", [P, 4])
        t_fc = sb("t_fc", [P, 2, 512])
        sT = sb("sT", [P, 2, HC, P])
        f_ps = [ps("f0", [P, 512]), ps("f1", [P, 512])]
        kv_ps, ag_ps, q_ps, t_ps, o_ps, m_ps = (ps(n, [P, 512]) for n in ("kv", "ag", "q", "t", "o", "m"))

        loaded_w, folded, const_ready = sem("loaded_w"), sem("folded"), sem("const_ready")
        x_loaded = [sem("x_loaded0"), sem("x_loaded1")]
        again_loaded = [sem("again_loaded0"), sem("again_loaded1")]
        stored = [sem.kept("stored0"), sem.kept("stored1")]
        h_ready, tx_done, hT_ready = sem("h_ready"), sem("tx_done"), sem("hT_ready")
        q_done, q_copied, qsq_ready, qms_ready, qr_ready, qn_ready, qt_done = (
            sem(n) for n in ("q_done", "q_copied", "qsq_ready", "qms_ready", "qr_ready", "qn_ready", "qt_done"))
        kv_done, kv_ready, ag_done, ag_ready, u_ready = (
            sem(n) for n in ("kv_done", "kv_ready", "ag_done", "ag_ready", "u_ready"))
        scan_step, y_ready, out_done, x1_ready, ms_ready, xr_ready, xs_ready = (
            sem(n) for n in ("scan_step", "y_ready", "out_done", "x1_ready", "ms_ready", "xr_ready", "xs_ready"))
        h2_ready, h2t_done, h2T_ready = sem("h2_ready"), sem("h2t_done"), sem("h2T_ready")
        fc_done, tanh_ready, s_ready, pr_done, xo_ready = (
            sem(n) for n in ("fc_done", "tanh_ready", "s_ready", "pr_done", "xo_ready"))
        half_ready, xr_step, clip_step, qr_step = (sem(n) for n in ("half_ready", "xr_step", "clip_step", "qr_step"))
        z_ready, gated = sem("z_ready"), sem("gated")
        ctx.callback(sem.clear)
        block = ctx.enter_context(nc.Block())

        def loaded(eng, sems, b):
            eng.wait_ge(sems[b.par], (b.n + (2 - b.par)) * 8)

        @block.sync
        def _(sp):
            for dst, key in ((w_in, "w_in"), (w_out, "w_out"), (w_fc, "w_fc"), (w_pr, "w_pr")):
                sp.dma_start(dst[:, :, :], w_dram[key]).then_inc(loaded_w, 16)
            for dst, key in ((norm1, "norm1"), (norm2, "norm2")):
                sp.dma_start(dst[:, :], w_dram[key]).then_inc(loaded_w, 16)

            def step(at):
                b0, b1, b3 = at(0), at(1), at(3)
                if b0:
                    wait(sp, h_ready, b0, 1, -1)
                    sp.dma_start(x_t[:, b0.par, :], x_in[b0.n]).then_inc(x_loaded[b0.par], 16)
                if b1:
                    wait(sp, xs_ready, b1, 1, -1)
                    sp.dma_start(x_again[:, b1.par, :], x_in[b1.n]).then_inc(again_loaded[b1.par], 16)
                if b3:
                    wait(sp, xo_ready, b3, 1, 1)
                    sp.dma_start(x_out[b3.n], x_o[:, b3.par, :]).then_inc(stored[b3.par], 16)
            pipeline(sp, count, 4, step)
            for par in range(2):
                sp.wait_ge(stored[par], 16 * (count // 2))

        @block.tensor
        def _(pe):
            pe.wait_ge(folded, 2)

            def transposes(src, b, done):
                for c in range(DC):
                    last = pe.transpose(t_ps[:, P * c:P * c + P], src[:, b.par, P * c:P * c + P], ident[:, :])
                last.then_inc(done, 1)

            def channels(b, bank, part0, parts, done):
                for m in range(parts * DC):
                    col = part0 * D + P * m
                    for c in range(DC):
                        last = pe.matmul(bank[:, P * m:P * m + P], w_in[:, c, col:col + P],
                                         hT[:, b.par, c, :], start=(c == 0), stop=(c == DC - 1))
                last.then_inc(done, 1)

            def hidden(b, j):
                wait(pe, h2T_ready, b, 1, 1)
                wait(pe, s_ready, b, 2, j - 1)
                for m in range(4):
                    for c in range(DC):
                        last = pe.matmul(f_ps[j][:, P * m:P * m + P],
                                         w_fc[:, c, 512 * j + P * m:512 * j + P * m + P],
                                         h2T[:, b.par, c, :], start=(c == 0), stop=(c == DC - 1))
                last.then_inc(fc_done, 1)

            def project(b, j):
                wait(pe, s_ready, b, 2, j + 1)
                if j == 0:
                    wait(pe, xo_ready, b, 1, 0)
                for c in range(4 * j, 4 * j + 4):
                    last = pe.matmul(m_ps[:, 0:D], sT[:, b.par, c, :], w_pr[:, c, :],
                                     start=(c == 0), stop=(c == HC - 1))
                if j == 1:
                    last.then_inc(pr_done, 1)

            def step(at):
                b0, b1, b2, b3 = at(0), at(1), at(2), at(3)
                if b3:
                    project(b3, 0)
                if b2:
                    wait(pe, h2_ready, b2, 1, 1)
                    wait(pe, z_ready, b2, 1, 1)
                    transposes(h2_n, b2, h2t_done)
                if b3:
                    project(b3, 1)
                if b0:
                    wait(pe, h_ready, b0, 1, 1)
                    if b2:
                        wait(pe, h2T_ready, b2, 1, 1)
                    transposes(h_n, b0, tx_done)
                if b2:
                    hidden(b2, 0)
                if b1:
                    wait(pe, qn_ready, b1, 1, 1)
                    if b0:
                        wait(pe, hT_ready, b0, 1, 1)
                    transposes(q_n, b1, qt_done)
                if b2:
                    hidden(b2, 1)
                if b0:
                    wait(pe, hT_ready, b0, 1, 1)
                    wait(pe, q_copied, b0, 1, 0)
                    for c in range(DC):
                        last = pe.matmul(q_ps[:, 0:D], hT[:, b0.par, c, :], w_in[:, c, 0:D],
                                         start=(c == 0), stop=(c == DC - 1))
                    last.then_inc(q_done, 1)
                    wait(pe, kv_ready, b0, 1, 0)
                    channels(b0, kv_ps, 1, 2, kv_done)
                if b1:
                    wait(pe, y_ready, b1, 1, 1)
                    wait(pe, x1_ready, b1, 1, 0)
                    for c in range(DC):
                        last = pe.matmul(o_ps[:, 0:D], yT[:, b1.par, c, :], w_out[:, c, :],
                                         start=(c == 0), stop=(c == DC - 1))
                    last.then_inc(out_done, 1)
                if b0:
                    wait(pe, ag_ready, b0, 1, 0)
                    channels(b0, ag_ps, 3, 2, ag_done)
            pipeline(pe, count, 4, step)

        @block.scalar
        def _(act):
            def step(at):
                b0, b1, b2 = at(0), at(1), at(2)
                if b2:
                    wait(act, h2t_done, b2, 1, 1)
                    wait(act, fc_done, b2, 2, -2)
                    act.copy(h2T[:, b2.par, :, :], t_ps[:, 0:D].rearrange("p (c t) -> p c t", c=DC))\
                       .then_inc(h2T_ready, 1)
                if b0:
                    wait(act, tx_done, b0, 1, 1)
                    wait(act, ag_done, b0, 1, -1)
                    act.copy(hT[:, b0.par, :, :], t_ps[:, 0:D].rearrange("p (c t) -> p c t", c=DC))\
                       .then_inc(hT_ready, 1)
                if b2:
                    for j in range(2):
                        wait(act, fc_done, b2, 2, j + 1)
                        wait(act, s_ready, b2, 2, j - 1)
                        act.activation(t_fc[:, j, :], f_ps[j][:, :], ACT.Tanh, scale=0.5).then_inc(tanh_ready, 1)
                if b0:
                    wait(act, q_done, b0, 1, 1)
                    wait(act, qn_ready, b0, 1, -1)
                    act.copy(q_t[:, b0.par, :], q_ps[:, 0:D]).then_inc(q_copied, 1)
                    wait(act, kv_done, b0, 1, 1)
                    wait(act, u_ready, b0, 1, -1)
                    wait(act, y_ready, b0, 1, -1)
                    act.activation(kT[:, b0.par, :, :], kv_ps[:, 0:D].rearrange("p (c t) -> p c t", c=DC), ACT.Tanh)
                    act.copy(vT[:, b0.par, :, :], kv_ps[:, D:2 * D].rearrange("p (c t) -> p c t", c=DC))\
                       .then_inc(kv_ready, 1)
                if b1:
                    wait(act, x1_ready, b1, 1, 1)
                    wait(act, xr_ready, b1, 1, -1)
                    act.activation(junk[:, b1.par, :], x_1[:, b1.par, :], ACT.Square, scale=D ** -0.5,
                                   accum_out=x_ms[:, b1.par:b1.par + 1]).then_inc(ms_ready, 1)
                if b0:
                    wait(act, ag_done, b0, 1, 1)
                    wait(act, scan_step, b0, 9, 1 - 18)
                    act.activation(aT[:, b0.par, :, :], ag_ps[:, 0:D].rearrange("p (c t) -> p c t", c=DC),
                                   ACT.Tanh, bias=one_col[:, :], scale=0.5)
                    act.activation(gT[:, b0.par, :, :], ag_ps[:, D:2 * D].rearrange("p (c t) -> p c t", c=DC),
                                   ACT.Tanh, scale=0.5).then_inc(ag_ready, 1)
            one_col = ones[:, 0:1]
            act.wait_ge(const_ready, 1)
            pipeline(act, count, 3, step)

        @block.vector
        def _(dve):
            dve.memset(ones[:, :], 1.0).then_inc(const_ready, 1)
            dve.wait_ge(loaded_w, 16 * 6)
            for c in range(DC):
                dve.tensor_scalar(w_in[:, c, :], w_in[:, c, :], norm1[:, c:c + 1], None, ALU.mult)
                last = dve.tensor_scalar(w_fc[:, c, :], w_fc[:, c, :], norm2[:, c:c + 1], None, ALU.mult)
                last.then_inc(folded, 1)
            dve.wait_ge(folded, 2)
            STEPS = 9

            def step(at):
                b0, b1, b2, b3 = at(0), at(1), at(2), at(3)
                if b0:
                    loaded(dve, x_loaded, b0)
                    wait(dve, tx_done, b0, 1, -1)
                    dve.tensor_scalar(h_n[:, b0.par, :], x_t[:, b0.par, :], mean[:, bass.ds(b0.n, 1)],
                                      scale[:, bass.ds(b0.n, 1)], ALU.subtract, ALU.mult)
                    dve.tensor_scalar(x_ln[:, b0.par, :], x_t[:, b0.par, :], mean[:, bass.ds(b0.n, 1)],
                                      rstd[:, bass.ds(b0.n, 1)], ALU.subtract, ALU.mult).then_inc(h_ready, 1)
                if b1:
                    wait(dve, ag_ready, b1, 1, 1)
                    dve.tensor_scalar(aT[:, b1.par, :, :], aT[:, b1.par, :, :], 0.5, 0.5, ALU.mult, ALU.add)\
                       .then_inc(clip_step, 1)
                    wait(dve, clip_step, b1, 2, 1)
                    dve.tensor_scalar(aT[:, b1.par, :, :], aT[:, b1.par, :, :], 0.9995, 0.6, ALU.min, ALU.max)\
                       .then_inc(clip_step, 1)
                    wait(dve, clip_step, b1, 2, 2)
                    for c in range(DC):
                        for s in range(P // CHUNK):
                            part = slice(CHUNK * s, CHUNK * s + CHUNK)
                            last = dve.tensor_tensor_scan(prefix[:, b1.par, c, part], aT[:, b1.par, c, part],
                                                          ones[:, :], 1.0, ALU.mult, ALU.mult)
                    last.then_inc(scan_step, 1)
                    wait(dve, scan_step, b1, STEPS, 1)
                    dve.tensor_scalar(inv_prefix[:, b1.par, :, :], prefix[:, b1.par, :, :], 1e-6, None, ALU.max)\
                       .then_inc(scan_step, 1)
                    wait(dve, scan_step, b1, STEPS, 2)
                    dve.reciprocal(inv_prefix[:, b1.par, :, :], inv_prefix[:, b1.par, :, :]).then_inc(scan_step, 1)
                    wait(dve, qr_ready, b1, 1, 1)
                    wait(dve, qt_done, b1, 1, -1)
                    dve.tensor_tensor(q_n[:, b1.par, :].rearrange("p (h d) -> p h d", h=HEADS),
                                      q_t[:, b1.par, :].rearrange("p (h d) -> p h d", h=HEADS),
                                      q_r[:, b1.par, :].unsqueeze(2).to_broadcast([P, HEADS, HD]),
                                      ALU.mult).then_inc(qn_ready, 1)
                    wait(dve, scan_step, b1, STEPS, 3)
                    wait(dve, u_ready, b1, 1, 1)
                    dve.tensor_tensor(inv_prefix[:, b1.par, :, :], inv_prefix[:, b1.par, :, :],
                                      uT[:, b1.par, :, :], ALU.mult).then_inc(scan_step, 1)
                    wait(dve, scan_step, b1, STEPS, 4)
                if b3:
                    wait(dve, pr_done, b3, 1, 1)
                    wait(dve, xs_ready, b3, 1, 1)
                    if not b3.known() or b3.n >= 2:
                        dve.wait_ge(stored[b3.par], (b3.n - b3.par) * 8)
                    dve.scalar_tensor_tensor(out=x_o[:, b3.par, :], in0=m_ps[:, 0:D], scalar=0.5 * RES,
                                             in1=x_s[:, b3.par, :], op0=ALU.mult, op1=ALU.add)\
                       .then_inc(xo_ready, 1)
                    wait(dve, xo_ready, b3, 1, 1)
                    dve.bn_stats(stats[:, b3.n, :], x_o[:, b3.par, :])
                if b1:
                    for s in range(P // CHUNK):
                        part = slice(CHUNK * s, CHUNK * s + CHUNK)
                        for c in range(DC):
                            first = 0.0 if s == 0 else memT[:, b1.par, c, CHUNK * s - 1:CHUNK * s]
                            last = dve.tensor_tensor_scan(accT[:, b1.par, c, part], ones[:, :],
                                                          inv_prefix[:, b1.par, c, part], first,
                                                          ALU.mult, ALU.add)
                        last.then_inc(scan_step, 1)
                        wait(dve, scan_step, b1, STEPS, 5 + 2 * s)
                        dve.tensor_tensor(memT[:, b1.par, :, part], accT[:, b1.par, :, part],
                                          prefix[:, b1.par, :, part], ALU.mult).then_inc(scan_step, 1)
                        wait(dve, scan_step, b1, STEPS, 6 + 2 * s)
                    wait(dve, qt_done, b1, 1, 1)
                    dve.tensor_tensor(zT[:, b1.par, :, :], t_ps[:, 0:D].rearrange("p (c t) -> p c t", c=DC),
                                      memT[:, b1.par, :, :], ALU.mult).then_inc(z_ready, 1)
                    wait(dve, z_ready, b1, 1, 1)
                    dve.tensor_tensor(zT[:, b1.par, :, :], zT[:, b1.par, :, :], vT[:, b1.par, :, :],
                                      ALU.subtract).then_inc(scan_step, 1)
                    wait(dve, scan_step, b1, STEPS, 9)
                    wait(dve, out_done, b1, 1, -1)
                    dve.scalar_tensor_tensor(out=zT[:, b1.par, :, :], in0=gT[:, b1.par, :, :], scalar=1.0,
                                             in1=zT[:, b1.par, :, :], op0=ALU.add, op1=ALU.mult)\
                       .then_inc(gated, 1)
                    wait(dve, gated, b1, 1, 1)
                    dve.scalar_tensor_tensor(out=yT[:, b1.par, :, :], in0=zT[:, b1.par, :, :], scalar=0.5,
                                             in1=vT[:, b1.par, :, :], op0=ALU.mult, op1=ALU.add)\
                       .then_inc(y_ready, 1)
                if b2:
                    for j in range(2):
                        wait(dve, tanh_ready, b2, 2, j + 1)
                        wait(dve, pr_done, b2, 1, -1)
                        dve.scalar_tensor_tensor(
                            out=sT[:, b2.par, 4 * j:4 * j + 4, :].rearrange("p c t -> p (c t)"),
                            in0=t_fc[:, j, :], scalar=1.0, in1=f_ps[j][:, :],
                            op0=ALU.add, op1=ALU.mult).then_inc(s_ready, 1)
                if b1:
                    wait(dve, out_done, b1, 1, 1)
                    wait(dve, xs_ready, b1, 1, -1)
                    wait(dve, ms_ready, b1, 1, -1)
                    dve.scalar_tensor_tensor(out=x_1[:, b1.par, :], in0=o_ps[:, 0:D], scalar=RES,
                                             in1=x_ln[:, b1.par, :], op0=ALU.mult, op1=ALU.add)\
                       .then_inc(x1_ready, 1)
                if b0:
                    wait(dve, q_copied, b0, 1, 1)
                    dve.tensor_tensor(q_sq[:, b0.par, :], q_t[:, b0.par, :], q_t[:, b0.par, :], ALU.mult)\
                       .then_inc(qsq_ready, 1)
                    wait(dve, qsq_ready, b0, 1, 1)
                    wait(dve, qr_ready, b0, 1, -1)
                    dve.tensor_reduce(q_ms[:, b0.par, :], q_sq[:, b0.par, :].rearrange("p (h d) -> p h d", h=HEADS),
                                      AX.X, ALU.add).then_inc(qms_ready, 1)
                if b1:
                    wait(dve, xr_ready, b1, 1, 1)
                    wait(dve, h2t_done, b1, 1, -1)
                    dve.tensor_scalar(h2_n[:, b1.par, :], x_1[:, b1.par, :], x_r[:, b1.par:b1.par + 1],
                                      None, ALU.mult).then_inc(h2_ready, 1)
            pipeline(dve, count, 4, step)

        @block.gpsimd
        def _(pool):
            for i, value in enumerate((-0.5, RMS_EPS, 1.0 / HD, Q_EPS)):
                pool.memset(consts[:, i:i + 1], value).then_inc(half_ready, 1)
            pool.wait_ge(half_ready, 4)

            def step(at):
                b0, b1, b2 = at(0), at(1), at(2)
                if b0:
                    wait(pool, kv_ready, b0, 1, 1)
                    wait(pool, scan_step, b0, 9, 4 - 18)
                    pool.tensor_tensor(uT[:, b0.par, :, :], kT[:, b0.par, :, :], vT[:, b0.par, :, :],
                                       ALU.mult).then_inc(u_ready, 1)
                if b1:
                    wait(pool, ms_ready, b1, 1, 1)
                    wait(pool, h2_ready, b1, 1, -1)
                    pool.tensor_tensor(x_r[:, b1.par:b1.par + 1], x_ms[:, b1.par:b1.par + 1], consts[:, 1:2],
                                       ALU.add).then_inc(xr_step, 1)
                    wait(pool, xr_step, b1, 1, 1)
                    pool.tensor_tensor(x_r[:, b1.par:b1.par + 1], x_r[:, b1.par:b1.par + 1], consts[:, 0:1],
                                       ALU.pow).then_inc(xr_ready, 1)
                    wait(pool, x1_ready, b1, 1, 1)
                    loaded(pool, again_loaded, b1)
                    wait(pool, xo_ready, b1, 1, -1)
                    pool.tensor_tensor(x_s[:, b1.par, :], x_1[:, b1.par, :], x_again[:, b1.par, :], ALU.add)\
                        .then_inc(xs_ready, 1)
                if b0:
                    wait(pool, qms_ready, b0, 1, 1)
                    wait(pool, qn_ready, b0, 1, -1)
                    pool.tensor_tensor(q_r[:, b0.par, :], q_ms[:, b0.par, :],
                                       consts[:, 2:3].to_broadcast([P, HEADS]), ALU.mult).then_inc(qr_step, 1)
                    wait(pool, qr_step, b0, 2, 1)
                    pool.tensor_tensor(q_r[:, b0.par, :], q_r[:, b0.par, :],
                                       consts[:, 3:4].to_broadcast([P, HEADS]), ALU.add).then_inc(qr_step, 1)
                    wait(pool, qr_step, b0, 2, 2)
                    pool.tensor_tensor(q_r[:, b0.par, :], q_r[:, b0.par, :],
                                       consts[:, 0:1].to_broadcast([P, HEADS]), ALU.pow)\
                        .then_inc(qr_ready, 1)
            pipeline(pool, count, 3, step)


def cross_values(nc, x_in, x_out, ctx_in, stats, mean, rstd, ident, w_dram, count=NB):
    name = "xv"
    with ExitStack() as ctx:
        def sb(n, shape, dt=F32):
            return ctx.enter_context(nc.sbuf_tensor(f"{name}_{n}", shape, dt))

        def ps(n):
            return ctx.enter_context(nc.psum_tensor(f"{name}_ps_{n}", [P, 512], F32))

        sem = Semaphores(nc, ctx, name)

        w_vk, w_lk, w_vv, w_lv = (sb(n, [P, DC, D]) for n in ("w_vk", "w_lk", "w_vv", "w_lv"))
        b_vk, b_lk = sb("b_vk", [P, DC]), sb("b_lk", [P, DC])
        b_vv, b_lv = sb("b_vv", [P, D]), sb("b_lv", [P, D])
        x_t, c_t, x_r, xn, vv, lv, x_o = (sb(n, [P, 2, D]) for n in ("x_t", "c_t", "x_r", "xn", "vv", "lv", "x_o"))
        srcT = sb("srcT", [P, 2, 2 * DC, P])
        vkT, lkT = sb("vkT", [P, 2, DC, P]), sb("lkT", [P, 2, DC, P])
        attn, attnT = sb("attn", [P, 2, P]), sb("attnT", [P, 2, P])
        neg_max, total, inv = sb("neg_max", [P, 2]), sb("total", [P, 2]), sb("inv", [P, 2])
        t_ps, vk_ps, lk_ps, vv_ps, s_ps, at_ps, l_ps, o_ps = (ps(n) for n in ("t", "vk", "lk", "vv", "s", "at", "l", "o"))
        loaded_w = sem("loaded_w")
        x_loaded, c_loaded, r_loaded = ([sem(f"{n}{i}") for i in range(2)] for n in ("x_loaded", "c_loaded", "r_loaded"))
        stored = [sem.kept("stored0"), sem.kept("stored1")]
        xn_ready, t_done, srcT_ready, vk_done, vk_ready, lk_done, lk_ready, vv_done, vv_ready = (
            sem(n) for n in ("xn_ready", "t_done", "srcT_ready", "vk_done", "vk_ready", "lk_done", "lk_ready",
                             "vv_done", "vv_ready"))
        s_done, max_ready, exp_ready, inv_ready, attn_ready, at_done, attnT_ready = (
            sem(n) for n in ("s_done", "max_ready", "exp_ready", "inv_ready", "attn_ready", "at_done", "attnT_ready"))
        l_done, lv_ready, out_done, xo_ready = (sem(n) for n in ("l_done", "lv_ready", "out_done", "xo_ready"))
        ctx.callback(sem.clear)
        block = ctx.enter_context(nc.Block())

        def loaded(eng, sems, b):
            eng.wait_ge(sems[b.par], (b.n + (2 - b.par)) * 8)

        @block.sync
        def _(sp):
            for dst, key in ((w_vk, "w_vk"), (w_lk, "w_lk"), (w_vv, "w_vv"), (w_lv, "w_lv")):
                sp.dma_start(dst[:, :, :], w_dram[key]).then_inc(loaded_w, 16)
            for dst, key in ((b_vk, "b_vk"), (b_lk, "b_lk"), (b_vv, "b_vv"), (b_lv, "b_lv")):
                sp.dma_start(dst[:, :], w_dram[key]).then_inc(loaded_w, 16)

            def step(at):
                b = at(0)
                if b:
                    wait(sp, xn_ready, b, 1, -1)
                    sp.dma_start(x_t[:, b.par, :], x_in[b.n]).then_inc(x_loaded[b.par], 16)
                    wait(sp, t_done, b, 1, -1)
                    sp.dma_start(c_t[:, b.par, :], ctx_in[b.n]).then_inc(c_loaded[b.par], 16)
                    wait(sp, xo_ready, b, 1, -1)
                    sp.dma_start(x_r[:, b.par, :], x_in[b.n]).then_inc(r_loaded[b.par], 16)
            pipeline(sp, count, 1, step)
            for par in range(2):
                sp.wait_ge(stored[par], 16 * (count // 2))

        @block.tensor
        def _(pe):
            pe.wait_ge(loaded_w, 16 * 8)

            def channels(b, bank, w, chunk0, done):
                for m in range(DC):
                    for c in range(DC):
                        last = pe.matmul(bank[:, P * m:P * m + P], w[:, c, P * m:P * m + P],
                                         srcT[:, b.par, chunk0 + c, :], start=(c == 0), stop=(c == DC - 1))
                last.then_inc(done, 1)

            def step(at):
                b0, b1, b2 = at(0), at(1), at(2)
                if b2:
                    wait(pe, lv_ready, b2, 1, 1)
                    wait(pe, attnT_ready, b2, 1, 1)
                    wait(pe, xo_ready, b2, 1, 0)
                    pe.matmul(o_ps[:, 0:D], attnT[:, b2.par, :], lv[:, b2.par, :], start=True, stop=True)\
                      .then_inc(out_done, 1)
                if b1:
                    wait(pe, vk_ready, b1, 1, 1)
                    wait(pe, lk_ready, b1, 1, 1)
                    wait(pe, exp_ready, b1, 1, 0)
                    for c in range(DC):
                        last = pe.matmul(s_ps[:, 0:P], vkT[:, b1.par, c, :], lkT[:, b1.par, c, :],
                                         start=(c == 0), stop=(c == DC - 1))
                    last.then_inc(s_done, 1)
                if b0:
                    wait(pe, xn_ready, b0, 1, 1)
                    loaded(pe, c_loaded, b0)
                    wait(pe, srcT_ready, b0, 1, 0)
                    for k in range(2 * DC):
                        src = xn if k < DC else c_t
                        last = pe.transpose(t_ps[:, P * k:P * k + P],
                                            src[:, b0.par, P * (k % DC):P * (k % DC) + P], ident[:, :])
                    last.then_inc(t_done, 1)
                if b1:
                    wait(pe, lv_ready, b1, 1, 0)
                    for c in range(DC):
                        pe.matmul(l_ps[:, 0:D], srcT[:, b1.par, DC + c, :], w_lv[:, c, :], start=(c == 0), stop=False)
                if b0:
                    wait(pe, srcT_ready, b0, 1, 1)
                    wait(pe, vk_ready, b0, 1, 0)
                    channels(b0, vk_ps, w_vk, 0, vk_done)
                if b1:
                    wait(pe, attn_ready, b1, 1, 1)
                    wait(pe, attnT_ready, b1, 1, 0)
                    pe.transpose(at_ps[:, 0:P], attn[:, b1.par, :], ident[:, :]).then_inc(at_done, 1)
                    wait(pe, vv_ready, b1, 1, 1)
                    pe.matmul(l_ps[:, 0:D], attn[:, b1.par, :], vv[:, b1.par, :], start=False, stop=True)\
                      .then_inc(l_done, 1)
                if b0:
                    wait(pe, lk_ready, b0, 1, 0)
                    channels(b0, lk_ps, w_lk, DC, lk_done)
                    wait(pe, vv_ready, b0, 1, 0)
                    for c in range(DC):
                        last = pe.matmul(vv_ps[:, 0:D], srcT[:, b0.par, c, :], w_vv[:, c, :],
                                         start=(c == 0), stop=(c == DC - 1))
                    last.then_inc(vv_done, 1)
            pipeline(pe, count, 3, step)

        @block.scalar
        def _(act):
            def step(at):
                b0, b1 = at(0), at(1)
                if b1:
                    wait(act, max_ready, b1, 1, 1)
                    wait(act, at_done, b1, 1, -1)
                    wait(act, l_done, b1, 1, -1)
                    act.activation(attn[:, b1.par, :], s_ps[:, 0:P], ACT.Exp, bias=neg_max[:, b1.par:b1.par + 1],
                                   scale=D ** -0.5, accum_out=total[:, b1.par:b1.par + 1]).then_inc(exp_ready, 1)
                if b0:
                    wait(act, t_done, b0, 1, 1)
                    wait(act, vv_done, b0, 1, -1)
                    wait(act, l_done, b0, 1, -1)
                    act.copy(srcT[:, b0.par, :, :], t_ps[:, :].rearrange("p (c t) -> p c t", c=2 * DC))\
                       .then_inc(srcT_ready, 1)
                if b1:
                    wait(act, at_done, b1, 1, 1)
                    wait(act, out_done, b1, 1, -1)
                    act.copy(attnT[:, b1.par, :], at_ps[:, 0:P]).then_inc(attnT_ready, 1)
            pipeline(act, count, 2, step)

        @block.vector
        def _(dve):
            dve.wait_ge(loaded_w, 16 * 8)

            def step(at):
                b0, b1, b2 = at(0), at(1), at(2)
                if b0:
                    loaded(dve, x_loaded, b0)
                    wait(dve, t_done, b0, 1, -1)
                    dve.tensor_scalar(xn[:, b0.par, :], x_t[:, b0.par, :], mean[:, bass.ds(b0.n, 1)],
                                      rstd[:, bass.ds(b0.n, 1)], ALU.subtract, ALU.mult).then_inc(xn_ready, 1)
                if b1:
                    wait(dve, s_done, b1, 1, 1)
                    wait(dve, exp_ready, b1, 1, -1)
                    dve.tensor_reduce(neg_max[:, b1.par:b1.par + 1], s_ps[:, 0:P], AX.X, ALU.max, negate=True)\
                       .then_inc(inv_ready, 1)
                    wait(dve, inv_ready, b1, 2, 1)
                    dve.tensor_scalar(neg_max[:, b1.par:b1.par + 1], neg_max[:, b1.par:b1.par + 1], D ** -0.5, None,
                                      ALU.mult).then_inc(max_ready, 1)
                if b2:
                    wait(dve, out_done, b2, 1, 1)
                    loaded(dve, r_loaded, b2)
                    if not b2.known() or b2.n >= 2:
                        dve.wait_ge(stored[b2.par], (b2.n - b2.par) * 8)
                    dve.tensor_tensor(x_o[:, b2.par, :], o_ps[:, 0:D], x_r[:, b2.par, :], ALU.add)\
                       .then_inc(xo_ready, 1)
                    wait(dve, xo_ready, b2, 1, 1)
                    dve.bn_stats(stats[:, b2.n, :], x_o[:, b2.par, :])
                if b1:
                    wait(dve, exp_ready, b1, 1, 1)
                    dve.reciprocal(inv[:, b1.par:b1.par + 1], total[:, b1.par:b1.par + 1]).then_inc(inv_ready, 1)
                    wait(dve, inv_ready, b1, 2, 2)
                    dve.tensor_scalar(attn[:, b1.par, :], attn[:, b1.par, :], inv[:, b1.par:b1.par + 1], None,
                                      ALU.mult).then_inc(attn_ready, 1)
                if b0:
                    wait(dve, vk_done, b0, 1, 1)
                    wait(dve, s_done, b0, 1, -1)
                    dve.tensor_tensor(vkT[:, b0.par, :, :], vk_ps[:, 0:D].rearrange("p (c t) -> p c t", c=DC),
                                      b_vk[:, :].unsqueeze(2).to_broadcast([P, DC, P]), ALU.add)\
                       .then_inc(vk_ready, 1)
                if b1:
                    wait(dve, l_done, b1, 1, 1)
                    wait(dve, out_done, b1, 1, -1)
                    dve.tensor_tensor(lv[:, b1.par, :], l_ps[:, 0:D], b_lv[:, :], ALU.add).then_inc(lv_ready, 1)
                if b0:
                    wait(dve, lk_done, b0, 1, 1)
                    dve.tensor_tensor(lkT[:, b0.par, :, :], lk_ps[:, 0:D].rearrange("p (c t) -> p c t", c=DC),
                                      b_lk[:, :].unsqueeze(2).to_broadcast([P, DC, P]), ALU.add)\
                       .then_inc(lk_ready, 1)
                    wait(dve, vv_done, b0, 1, 1)
                    wait(dve, l_done, b0, 1, -1)
                    dve.tensor_tensor(vv[:, b0.par, :], vv_ps[:, 0:D], b_vv[:, :], ALU.add).then_inc(vv_ready, 1)
            pipeline(dve, count, 3, step)

        @block.gpsimd
        def _(pool):
            def step(at):
                b2 = at(2)
                if b2:
                    wait(pool, xo_ready, b2, 1, 1)
                    pool.dma_start(x_out[b2.n], x_o[:, b2.par, :]).then_inc(stored[b2.par], 16)
            pipeline(pool, count, 3, step)


MAGIC = 12582912.0
TAPS = 3


def quantised_ffn(nc, x_in, x_out, mean, rstd, ident, ident_b, w_dram, count=NB):
    name = "qf"
    with ExitStack() as ctx:
        def sb(n, shape, dt=F32):
            return ctx.enter_context(nc.sbuf_tensor(f"{name}_{n}", shape, dt))

        def ps(n, shape, dt=F32):
            return ctx.enter_context(nc.psum_tensor(f"{name}_ps_{n}", shape, dt))

        sem = Semaphores(nc, ctx, name)

        w1, w2 = sb("w1", [P, DC * HID]), sb("w2", [P, HC * D])
        w1_q, w2_q = sb("w1_q", [P, DC, HID], BF16), sb("w2_q", [P, HC, D], BF16)
        conv_w = sb("conv_w", [P, TAPS, HC])
        diag = sb("diag", [P, TAPS, HC, P])
        bias = sb("bias", [1, HID])
        bias_p = sb("bias_p", [1, 3, HID], BF16)
        bias3 = sb("bias3", [3, HID], BF16)
        ones3 = sb("ones3", [3, P], BF16)
        ones = sb("ones", [P, P])
        w_sum, w_mean, w_inv, factor = sb("w_sum", [P, 2]), sb("w_mean", [P, 2]), sb("w_inv", [P, 2]), sb("factor", [P, 2])
        x_t, x_r, xn, rounded, x_o = (sb(n, [P, 2, D]) for n in ("x_t", "x_r", "xn", "rounded", "x_o"))
        q1 = sb("q1", [P, 2, D])
        q1T = sb("q1T", [P, 2, DC, P], BF16)
        peak1, step1, inv1, fac1 = (sb(n, [P, 2]) for n in ("peak1", "step1", "inv1", "fac1"))
        peak2, step2, inv2, fac2 = (sb(n, [P, 2]) for n in ("peak2", "step2", "inv2", "fac2"))
        fac_row = sb("fac_row", [P, 2, P])
        h_pad = sb("h_pad", [P, 2, HC, P + 2])
        t_h = sb("t_h", [P, 2, 512])
        sT = sb("sT", [P, HC, P])
        rounded2 = sb("rounded2", [P, HID])
        q2 = sb("q2", [P, 2, HID], BF16)
        q2T = sb("q2T", [P, HC, P], BF16)
        h_ps, z_ps, st_ps = ps("h", [P, 2, 512]), ps("z", [P, 2, 512]), ps("st", [P, 2, 512])
        q2_ps = ps("q2", [P, HC, P], BF16)
        m_ps = ps("m", [P, 512])
        f_ps, q1_ps, o_ps = m_ps[:, 0:P], m_ps[:, P:P + D], m_ps[:, 0:D]

        loaded_w, w_step, sums_ready, sum_done, weights_ready, bias_ready, bias_stacked, pads_ready = (
            sem(n) for n in ("loaded_w", "w_step", "sums_ready", "sum_done", "weights_ready", "bias_ready",
                             "bias_stacked", "pads_ready"))
        x_loaded, r_loaded = ([sem(f"{n}{i}") for i in range(2)] for n in ("x_loaded", "r_loaded"))
        stored = [sem.kept("stored0"), sem.kept("stored1")]
        small, xn_ready, round1_ready, q1_ready, q1t_done, q1T_ready, fac1_ready, f_ready = (
            sem(n) for n in ("small", "xn_ready", "round1_ready", "q1_ready", "q1t_done", "q1T_ready", "fac1_ready",
                             "f_ready"))
        h_done, h_ready, z_done, tanh_ready, s_ready, st_done, small2, round2_ready, q2_ready = (
            sem(n) for n in ("h_done", "h_ready", "z_done", "tanh_ready", "s_ready", "st_done", "small2",
                             "round2_ready", "q2_ready"))
        scaled1, scaled2 = sem("scaled1"), sem("scaled2")
        q2t_done, q2T_ready, o_done, xo_ready = (sem(n) for n in ("q2t_done", "q2T_ready", "o_done", "xo_ready"))
        block = ctx.enter_context(nc.Block())

        def loaded(eng, sems, b):
            eng.wait_ge(sems[b.par], (b.n + (2 - b.par)) * 8)

        @block.sync
        def _(sp):
            sp.dma_start(w1[:, :], w_dram["w1"]).then_inc(loaded_w, 16)
            sp.dma_start(w2[:, :], w_dram["w2"]).then_inc(loaded_w, 16)
            sp.dma_start(conv_w[:, :, :], w_dram["conv_w"]).then_inc(loaded_w, 16)
            sp.dma_start(bias[:, :], w_dram["conv_b"]).then_inc(loaded_w, 16)
            sp.wait_ge(bias_ready, 1)
            for part in range(3):
                sp.dma_start(bias3[part:part + 1, :], bias_p[:, part, :]).then_inc(bias_stacked, 16)

            def step(at):
                b0, b2, b3 = at(0), at(2), at(3)
                if b0:
                    wait(sp, xn_ready, b0, 1, -1)
                    sp.dma_start(x_t[:, b0.par, :], x_in[b0.n]).then_inc(x_loaded[b0.par], 16)
                if b2:
                    wait(sp, xo_ready, b2, 1, -1)
                    sp.dma_start(x_r[:, b2.par, :], x_in[b2.n]).then_inc(r_loaded[b2.par], 16)
                if b3:
                    wait(sp, xo_ready, b3, 1, 1)
                    sp.dma_start(x_out[b3.n], x_o[:, b3.par, :]).then_inc(stored[b3.par], 16)
            pipeline(sp, count, 4, step)
            for par in range(2):
                sp.wait_ge(stored[par], 16 * (count // 2))

        @block.tensor
        def _(pe):
            pe.wait_ge(sums_ready, 1)
            pe.matmul(m_ps[:, 0:2], ones[:, :], w_sum[:, :], start=True, stop=True).then_inc(sum_done, 1)
            pe.wait_ge(weights_ready, 1)
            pe.wait_ge(bias_stacked, 48)

            def convolve(b, j):
                wait(pe, h_ready, b, 2, j + 1)
                wait(pe, s_ready, b, 2, j - 1)
                for c in range(4 * j, 4 * j + 4):
                    out = z_ps[:, j, P * (c % 4):P * (c % 4) + P]
                    for tap in range(TAPS):
                        pe.matmul(out, diag[:, tap, c, :], h_pad[:, b.par, c, tap:tap + P],
                                  start=(tap == 0), stop=False)
                    last = pe.matmul(out, bias3[:, P * c:P * c + P], ones3[:, :], start=False, stop=True)
                last.then_inc(z_done, 1)

            def silu_transpose(b, j):
                wait(pe, s_ready, b, 2, j + 1)
                if j == 0:
                    wait(pe, round2_ready, b, 1, 0)
                for c in range(4 * j, 4 * j + 4):
                    last = pe.transpose(st_ps[:, j, P * (c % 4):P * (c % 4) + P], sT[:, c, :], ident[:, :])
                if j == 1:
                    last.then_inc(st_done, 1)

            def step(at):
                b0, b1, b2 = at(0), at(1), at(2)
                if b1:
                    convolve(b1, 0)
                    convolve(b1, 1)
                if b2:
                    wait(pe, q2_ready, b2, 1, 1)
                    wait(pe, q2T_ready, b2, 1, 0)
                    for c in range(HC):
                        last = pe.transpose(q2_ps[:, c, :], q2[:, b2.par, P * c:P * c + P], ident_b[:, :])
                    last.then_inc(q2t_done, 1)
                if b1:
                    silu_transpose(b1, 0)
                if b0:
                    wait(pe, q1_ready, b0, 1, 1)
                    wait(pe, fac1_ready, b0, 1, 1)
                    wait(pe, xo_ready, b0, 1, -2)
                    for c in range(DC):
                        pe.transpose(q1_ps[:, P * c:P * c + P], q1[:, b0.par, P * c:P * c + P], ident[:, :])
                    pe.transpose(f_ps, fac1[:, b0.par:b0.par + 1].to_broadcast([P, P]), ident[:, :])\
                      .then_inc(q1t_done, 1)
                if b1:
                    silu_transpose(b1, 1)
                if b0:
                    wait(pe, q1T_ready, b0, 1, 1)
                    for j in range(2):
                        wait(pe, h_ready, b0, 2, j - 1)
                        for m in range(4 * j, 4 * j + 4):
                            for c in range(DC):
                                last = pe.matmul(h_ps[:, j, P * (m % 4):P * (m % 4) + P], w1_q[:, c, P * m:P * m + P],
                                                 q1T[:, b0.par, c, :], start=(c == 0), stop=(c == DC - 1))
                        last.then_inc(h_done, 1)
                if b2:
                    wait(pe, q2T_ready, b2, 1, 1)
                    wait(pe, xo_ready, b2, 1, 0)
                    if b0:
                        wait(pe, f_ready, b0, 1, 1)
                    for c in range(HC):
                        last = pe.matmul(o_ps, q2T[:, c, :], w2_q[:, c, :], start=(c == 0), stop=(c == HC - 1))
                    last.then_inc(o_done, 1)
            pipeline(pe, count, 3, step)

        @block.scalar
        def _(act):
            def silu_tanh(b, j):
                wait(act, z_done, b, 2, j + 1)
                wait(act, s_ready, b, 2, j - 1)
                act.activation(t_h[:, j, :], z_ps[:, j, :], ACT.Tanh, scale=0.5).then_inc(tanh_ready, 1)

            def step(at):
                b0, b1, b2 = at(0), at(1), at(2)
                if b1:
                    silu_tanh(b1, 0)
                if b2:
                    wait(act, round2_ready, b2, 1, 1)
                    wait(act, q2t_done, b2, 1, -1)
                    act.activation(q2[:, b2.par, :], rounded2[:, :], ACT.Copy, bias=-MAGIC, scale=1.0)\
                       .then_inc(q2_ready, 1)
                if b1:
                    silu_tanh(b1, 1)
                if b0:
                    wait(act, round1_ready, b0, 1, 1)
                    wait(act, q1t_done, b0, 1, -1)
                    act.activation(q1[:, b0.par, :], rounded[:, b0.par, :], ACT.Copy, bias=-MAGIC, scale=1.0)\
                       .then_inc(q1_ready, 1)
                    wait(act, q1t_done, b0, 1, 1)
                    wait(act, h_done, b0, 2, -2)
                    act.copy(q1T[:, b0.par, :, :], q1_ps.rearrange("p (c t) -> p c t", c=DC)).then_inc(q1T_ready, 1)
                    wait(act, h_ready, b0, 2, -2)
                    act.copy(fac_row[:, b0.par, :], f_ps).then_inc(f_ready, 1)
                if b2:
                    wait(act, q2t_done, b2, 1, 1)
                    wait(act, o_done, b2, 1, 0)
                    act.copy(q2T[:, :, :], q2_ps[:, :, :]).then_inc(q2T_ready, 1)
            pipeline(act, count, 3, step)

        @block.vector
        def _(dve):
            done = [0]

            def link(instruction):
                done[0] += 1
                instruction.then_inc(w_step, 1)
                dve.wait_ge(w_step, done[0])

            link(dve.memset(ones[:, :], 1.0))
            link(dve.memset(ones3[:, :], 1.0))
            link(dve.memset(h_pad[:, :, :, :], 0.0))
            dve.wait_ge(loaded_w, 16 * 4)
            for part in range(3):
                link(dve.tensor_copy(bias_p[:, part, :], bias[:, :]))
                if part < 2:
                    link(dve.tensor_tensor(bias[:, :], bias[:, :], bias_p[:, part, :], ALU.subtract))
            dve.sem_inc(bias_ready, 1)
            link(dve.tensor_tensor(diag[:, :, :, :].rearrange("p a c t -> p (a c) t"),
                                   ident[:, :].unsqueeze(1).to_broadcast([P, TAPS * HC, P]),
                                   conv_w[:, :, :].rearrange("p a c -> p (a c)").unsqueeze(2).to_broadcast([P, TAPS * HC, P]),
                                   ALU.mult))
            link(dve.tensor_reduce(w_sum[:, 0:1], w1[:, :], AX.X, ALU.add, apply_absolute_value=True))
            link(dve.tensor_reduce(w_sum[:, 1:2], w2[:, :], AX.X, ALU.add, apply_absolute_value=True))
            dve.sem_inc(sums_ready, 1)
            dve.wait_ge(sum_done, 1)
            link(dve.tensor_scalar(w_mean[:, :], m_ps[:, 0:2], 1.0 / (D * HID), 1e-5, ALU.mult, ALU.max))
            link(dve.reciprocal(w_inv[:, :], w_mean[:, :]))
            for i, (w, w_q) in enumerate(((w1, w1_q), (w2, w2_q))):
                link(dve.tensor_scalar(w[:, :], w[:, :], w_inv[:, i:i + 1], None, ALU.mult))
                link(dve.tensor_scalar(w[:, :], w[:, :], MAGIC, MAGIC, ALU.add, ALU.subtract))
                link(dve.tensor_scalar(w_q[:, :, :].rearrange("p a b -> p (a b)"), w[:, :], 1.0, -1.0, ALU.min, ALU.max))
            link(dve.tensor_copy(factor[:, 0:1], w_mean[:, 0:1]))
            link(dve.tensor_scalar(factor[:, 1:2], w_mean[:, 1:2], 0.5, None, ALU.mult))
            dve.sem_inc(weights_ready, 1)

            def scales(src, par, floor, peak, stp, inv, fac, factor_col, sem_, b):
                dve.tensor_reduce(peak[:, par:par + 1], src, AX.X if len(src.shape) == 2 else AX.XY, ALU.max,
                                  apply_absolute_value=True).then_inc(sem_, 1)
                wait(dve, sem_, b, 3, 1)
                dve.tensor_scalar(stp[:, par:par + 1], peak[:, par:par + 1], floor, 1.0 / 127.0, ALU.max, ALU.mult)\
                   .then_inc(sem_, 1)
                wait(dve, sem_, b, 3, 2)
                dve.reciprocal(inv[:, par:par + 1], stp[:, par:par + 1]).then_inc(sem_, 1)
                return dve.tensor_scalar(fac[:, par:par + 1], stp[:, par:par + 1], factor[:, factor_col:factor_col + 1],
                                         None, ALU.mult)

            def silu(b, j):
                wait(dve, tanh_ready, b, 2, j + 1)
                wait(dve, st_done, b, 1, 0)
                dve.scalar_tensor_tensor(
                    out=sT[:, 4 * j:4 * j + 4, :].rearrange("p c t -> p (c t)"), in0=t_h[:, j, :],
                    scalar=1.0, in1=z_ps[:, j, :], op0=ALU.add, op1=ALU.mult).then_inc(s_ready, 1)

            def step(at):
                b0, b1, b2, b3 = at(0), at(1), at(2), at(3)
                if b1:
                    wait(dve, f_ready, b1, 1, 1)
                    wait(dve, z_done, b1, 2, -2)
                    for j in range(2):
                        wait(dve, h_done, b1, 2, j + 1)
                        dve.tensor_tensor(h_pad[:, b1.par, 4 * j:4 * j + 4, 1:P + 1],
                                          h_ps[:, j, :].rearrange("p (c t) -> p c t", c=4),
                                          fac_row[:, b1.par, :].unsqueeze(1).to_broadcast([P, 4, P]),
                                          ALU.mult).then_inc(h_ready, 1)
                if b2:
                    wait(dve, st_done, b2, 1, 1)
                    scales(st_ps[:, :, :], b2.par, 2e-5, peak2, step2, inv2, fac2, 1, small2, b2)
                    wait(dve, small2, b2, 3, 3)
                    wait(dve, q2_ready, b2, 1, 0)
                    dve.tensor_scalar(rounded2[:, :], st_ps[:, :, :].rearrange("p a b -> p (a b)"),
                                      inv2[:, b2.par:b2.par + 1], MAGIC, ALU.mult, ALU.add).then_inc(scaled2, 1)
                    wait(dve, scaled2, b2, 1, 1)
                    dve.tensor_scalar(rounded2[:, :], rounded2[:, :], MAGIC + 127.0, MAGIC - 128.0,
                                      ALU.min, ALU.max).then_inc(round2_ready, 1)
                if b3:
                    wait(dve, o_done, b3, 1, 1)
                    loaded(dve, r_loaded, b3)
                    if not b3.known() or b3.n >= 2:
                        dve.wait_ge(stored[b3.par], (b3.n - b3.par) * 8)
                    dve.scalar_tensor_tensor(out=x_o[:, b3.par, :], in0=o_ps, scalar=fac2[:, b3.par:b3.par + 1],
                                             in1=x_r[:, b3.par, :], op0=ALU.mult, op1=ALU.add).then_inc(xo_ready, 1)
                if b1:
                    silu(b1, 0)
                if b0:
                    loaded(dve, x_loaded, b0)
                    dve.tensor_scalar(xn[:, b0.par, :], x_t[:, b0.par, :], mean[:, bass.ds(b0.n, 1)],
                                      rstd[:, bass.ds(b0.n, 1)], ALU.subtract, ALU.mult).then_inc(xn_ready, 1)
                    wait(dve, xn_ready, b0, 1, 1)
                    wait(dve, q1t_done, b0, 1, -1)
                    scales(xn[:, b0.par, :], b0.par, 1e-5, peak1, step1, inv1, fac1, 0, small, b0)\
                        .then_inc(fac1_ready, 1)
                    wait(dve, small, b0, 3, 3)
                    dve.tensor_scalar(xn[:, b0.par, :], xn[:, b0.par, :], inv1[:, b0.par:b0.par + 1], MAGIC,
                                      ALU.mult, ALU.add).then_inc(scaled1, 1)
                    wait(dve, scaled1, b0, 1, 1)
                    wait(dve, q1_ready, b0, 1, -1)
                    dve.tensor_scalar(rounded[:, b0.par, :], xn[:, b0.par, :], MAGIC + 127.0, MAGIC - 128.0,
                                      ALU.min, ALU.max).then_inc(round1_ready, 1)
                if b1:
                    silu(b1, 1)
            pipeline(dve, count, 4, step)


def decoder(nc, ins, scratch, x_out):
    with ExitStack() as ctx:
        def sb(n, shape, dt=F32):
            return ctx.enter_context(nc.sbuf_tensor(n, shape, dt))

        ident, ident_b = sb("ident", [P, P]), sb("ident_b", [P, P], BF16)
        mean, rstd, rms_scale = sb("mean", [P, NB]), sb("rstd", [P, NB]), sb("rms_scale", [P, NB])
        stats = sb("stats", [P, NB, 6])
        consts_loaded = ctx.enter_context(nc.semaphore("consts_loaded"))
        with nc.Block() as block:
            @block.sync
            def _(sp):
                sp.dma_start(ident[:, :], ins["ident"]).then_inc(consts_loaded, 16)
                sp.dma_start(ident_b[:, :], ins["ident_b"]).then_inc(consts_loaded, 16)
                sp.wait_ge(consts_loaded, 32)

        def part(prefix):
            return {n[len(prefix):]: ap for n, ap in {**ins, **scratch}.items() if n.startswith(prefix)}

        x = [ins["x"]] + [scratch[f"x{i}"] for i in range(1, 6)] + [x_out]

        latent_weights(nc, part("latent_"), part("self_"))
        alibi_rows(nc, ins["q_pos"], ins["k_pos"], ins["slope_rows"], scratch["alibi_q"], scratch["alibi_k"])
        first_statistics(nc, x[0], stats)
        norm_scales(nc, "norm0", stats, mean, rstd)
        attention(nc, "self", False, x[0], x[1], None, None, None, stats, mean, rstd, ident, ident_b, part("self_"), None)
        norm_scales(nc, "norm1", stats, mean, rstd)
        attention(nc, "cross", True, x[1], x[2], ins["ctx"], ins["mask"],
                  dict(q=scratch["alibi_q"], k=scratch["alibi_k"], slopes=ins["slope_parts"]),
                  stats, mean, rstd, ident, ident_b, part("cross_"), None)
        norm_scales(nc, "norm2", stats, mean, rstd)
        experts_ffn(nc, x[2], x[3], stats, mean, rstd, ident, part("moe_"), scratch["sorted_x"], scratch["sorted_y"])
        norm_scales(nc, "norm3", stats, mean, rstd, rms_scale=rms_scale)
        mixer(nc, x[3], x[4], stats, mean, rstd, rms_scale, ident, part("mix_"))
        norm_scales(nc, "norm4", stats, mean, rstd)
        cross_values(nc, x[4], x[5], ins["ctx"], stats, mean, rstd, ident, part("vis_"))
        norm_scales(nc, "norm5", stats, mean, rstd)
        quantised_ffn(nc, x[5], x[6], mean, rstd, ident, ident_b, part("q_"))


def by_chunks(w):
    return w.reshape(w.shape[0] // P, P, w.shape[1]).transpose(1, 0, 2)


def column(v):
    return v.reshape(-1, P).T


def rows(v):
    return np.broadcast_to(v.reshape(-1), (P, v.size))


def kernel(**inputs):
    import concourse.bacc as bacc
    import ml_dtypes
    from concourse.bass_utils import run_bass_kernel_spmd

    inp = {name: np.asarray(a) for name, a in inputs.items()}
    bf16 = ml_dtypes.bfloat16

    slope = np.asarray([(2.0 ** (-8.0 / HEADS)) ** i for i in range(1, HEADS + 1)], np.float32)
    slope_parts, rest = [], slope
    for _ in range(3):
        slope_parts.append(rest.astype(bf16))
        rest = rest - slope_parts[-1].astype(np.float32)
    negated = np.stack([np.repeat(-part, P) for part in slope_parts])
    head_mask = (np.arange(P)[:, None] // HD == np.arange(P // HD)[None, :]).astype(np.float32)
    tiles = expert_tiles(NB)
    zeros = np.zeros(D, np.float32)

    lay = {
        "x": inp["x"], "ctx": inp["ctx_1024"], "mask": inp["mask_BxSxS2_if1"],
        "q_pos": inp["itok_BxS_8_8191"], "k_pos": inp["itok_BxS2_1_8191"],
        "ident": np.eye(P, dtype=np.float32), "ident_b": np.eye(P, dtype=np.float32).astype(bf16),
        "slope_rows": np.broadcast_to(slope, (NB, HEADS)), "slope_parts": np.tile(negated, (3, 1)),

        "latent_down": inp["L0_attn_Wl"].T,
        "latent_up": np.concatenate([inp["L0_attn_Wk"], inp["L0_attn_Wv"]], 1),
        "latent_bl": inp["L0_attn_bl"].reshape(LATENT, 1),
        "latent_bk": column(inp["L0_attn_bk"]), "latent_bv": rows(inp["L0_attn_bv"]),
        "self_wq": by_chunks(inp["L0_attn_Wq"]), "self_wo": by_chunks(inp["L0_attn_Wo"]),
        "self_bq": column(inp["L0_attn_bq"]), "self_bo": rows(inp["L0_attn_bo"]), "self_head_mask": head_mask,

        "cross_wq": by_chunks(inp["L0_xattn_W_q"].T), "cross_wk": by_chunks(inp["L0_xattn_W_k"].T),
        "cross_wv": by_chunks(inp["L0_xattn_W_v"].T), "cross_wo": by_chunks(inp["L0_xattn_W_o"].T),
        "cross_bq": column(zeros), "cross_bk": column(zeros), "cross_bv": rows(zeros), "cross_bo": rows(zeros),
        "cross_head_mask": head_mask,

        "moe_wr": by_chunks(inp["L0_ffn_Wr"]), "moe_br": rows(inp["L0_ffn_br"]),
        "moe_w1": inp["L0_ffn_W1"].reshape(EXPERTS, DC, P, HID).transpose(2, 0, 1, 3),
        "moe_w2": inp["L0_ffn_W2"].reshape(EXPERTS, HC, P, D).transpose(2, 0, 1, 3),
        "moe_b1": inp["L0_ffn_b1"].reshape(EXPERTS * HC, P).T, "moe_b2": rows(inp["L0_ffn_b2"]),
        "moe_falling": rows(np.arange(EXPERTS, 0, -1).astype(np.float32)),
        "moe_before": np.triu(np.ones((P, P), np.float32), 1), "moe_ones": np.ones((P, P), np.float32),
        "moe_tile_no": np.arange(tiles, dtype=np.float32)[None],

        "mix_w_in": by_chunks(inp["L1_attn_in_proj_w"].T), "mix_w_out": by_chunks(inp["L1_attn_out_proj_w"].T),
        "mix_w_fc": by_chunks(inp["L1_attn_fc_w"].T), "mix_w_pr": by_chunks(inp["L1_attn_proj_w"].T),
        "mix_norm1": column(inp["L1_attn_norm1_w"]), "mix_norm2": column(inp["L1_attn_norm2_w"]),

        "vis_w_vk": by_chunks(inp["L1_xattn_W_vk"].T), "vis_w_lk": by_chunks(inp["L1_xattn_W_lk"].T),
        "vis_w_vv": by_chunks(inp["L1_xattn_W_vv"].T), "vis_w_lv": by_chunks(inp["L1_xattn_W_lv"].T),
        "vis_b_vk": column(inp["L1_xattn_b_vk"]), "vis_b_lk": column(inp["L1_xattn_b_lk"]),
        "vis_b_vv": rows(inp["L1_xattn_b_vv"]), "vis_b_lv": rows(inp["L1_xattn_b_lv"]),

        "q_w1": by_chunks(inp["L1_ffn_w1"].T).reshape(P, -1), "q_w2": by_chunks(inp["L1_ffn_w2"].T).reshape(P, -1),
        "q_conv_w": inp["L1_ffn_conv_w"].reshape(HC, P, 3).transpose(1, 2, 0),
        "q_conv_b": inp["L1_ffn_conv_b"].reshape(1, HID),
    }

    nc = bacc.Bacc("TRN2", target_bir_lowering=False, num_devices=1)
    arrays, ins = {}, {}
    for name, a in lay.items():
        arrays[f"in_{name}"] = np.ascontiguousarray(a)
        ins[name] = nc.dram_tensor(f"in_{name}", list(a.shape), mybir.dt.from_np(a.dtype), kind="ExternalInput").ap()

    def internal(name, shape, dt=F32):
        return nc.dram_tensor(f"dram_{name}", shape, dt, kind="Internal").ap()

    scratch = {f"x{i}": internal(f"x{i}", [NB, P, D]) for i in range(1, 6)}
    scratch["self_wk"], scratch["self_wv"] = internal("self_wk", [P, DC, D]), internal("self_wv", [P, DC, D])
    scratch["self_bk"], scratch["self_bv"] = internal("self_bk", [P, DC]), internal("self_bv", [P, D])
    scratch["alibi_q"], scratch["alibi_k"] = internal("alibi_q", [12, NB, P], BF16), internal("alibi_k", [NB, 3, HEADS * P], BF16)
    scratch["sorted_x"], scratch["sorted_y"] = internal("sorted_x", [tiles * P, D]), internal("sorted_y", [tiles * P, D])
    x_out = nc.dram_tensor("x_out", [NB, P, D], F32, kind="ExternalOutput").ap()
    decoder(nc, ins, scratch, x_out)
    return run_bass_kernel_spmd(nc, [arrays], core_ids=[0]).results[0]["x_out"]
```

```python
from contextlib import ExitStack

import numpy as np

import concourse.bass as bass
from concourse import mybir

F32, BF16, I32, U32 = mybir.dt.float32, mybir.dt.bfloat16, mybir.dt.int32, mybir.dt.uint32
ALU = mybir.AluOpType
ACT = mybir.ActivationFunctionType
AX = mybir.AxisListType

P = 128
NB = 32
D = 256
DC = D // P
HEADS = 16
HD = D // HEADS
LATENT = D // 4
QUADS = HEADS // 4
LN_EPS = 1e-5


class Semaphores:

    def __init__(self, nc, ctx, name):
        self.nc, self.ctx, self.name, self.cleared = nc, ctx, name, []

    def __call__(self, n):
        s = self.ctx.enter_context(self.nc.semaphore(f"{self.name}_{n}"))
        self.cleared.append(s)
        return s

    def kept(self, n):
        return self.nc.alloc_semaphore(f"{self.name}_{n}")

    def clear(self):
        with self.nc.Block() as block:
            @block.gpsimd
            def _(pool):
                for s in self.cleared:
                    pool.sem_clear(s)


class Batch:

    def __init__(self, number, parity):
        self.n, self.par = number, parity

    def known(self):
        return isinstance(self.n, int)


def wait(eng, sem, batch, per_batch, done):
    value = batch.n * per_batch + done if per_batch != 1 else batch.n + done
    if batch.known() and value <= 0:
        return
    eng.wait_ge(sem, value)


def pipeline(eng, count, depth, step):
    lag = depth - 1
    start = (lag + 3) // 2 * 2

    def one(t, parity):
        def at(k):
            if isinstance(t, int):
                return Batch(t - k, (t - k) % 2) if 0 <= t - k < count else None
            return Batch(t - k if k else t, (parity - k) % 2)
        step(at)

    end = start + (count - start) // 2 * 2
    for t in range(start):
        one(t, t % 2)
    with eng.Fori(start, end - 1, 2) as i:
        one(i, 0)
        one(i + 1, 1)
    for t in range(end, count + lag):
        one(t, t % 2)


def chained(eng, sem):
    count = [0]

    def link(instruction):
        count[0] += 1
        instruction.then_inc(sem, 1)
        eng.wait_ge(sem, count[0])
    return link


def first_statistics(nc, x_in, stats, count=NB, name="first"):
    per = 4
    with ExitStack() as ctx:
        x_a = ctx.enter_context(nc.sbuf_tensor(f"{name}_x", [P, 2, per, D], F32))
        loaded = [nc.alloc_semaphore(f"{name}_loaded{i}") for i in range(2)]
        done = nc.alloc_semaphore(f"{name}_done")
        block = ctx.enter_context(nc.Block())

        @block.sync
        def _(sp):
            for g in range(count // per):
                if g >= 2:
                    sp.wait_ge(done, per * (g - 1))
                sp.dma_start(x_a[:, g % 2, :, :], x_in[per * g:per * g + per].rearrange("b t d -> t b d"))\
                  .then_inc(loaded[g % 2], 16)

        @block.vector
        def _(dve):
            for g in range(count // per):
                dve.wait_ge(loaded[g % 2], 16 * (g // 2 + 1))
                for i in range(per):
                    dve.bn_stats(stats[:, per * g + i, :], x_a[:, g % 2, i, :]).then_inc(done, 1)


def norm_scales(nc, name, stats, mean, rstd, rms_scale=None, rms_eps=1e-6, count=NB):
    with ExitStack() as ctx:
        def sb(n):
            return ctx.enter_context(nc.sbuf_tensor(f"{name}_{n}", [P, count], F32))
        diff, var, root, tmp = sb("diff"), sb("var"), sb("root"), sb("tmp")
        dve_step = nc.alloc_semaphore(f"{name}_dve_step")
        var_ready = nc.alloc_semaphore(f"{name}_var_ready")
        root_ready = nc.alloc_semaphore(f"{name}_root_ready")
        block = ctx.enter_context(nc.Block())
        rounds = 1 if rms_scale is None else 2

        @block.vector
        def _(dve):
            link = chained(dve, dve_step)

            def tt(out, a, b, op):
                link(dve.tensor_tensor(out, a, b, op))

            def inverse_root(out, turn):
                link(dve.tensor_copy(tmp[:, :], var[:, :]))
                dve.sem_inc(var_ready, 1)
                dve.wait_ge(root_ready, turn)
                link(dve.reciprocal(out, root[:, :]))
                tt(tmp[:, :], out, out, ALU.mult)
                tt(tmp[:, :], tmp[:, :], var[:, :], ALU.mult)
                link(dve.tensor_scalar(tmp[:, :], tmp[:, :], -0.5, 1.5, ALU.mult, ALU.add))
                tt(out, out, tmp[:, :], ALU.mult)

            tt(mean[:, :], stats[:, :, 1], stats[:, :, 4], ALU.add)
            link(dve.tensor_scalar(mean[:, :], mean[:, :], 0.5, None, ALU.mult))
            tt(diff[:, :], stats[:, :, 1], stats[:, :, 4], ALU.subtract)
            tt(diff[:, :], diff[:, :], diff[:, :], ALU.mult)
            link(dve.tensor_scalar(diff[:, :], diff[:, :], 0.25, LN_EPS, ALU.mult, ALU.add))
            tt(var[:, :], stats[:, :, 2], stats[:, :, 5], ALU.add)
            link(dve.tensor_scalar(var[:, :], var[:, :], 1.0 / D, None, ALU.mult))
            if rms_scale is not None:
                tt(rms_scale[:, :], var[:, :], diff[:, :], ALU.add)
                link(dve.tensor_scalar(rms_scale[:, :], rms_scale[:, :], -LN_EPS, None, ALU.add))
            tt(var[:, :], var[:, :], diff[:, :], ALU.add)
            inverse_root(rstd[:, :], 1)
            if rms_scale is not None:
                tt(tmp[:, :], rstd[:, :], rstd[:, :], ALU.mult)
                tt(var[:, :], rms_scale[:, :], tmp[:, :], ALU.mult)
                link(dve.tensor_scalar(var[:, :], var[:, :], rms_eps, None, ALU.add))
                inverse_root(rms_scale[:, :], 2)
                tt(rms_scale[:, :], rms_scale[:, :], rstd[:, :], ALU.mult)

        @block.scalar
        def _(act):
            for turn in range(rounds):
                act.wait_ge(var_ready, turn + 1)
                act.activation(root[:, :], var[:, :], ACT.Sqrt).then_inc(root_ready, 1)


def alibi_rows(nc, q_pos, k_pos, slope_bc, q_rows, k_rows, count=NB):
    with ExitStack() as ctx:
        def sb(n, shape, dt):
            return ctx.enter_context(nc.sbuf_tensor(f"alibi_{n}", shape, dt))
        ints = sb("ints", [count, 2, P], I32)
        pos = sb("pos", [count, 2, P], F32)
        slope = sb("slope", [count, HEADS], F32)
        prod = sb("prod", [count, HEADS, P], F32)
        parts = sb("parts", [count, 3, HEADS, P], BF16)
        q_parts = sb("q_parts", [count, 4, P], BF16)
        loaded, step, stored = (nc.alloc_semaphore(f"alibi_{n}") for n in ("loaded", "step", "stored"))
        parts_ready = nc.alloc_semaphore("alibi_parts_ready")
        block = ctx.enter_context(nc.Block())

        @block.sync
        def _(sp):
            sp.dma_start(ints[:, 0, :], q_pos).then_inc(loaded, 16)
            sp.dma_start(ints[:, 1, :], k_pos).then_inc(loaded, 16)
            sp.dma_start(slope[:, :], slope_bc).then_inc(loaded, 16)
            sp.wait_ge(parts_ready, 1)
            for row in range(12):
                a = 3 if row < 3 else (row - 3) // 3
                sp.dma_start(q_rows[row], q_parts[:, a, :]).then_inc(stored, 16)
            sp.dma_start(k_rows.rearrange("b a n -> b (a n)"),
                         parts[:, :, :, :].rearrange("b a h t -> b (a h t)")).then_inc(stored, 16)
            sp.wait_ge(stored, 16 * 13)

        @block.vector
        def _(dve):
            link = chained(dve, step)
            dve.wait_ge(loaded, 48)
            link(dve.tensor_copy(pos[:, :, :], ints[:, :, :]))
            link(dve.memset(q_parts[:, 3, :], 1.0))
            link(dve.tensor_tensor(prod[:, :, :], pos[:, 1, :].unsqueeze(1).to_broadcast([count, HEADS, P]),
                                   slope[:, :].unsqueeze(2).to_broadcast([count, HEADS, P]), ALU.mult))
            for part in range(3):
                link(dve.tensor_copy(parts[:, part, :, :], prod[:, :, :]))
                link(dve.tensor_copy(q_parts[:, part, :], pos[:, 0, :]))
                if part < 2:
                    link(dve.tensor_tensor(prod[:, :, :], prod[:, :, :], parts[:, part, :, :], ALU.subtract))
                    link(dve.tensor_tensor(pos[:, 0, :], pos[:, 0, :], q_parts[:, part, :], ALU.subtract))
            dve.sem_inc(parts_ready, 1)


def latent_weights(nc, w_in, w_out):
    with ExitStack() as ctx:
        def sb(n, shape):
            return ctx.enter_context(nc.sbuf_tensor(f"latent_{n}", shape, F32))

        def sem(n):
            return nc.alloc_semaphore(f"latent_{n}")

        down, up = sb("down", [LATENT, D]), sb("up", [LATENT, 2 * D])
        bl, bl_rows = sb("bl", [LATENT, 1]), sb("bl_rows", [LATENT, P])
        bk, bv = sb("bk", [P, DC]), sb("bv", [P, D])
        both = sb("both", [P, DC, 2 * D])
        w_ps = ctx.enter_context(nc.psum_tensor("latent_w_ps", [P, DC, 2 * D], F32))
        v_ps = ctx.enter_context(nc.psum_tensor("latent_v_ps", [P, 2 * D], F32))
        k_ps = ctx.enter_context(nc.psum_tensor("latent_k_ps", [P, 2 * D], F32))
        loaded, rows_ready, done, ready, stored = (sem(n) for n in ("loaded", "rows_ready", "done", "ready", "stored"))
        block = ctx.enter_context(nc.Block())

        @block.sync
        def _(sp):
            for dst, key in ((down, "down"), (up, "up"), (bl, "bl"), (bk, "bk"), (bv, "bv")):
                sp.dma_start(dst[:, :], w_in[key]).then_inc(loaded, 16)
            sp.wait_ge(ready, 3)
            sp.dma_start(w_out["wk"], both[:, :, 0:D]).then_inc(stored, 16)
            sp.dma_start(w_out["wv"], both[:, :, D:2 * D]).then_inc(stored, 16)
            sp.dma_start(w_out["bk"], bk[:, :]).then_inc(stored, 16)
            sp.dma_start(w_out["bv"], bv[:, :]).then_inc(stored, 16)
            sp.wait_ge(stored, 64)

        @block.tensor
        def _(pe):
            pe.wait_ge(loaded, 80)
            for c in range(DC):
                pe.matmul(w_ps[:, c, :], down[:, P * c:P * c + P], up[:, :], start=True, stop=True)
            for c in range(DC):
                pe.matmul(k_ps[:, c:c + 1], up[:, P * c:P * c + P], bl[:, :], start=True, stop=True)
            pe.wait_ge(rows_ready, 1)
            pe.matmul(v_ps[:, 0:D], bl_rows[:, :], up[:, D:2 * D], start=True, stop=True).then_inc(done, 1)

        @block.vector
        def _(dve):
            dve.wait_ge(loaded, 80)
            dve.tensor_copy(bl_rows[:, :], bl[:, :].to_broadcast([LATENT, P])).then_inc(rows_ready, 1)
            dve.wait_ge(done, 1)
            dve.tensor_copy(both[:, :, :], w_ps[:, :, :]).then_inc(ready, 1)
            dve.tensor_tensor(bk[:, :], k_ps[:, 0:DC], bk[:, :], ALU.add).then_inc(ready, 1)
            dve.tensor_tensor(bv[:, :], v_ps[:, 0:D], bv[:, :], ALU.add).then_inc(ready, 1)


def attention(nc, name, cross, x_in, x_out, ctx_in, mask_in, alibi, stats, mean, rstd, ident,
              ident_b, w_dram, const, count=NB):
    with ExitStack() as ctx:
        def sb(n, shape, dt=F32):
            return ctx.enter_context(nc.sbuf_tensor(f"{name}_{n}", shape, dt))

        def ps(n, shape):
            return ctx.enter_context(nc.psum_tensor(f"{name}_{n}", shape, F32))

        sem = Semaphores(nc, ctx, name)

        wq, wk, wv, wo = (sb(n, [P, DC, D]) for n in ("wq", "wk", "wv", "wo"))
        bq, bk = sb("bq", [P, DC]), sb("bk", [P, DC])
        bv, bo = sb("bv", [P, D]), sb("bo", [P, D])
        head_mask = sb("head_mask", [P, 8])
        x_t, x_r, xn, o_n, x_o = (sb(n, [P, 2, D]) for n in ("x_t", "x_r", "xn", "o_n", "x_o"))
        xnT, o_nT, qT, kT = (sb(n, [P, 2, DC, P]) for n in ("xnT", "o_nT", "qT", "kT"))
        k_diag = sb("k_diag", [P, 2, HEADS, P])
        v_pad = sb("v_pad", [P, 2, HEADS, 32])
        probs = sb("probs", [P, QUADS, 4, P])
        probsT = sb("probsT", [P, 2, 4, P])
        oT = sb("oT", [P, QUADS, P])
        neg_max, sums, inv = (sb(n, [P, 2, HEADS]) for n in ("neg_max", "sums", "inv"))
        s_ps = ps("scores", [P, QUADS, 4, P])
        o_ps = ps("o_ps", [P, QUADS, P])
        b_ps = ps("b_ps", [P, 512])
        p_ps = [ps("p0", [P, 512]), ps("p1", [P, 512])]

        loaded_w, scaled = sem("loaded_w"), sem("scaled")
        x_loaded = [sem("x_loaded0"), sem("x_loaded1")]
        r_loaded = [sem("r_loaded0"), sem("r_loaded1")]
        xn_ready, xt_done, xnT_ready = sem("xn_ready"), sem("xt_done"), sem("xnT_ready")
        q_done, k_done, v_done = sem("q_done"), sem("k_done"), sem("v_done")
        q_ready, k_ready, v_ready, diag_ready = sem("q_ready"), sem("k_ready"), sem("v_ready"), sem("diag_ready")
        s_done, max_ready, exp_ready = sem("s_done"), sem("max_ready"), sem("exp_ready")
        pt_done, pt_ready, pv_done = sem("pt_done"), sem("pt_ready"), sem("pv_done")
        oT_ready, back_done, on_ready, inv_ready = sem("oT_ready"), sem("back_done"), sem("on_ready"), sem("inv_ready")
        ont_done, onT_ready, wo_done = sem("ont_done"), sem("onT_ready"), sem("wo_done")
        r_biased, xo_ready, stat_ready = sem("r_biased"), sem("xo_ready"), sem("stat_ready")
        stored = [sem.kept("stored0"), sem.kept("stored1")]
        if cross:
            c_t = sb("c_t", [P, 2, D])
            cT = sb("cT", [P, 2, DC, P])
            mask_t = sb("mask_t", [P, 2, P], I32)
            mask_b = sb("mask_b", [P, 2, P], BF16)
            rows_k = sb("rows_k", [12, 2, HEADS * P], BF16)
            rows_q = sb("rows_q", [12, NB, P], BF16)
            c_loaded = [sem("c_loaded0"), sem("c_loaded1")]
            m_loaded = [sem("m_loaded0"), sem("m_loaded1")]
            k_rows_loaded = [sem("k_rows0"), sem("k_rows1")]
            ct_done, cT_ready, mask_ready = sem("ct_done"), sem("cT_ready"), sem("mask_ready")
        ctx.callback(sem.clear)
        block = ctx.enter_context(nc.Block())
        n_w = 9 + (3 if cross else 0)

        @block.sync
        def _(sp):
            for dst, key in ((wq, "wq"), (wk, "wk"), (wv, "wv"), (wo, "wo")):
                sp.dma_start(dst[:, :, :], w_dram[key]).then_inc(loaded_w, 16)
            for dst, key in ((bq, "bq"), (bk, "bk"), (bv, "bv"), (bo, "bo"), (head_mask, "head_mask")):
                sp.dma_start(dst[:, :], w_dram[key]).then_inc(loaded_w, 16)
            if cross:
                sp.dma_start(rows_q[:, :, :], alibi["q"]).then_inc(loaded_w, 16)
                for par in range(2):
                    sp.dma_start(rows_k[3:12, par, :], alibi["slopes"]).then_inc(loaded_w, 16)

            def step(at):
                b = at(0)
                if b:
                    wait(sp, xn_ready, b, 1, -1)
                    sp.dma_start(x_t[:, b.par, :], x_in[b.n]).then_inc(x_loaded[b.par], 16)
                    if cross:
                        wait(sp, ct_done, b, 1, -1)
                        sp.dma_start(c_t[:, b.par, :], ctx_in[b.n]).then_inc(c_loaded[b.par], 16)
                        wait(sp, mask_ready, b, 1, -1)
                        sp.dma_start(mask_t[:, b.par, :], mask_in[b.n]).then_inc(m_loaded[b.par], 16)
                        wait(sp, s_done, b, QUADS, -QUADS)
                        sp.dma_start(rows_k[0:3, b.par, :], alibi["k"][b.n]).then_inc(k_rows_loaded[b.par], 16)
                    wait(sp, xo_ready, b, 1, -1)
                    sp.dma_start(x_r[:, b.par, :], x_in[b.n]).then_inc(r_loaded[b.par], 16)
            pipeline(sp, count, 1, step)
            for par in range(2):
                sp.wait_ge(stored[par], 16 * (count // 2))

        def loaded(eng, sems, b):
            eng.wait_ge(sems[b.par], (b.n + (2 - b.par)) * 8)

        @block.tensor
        def _(pe):
            pe.wait_ge(scaled, 1)

            def scores(b, j):
                if j == 0:
                    wait(pe, q_ready, b, 1, 1)
                    wait(pe, diag_ready, b, 1, 1)
                    if cross:
                        wait(pe, mask_ready, b, 1, 1)
                        loaded(pe, k_rows_loaded, b)
                wait(pe, pt_ready, b, QUADS, j - 3)
                last = pe.matmul(s_ps[:, j, :, :], qT[:, b.par, j // 2, :],
                                 k_diag[:, b.par, 4 * j:4 * j + 4, :], start=True, stop=not cross)
                if cross:
                    pe.matmul(s_ps[:, j, :, :], ident_b[:, :],
                              mask_b[:, b.par, :].unsqueeze(1).to_broadcast([P, 4, P]), start=False, stop=False)
                    last = pe.matmul(s_ps[:, j, :, :], rows_q[:, b.n, :],
                                     rows_k[:, b.par, 512 * j:512 * j + 512].rearrange("p (a c) -> p a c", a=4),
                                     start=False, stop=True)
                last.then_inc(s_done, 1)

            def back(b):
                wait(pe, oT_ready, b, 1, 1)
                wait(pe, xo_ready, b, 1, 0)
                for j in range(QUADS):
                    last = pe.transpose(b_ps[:, P * j:P * j + P], oT[:, j, :], ident[:, :])
                last.then_inc(back_done, 1)

            def x_transpose(b):
                wait(pe, xn_ready, b, 1, 1)
                wait(pe, v_ready, b, 1, 0)
                for c in range(DC):
                    last = pe.transpose(p_ps[0][:, P * c:P * c + P], xn[:, b.par, P * c:P * c + P], ident[:, :])
                last.then_inc(xt_done, 1)
                if cross:
                    loaded(pe, c_loaded, b)
                    wait(pe, k_ready, b, 1, 0)
                    for c in range(DC):
                        last = pe.transpose(p_ps[1][:, P * c:P * c + P], c_t[:, b.par, P * c:P * c + P], ident[:, :])
                    last.then_inc(ct_done, 1)

            def on_transpose(b):
                wait(pe, on_ready, b, 1, 1)
                for c in range(DC):
                    last = pe.transpose(b_ps[:, P * c:P * c + P], o_n[:, b.par, P * c:P * c + P], ident[:, :])
                last.then_inc(ont_done, 1)

            def probs_transpose(b, j):
                wait(pe, exp_ready, b, QUADS, j + 1)
                for i in range(4):
                    last = pe.transpose(s_ps[:, j, i, :], probs[:, j, i, :], ident[:, :])
                last.then_inc(pt_done, 1)

            def project(b, w, src, bank, done):
                for m in range(DC):
                    for c in range(DC):
                        last = pe.matmul(p_ps[bank][:, P * m:P * m + P], w[:, c, P * m:P * m + P],
                                         src[:, b.par, c, :], start=(c == 0), stop=(c == DC - 1))
                last.then_inc(done, 1)

            def values(b, j):
                if j == 0:
                    wait(pe, v_ready, b, 1, 1)
                    wait(pe, oT_ready, b, 1, 0)
                wait(pe, pt_ready, b, QUADS, j + 1)
                for i in range(4):
                    last = pe.matmul(o_ps[32 * i:32 * i + 32, j, :], v_pad[:, b.par, 4 * j + i, :],
                                     probsT[:, j % 2, i, :], start=True, stop=True)
                last.then_inc(pv_done, 1)

            def step(at):
                b0, b1, b2 = at(0), at(1), at(2)
                src = cT if cross else xnT
                if b1:
                    scores(b1, 0)
                    scores(b1, 1)
                if b2:
                    back(b2)
                if b1:
                    scores(b1, 2)
                if b0:
                    x_transpose(b0)
                if b1:
                    scores(b1, 3)
                if b2:
                    on_transpose(b2)
                if b1:
                    probs_transpose(b1, 0)
                if b0:
                    if cross:
                        wait(pe, cT_ready, b0, 1, 1)
                    else:
                        wait(pe, xnT_ready, b0, 1, 1)
                        wait(pe, k_ready, b0, 1, 0)
                    project(b0, wk, src, 1, k_done)
                if b1:
                    probs_transpose(b1, 1)
                    values(b1, 0)
                if b0:
                    wait(pe, xnT_ready, b0, 1, 1)
                    project(b0, wq, xnT, 0, q_done)
                if b1:
                    probs_transpose(b1, 2)
                    values(b1, 1)
                if b2:
                    wait(pe, onT_ready, b2, 1, 1)
                    for c in range(DC):
                        last = pe.matmul(b_ps[:, 0:D], o_nT[:, b2.par, c, :], wo[:, c, :],
                                         start=(c == 0), stop=(c == DC - 1))
                    last.then_inc(wo_done, 1)
                if b1:
                    probs_transpose(b1, 3)
                    values(b1, 2)
                if b0:
                    wait(pe, q_ready, b0, 1, 1)
                    for c in range(DC):
                        last = pe.matmul(p_ps[0][:, 0:D], src[:, b0.par, c, :], wv[:, c, :],
                                         start=(c == 0), stop=(c == DC - 1))
                    last.then_inc(v_done, 1)
                if b1:
                    values(b1, 3)
            pipeline(pe, count, 3, step)

        @block.scalar
        def _(act):
            def exps(b, j):
                wait(act, max_ready, b, QUADS, j + 1)
                wait(act, pt_done, b, QUADS, j - 3)
                if j == 0:
                    wait(act, on_ready, b, 1, -1)
                for i in range(4):
                    h = 4 * j + i
                    last = act.activation(probs[:, j, i, :], s_ps[:, j, i, :], ACT.Exp,
                                          bias=neg_max[:, b.par, h:h + 1], scale=1.0,
                                          accum_out=sums[:, b.par, h:h + 1])
                last.then_inc(exp_ready, 1)

            def step(at):
                b0, b1, b2 = at(0), at(1), at(2)
                if b2:
                    wait(act, pv_done, b2, QUADS, QUADS)
                    act.copy(oT[:, :, :], o_ps[:, :, :]).then_inc(oT_ready, 1)
                if b1:
                    exps(b1, 0)
                if b0:
                    wait(act, xt_done, b0, 1, 1)
                    wait(act, v_done if not cross else q_done, b0, 1, -1)
                    act.copy(xnT[:, b0.par, :, :], p_ps[0][:, 0:D].rearrange("p (c t) -> p c t", c=DC))\
                       .then_inc(xnT_ready, 1)
                    if cross:
                        wait(act, ct_done, b0, 1, 1)
                        wait(act, v_done, b0, 1, -1)
                        act.copy(cT[:, b0.par, :, :], p_ps[1][:, 0:D].rearrange("p (c t) -> p c t", c=DC))\
                           .then_inc(cT_ready, 1)
                if b1:
                    exps(b1, 1)
                if b2:
                    wait(act, ont_done, b2, 1, 1)
                    wait(act, wo_done, b2, 1, -1)
                    act.copy(o_nT[:, b2.par, :, :], b_ps[:, 0:D].rearrange("p (c t) -> p c t", c=DC))\
                       .then_inc(onT_ready, 1)
                if b1:
                    exps(b1, 2)
                    exps(b1, 3)
            pipeline(act, count, 3, step)

        @block.vector
        def _(dve):
            dve.memset(v_pad[:, :, :, :], 0.0)
            dve.wait_ge(loaded_w, 16 * n_w)
            dve.tensor_scalar(wq[:, :, :], wq[:, :, :], HD ** -0.5, None, ALU.mult)
            dve.tensor_scalar(bq[:, :], bq[:, :], HD ** -0.5, None, ALU.mult).then_inc(scaled, 1)
            dve.wait_ge(scaled, 1)

            def maxima(b, j):
                wait(dve, s_done, b, QUADS, j + 1)
                if j == 0:
                    wait(dve, exp_ready, b, QUADS, -QUADS)
                dve.tensor_reduce(neg_max[:, b.par, 4 * j:4 * j + 4], s_ps[:, j, :, :], AX.X, ALU.max,
                                  negate=True).then_inc(max_ready, 1)

            def probsT_copy(b, j):
                wait(dve, pt_done, b, QUADS, j + 1)
                wait(dve, pv_done, b, QUADS, j - 1)
                dve.tensor_copy(probsT[:, j % 2, :, :], s_ps[:, j, :, :]).then_inc(pt_ready, 1)

            def step(at):
                b0, b1, b2 = at(0), at(1), at(2)
                if b0:
                    loaded(dve, x_loaded, b0)
                    wait(dve, xt_done, b0, 1, -1)
                    dve.tensor_scalar(xn[:, b0.par, :], x_t[:, b0.par, :], mean[:, bass.ds(b0.n, 1)],
                                      rstd[:, bass.ds(b0.n, 1)], ALU.subtract, ALU.mult).then_inc(xn_ready, 1)
                    if cross:
                        loaded(dve, m_loaded, b0)
                        wait(dve, s_done, b0, QUADS, -QUADS)
                        dve.tensor_scalar(mask_b[:, b0.par, :], mask_t[:, b0.par, :], 0.0, -3.0e38,
                                          ALU.is_equal, ALU.mult).then_inc(mask_ready, 1)
                if b1:
                    maxima(b1, 0)
                if b2:
                    src = sums
                    wait(dve, exp_ready, b2, QUADS, QUADS)
                    if cross:
                        dve.tensor_scalar(sums[:, b2.par, :], sums[:, b2.par, :], 1.0, None, ALU.add)\
                           .then_inc(inv_ready, 1)
                        wait(dve, inv_ready, b2, 2, 1)
                    dve.reciprocal(inv[:, b2.par, :], sums[:, b2.par, :]).then_inc(inv_ready, 1)
                    wait(dve, inv_ready, b2, 1 + cross, 1 + cross)
                    wait(dve, back_done, b2, 1, 1)
                    wait(dve, ont_done, b2, 1, -1)
                    dve.tensor_tensor(o_n[:, b2.par, :].rearrange("p (h d) -> p h d", h=HEADS),
                                      b_ps[:, :].rearrange("p (h d) -> p h d", h=HEADS)[:, :, 0:HD],
                                      inv[:, b2.par, :].unsqueeze(2).to_broadcast([P, HEADS, HD]),
                                      ALU.mult).then_inc(on_ready, 1)
                if b1:
                    maxima(b1, 1)
                    maxima(b1, 2)
                    maxima(b1, 3)
                    probsT_copy(b1, 0)
                if b0:
                    wait(dve, k_done, b0, 1, 1)
                    wait(dve, diag_ready, b0, 1, -1)
                    dve.tensor_tensor(kT[:, b0.par, :, :], p_ps[1][:, 0:D].rearrange("p (c t) -> p c t", c=DC),
                                      bk[:, :].unsqueeze(2).to_broadcast([P, DC, P]), ALU.add)\
                       .then_inc(k_ready, 1)
                if b1:
                    probsT_copy(b1, 1)
                if b0:
                    wait(dve, q_done, b0, 1, 1)
                    wait(dve, s_done, b0, QUADS, -QUADS)
                    dve.tensor_tensor(qT[:, b0.par, :, :], p_ps[0][:, 0:D].rearrange("p (c t) -> p c t", c=DC),
                                      bq[:, :].unsqueeze(2).to_broadcast([P, DC, P]), ALU.add)\
                       .then_inc(q_ready, 1)
                if b1:
                    probsT_copy(b1, 2)
                if b2:
                    wait(dve, wo_done, b2, 1, 1)
                    wait(dve, r_biased, b2, 1, 1)
                    if not b2.known() or b2.n >= 2:
                        dve.wait_ge(stored[b2.par], (b2.n - b2.par) * 8)
                    dve.tensor_tensor(x_o[:, b2.par, :], b_ps[:, 0:D], x_r[:, b2.par, :], ALU.add)\
                       .then_inc(xo_ready, 1)
                    wait(dve, xo_ready, b2, 1, 1)
                    dve.bn_stats(stats[:, b2.n, :], x_o[:, b2.par, :]).then_inc(stat_ready, 1)
                if b1:
                    probsT_copy(b1, 3)
                if b0:
                    wait(dve, v_done, b0, 1, 1)
                    wait(dve, pv_done, b0, QUADS, -QUADS)
                    dve.tensor_tensor(v_pad[:, b0.par, :, 0:HD], p_ps[0][:, 0:D].rearrange("p (h d) -> p h d", h=HEADS),
                                      bv[:, :].rearrange("p (h d) -> p h d", h=HEADS), ALU.add)\
                       .then_inc(v_ready, 1)
            pipeline(dve, count, 3, step)

        @block.gpsimd
        def _(pool):
            pool.wait_ge(loaded_w, 16 * n_w)

            def step(at):
                b0, b1, b2 = at(0), at(1), at(2)
                if b2:
                    loaded(pool, r_loaded, b2)
                    pool.tensor_tensor(x_r[:, b2.par, :], x_r[:, b2.par, :], bo[:, :], ALU.add)\
                        .then_inc(r_biased, 1)
                if b0:
                    wait(pool, k_ready, b0, 1, 1)
                    wait(pool, s_done, b0, QUADS, -QUADS)
                    for c in range(DC):
                        last = pool.tensor_tensor(
                            k_diag[:, b0.par, 8 * c:8 * c + 8, :],
                            kT[:, b0.par, c, :].unsqueeze(1).to_broadcast([P, 8, P]),
                            head_mask[:, :].unsqueeze(2).to_broadcast([P, 8, P]), ALU.mult)
                    last.then_inc(diag_ready, 1)
                if b2:
                    wait(pool, xo_ready, b2, 1, 1)
                    pool.dma_start(x_out[b2.n], x_o[:, b2.par, :]).then_inc(stored[b2.par], 16)
            pipeline(pool, count, 3, step)


HID = 1024
HC = HID // P
EXPERTS = 8
NEG_INF = -1.0e9
ROUNDER = 12582912.0
PAIR = 2
WIDE = D + 2
ROUTE_STEPS = 24


def expert_tiles(count):
    return 2 * count + EXPERTS - 1


def expert_rows(count):
    return (count + 1) * P


def sorted_rows(count):
    return EXPERTS * expert_rows(count) + EXPERTS * P


def experts_ffn(nc, x_in, x_out, mean, rstd, ident, w_dram, xg, count=NB):
    name = "moe"
    tiles, pairs, part = expert_tiles(count), count // PAIR, expert_rows(count)
    with ExitStack() as ctx:
        def sb(n, shape, dt=F32, where=None):
            return (where or ctx).enter_context(nc.sbuf_tensor(f"{name}_{n}", shape, dt))

        def ps(n, shape, where):
            return where.enter_context(nc.psum_tensor(f"{name}_ps_{n}", shape, F32))

        sem = Semaphores(nc, ctx, name)

        w1, w2 = sb("w1", [P, EXPERTS, DC, HID]), sb("w2", [P, EXPERTS, HC, D])
        b1, b2 = sb("b1", [P, EXPERTS * HC]), sb("b2", [P, EXPERTS * D])
        tile_expert, tile_row = sb("tile_expert", [1, tiles], I32), sb("tile_row", [1, tiles], I32)
        pad_row = sb("pad_row", [1, EXPERTS], I32)
        seen = sb("seen", [P, EXPERTS])
        padding = sb("padding", [P, WIDE])
        ones = sb("ones", [P, P])
        w1_loaded, w2_loaded, b_loaded, r_loaded = sem("w1_loaded"), sem("w2_loaded"), sem("b_loaded"), sem("r_loaded")
        out_begun, padded = sem("out_begun"), sem("padded")

        with ExitStack() as route:
            wr, br, falling = (sb(n, shape, where=route) for n, shape in (
                ("wr", [P, DC, EXPERTS]), ("br", [P, EXPERTS]), ("falling", [P, EXPERTS])))
            before, base = sb("before", [P, P], where=route), sb("base", [P, EXPERTS], where=route)
            token_no = sb("token_no", [P, count], where=route)
            nothing, numbers = sb("nothing", [P, PAIR], where=route), sb("numbers", [P, 2, PAIR], where=route)
            x_t = sb("x_t", [P, 2, PAIR, D], where=route)
            row = sb("row", [P, 2, PAIR, 2, WIDE], where=route)
            xnT = sb("xnT", [P, 2, PAIR, DC, P], where=route)
            shape = [P, PAIR, EXPERTS]
            logits, equal, rest, chosen, place = (sb(n, shape, where=route) for n in (
                "logits", "equal", "rest", "chosen", "place"))
            hot, mine = (sb(n, [P, 2, PAIR, EXPERTS], where=route) for n in ("hot", "mine"))
            tops, exps = (sb(n, [P, PAIR, EXPERTS], where=route) for n in ("tops", "exps"))
            key, low, total = (sb(n, [P, PAIR], where=route) for n in ("key", "low", "total"))
            slot = sb("slot", [P, 2, PAIR], where=route)
            index = sb("index", [P, 2, 2, PAIR], I32, where=route)
            xt_ps, l_ps = ps("xt", [P, 2, 512], route), ps("l", [P, 2, 512], route)
            rank_ps = ps("rank", [P, 512], route)
            x_loaded = [sem("x_loaded0"), sem("x_loaded1")]
            scattered = [sem.kept("scattered0"), sem.kept("scattered1")]
            prepared, xn_ready, twin_ready, xt_done, xnT_ready, l_done = (
                sem(n) for n in ("prepared", "xn_ready", "twin_ready", "xt_done", "xnT_ready", "l_done"))
            route_step, chosen_ready, rank_done, low_ready, exps_ready, index_ready, token_ready = (
                sem(n) for n in ("route_step", "chosen_ready", "rank_done", "low_ready", "exps_ready",
                                 "index_ready", "token_ready"))

            def row_free(eng, g):
                if not g.known() or g.n >= 2:
                    eng.wait_ge(scattered[g.par], (g.n - g.par) * 8 * 2 * PAIR)

            with nc.Block() as block:
                @block.sync
                def _(sp):
                    for dst, key_ in ((br, "br"), (falling, "falling"), (before, "before"), (base, "base"),
                                      (ones, "ones"), (token_no, "token_no"), (padding, "padding")):
                        sp.dma_start(dst[:, :], w_dram[key_]).then_inc(r_loaded, 16)
                    sp.dma_start(wr[:, :, :], w_dram["wr"]).then_inc(r_loaded, 16)

                    def step(at):
                        g = at(0)
                        if g:
                            wait(sp, xn_ready, g, 1, -1)
                            sp.dma_start(x_t[:, g.par, :, :],
                                         x_in.rearrange("(g r) p d -> g p r d", r=PAIR)[g.n]).then_inc(x_loaded[g.par], 16)
                    pipeline(sp, pairs, 1, step)

                @block.tensor
                def _(pe):
                    pe.wait_ge(r_loaded, 16 * 8)
                    pe.wait_ge(prepared, 1)

                    def step(at):
                        g0, g1 = at(0), at(1)
                        if g1:
                            wait(pe, xnT_ready, g1, 1, 1)
                            wait(pe, chosen_ready, g1, 1, -1)
                            for r in range(PAIR):
                                for c in range(DC):
                                    last = pe.matmul(l_ps[:, g1.par, EXPERTS * r:EXPERTS * r + EXPERTS],
                                                     xnT[:, g1.par, r, c, :], wr[:, c, :], start=(c == 0), stop=(c == DC - 1))
                            last.then_inc(l_done, 1)
                        if g1:
                            wait(pe, chosen_ready, g1, 1, 1)
                            for r in range(PAIR):
                                out = rank_ps[:, EXPERTS * r:EXPERTS * r + EXPERTS]
                                pe.matmul(out, before[:, :], chosen[:, r, :], start=True, stop=False)
                                for earlier in range(r):
                                    pe.matmul(out, ones[:, :], chosen[:, earlier, :], start=False, stop=False)
                                last = pe.matmul(out, ones[:, :], seen[:, :], start=False, stop=True)
                            last.then_inc(rank_done, 1)
                        if g0:
                            wait(pe, xn_ready, g0, 1, 1)
                            wait(pe, xnT_ready, g0, 1, -1)
                            for r in range(PAIR):
                                for c in range(DC):
                                    col = P * (DC * r + c)
                                    last = pe.transpose(xt_ps[:, g0.par, col:col + P], row[:, g0.par, r, 0, P * c:P * c + P],
                                                        ident[:, :])
                            last.then_inc(xt_done, 1)
                    pipeline(pe, pairs, 2, step)

                @block.scalar
                def _(act):
                    act.dma_start(b1[:, :], w_dram["b1"]).then_inc(b_loaded, 16)
                    act.dma_start(b2[:, :], w_dram["b2"]).then_inc(b_loaded, 16)
                    act.wait_ge(r_loaded, 16 * 8)
                    act.dma_start(x_out[count], padding[:, 0:D]).then_inc(out_begun, 16)
                    act.dma_start(xg[EXPERTS * part:EXPERTS * (part + P)].rearrange("(t p) w -> p t w", p=P),
                                  padding[:, :].unsqueeze(1).to_broadcast([P, EXPERTS, WIDE])).then_inc(padded, 16)
                    loads = [(w[:, :, :, :].rearrange("p a b c -> p (a b c)").rearrange("p (g n) -> p g n", g=pairs),
                              w_dram[key_].rearrange("p a b c -> p (a b c)").rearrange("p (g n) -> p g n", g=pairs), done)
                             for w, key_, done in ((w1, "w1", w1_loaded), (w2, "w2", w2_loaded))]

                    def step(at):
                        g0, g1 = at(0), at(1)
                        if g0:
                            here = slice(g0.n, g0.n + 1) if g0.known() else bass.ds(g0.n, 1)
                            for w_sb, w_in, done in loads:
                                act.dma_start(w_sb[:, here, :], w_in[:, here, :]).then_inc(done, 16)
                            act.dma_start(x_out[0:count].rearrange("(g r) p d -> g (r p) d", r=PAIR)[g0.n],
                                          x_in.rearrange("(g r) p d -> g (r p) d", r=PAIR)[g0.n]).then_inc(out_begun, 16)
                        if g1:
                            wait(act, low_ready, g1, 1, 1)
                            for r in range(PAIR):
                                last = act.activation(exps[:, r, :], tops[:, r, :], ACT.Exp, bias=low[:, r:r + 1], scale=1.0,
                                                      accum_out=total[:, r:r + 1])
                            last.then_inc(exps_ready, 1)
                        if g0:
                            wait(act, xn_ready, g0, 1, 1)
                            row_free(act, g0)
                            act.copy(row[:, g0.par, :, 1, 0:D], row[:, g0.par, :, 0, 0:D]).then_inc(twin_ready, 1)
                            wait(act, xt_done, g0, 1, 1)
                            wait(act, l_done, g0, 1, -1)
                            act.copy(xnT[:, g0.par, :, :, :].rearrange("p r c t -> p (r c t)"), xt_ps[:, g0.par, :])\
                               .then_inc(xnT_ready, 1)
                    pipeline(act, pairs, 2, step)

                @block.vector
                def _(dve):
                    dve.memset(seen[:, :], 0.0)
                    dve.memset(tops[:, :, :], NEG_INF)
                    dve.memset(nothing[:, :], 0.0).then_inc(prepared, 1)
                    dve.wait_ge(prepared, 1)
                    dve.wait_ge(r_loaded, 16 * 8)
                    experts = falling[:, :].unsqueeze(1).to_broadcast(shape)

                    def over_experts(t):
                        return t.unsqueeze(2).to_broadcast(shape)

                    def step(at):
                        g0, g1 = at(0), at(1)
                        if g1:
                            done = [0]

                            def link(instruction):
                                done[0] += 1
                                instruction.then_inc(route_step, 1)
                                wait(dve, route_step, g1, ROUTE_STEPS, done[0])

                            def largest(scores, k):
                                top = tops[:, :, k]
                                link(dve.tensor_reduce(top, scores[:, :, :], AX.X, ALU.max))
                                link(dve.tensor_tensor(equal[:, :, :], scores[:, :, :], over_experts(top), ALU.is_equal))
                                link(dve.tensor_tensor(equal[:, :, :], equal[:, :, :], experts, ALU.mult))
                                link(dve.tensor_reduce(key[:, :], equal[:, :, :], AX.X, ALU.max))
                                link(dve.tensor_tensor(hot[:, k, :, :], experts, over_experts(key[:, :]), ALU.is_equal))

                            wait(dve, l_done, g1, 1, 1)
                            wait(dve, exps_ready, g1, 1, 0)
                            link(dve.tensor_tensor(logits[:, :, :],
                                                   l_ps[:, g1.par, 0:PAIR * EXPERTS].rearrange("p (r e) -> p r e", r=PAIR),
                                                   br[:, :].unsqueeze(1).to_broadcast(shape), ALU.add))
                            largest(logits, 0)
                            link(dve.scalar_tensor_tensor(out=rest[:, :, :], in0=hot[:, 0, :, :], scalar=-3.0e38,
                                                          in1=logits[:, :, :], op0=ALU.mult, op1=ALU.add))
                            largest(rest, 1)
                            dve.tensor_tensor(chosen[:, :, :], hot[:, 0, :, :], hot[:, 1, :, :], ALU.add)\
                                .then_inc(chosen_ready, 1)
                            dve.tensor_scalar(low[:, :], tops[:, :, 0], NEG_INF, -1.0, ALU.max, ALU.mult)\
                                .then_inc(low_ready, 1)
                            wait(dve, rank_done, g1, 1, 1)
                            link(dve.tensor_tensor(place[:, :, :],
                                                   rank_ps[:, 0:PAIR * EXPERTS].rearrange("p (r e) -> p r e", r=PAIR),
                                                   base[:, :].unsqueeze(1).to_broadcast(shape), ALU.add))
                            for r in range(PAIR):
                                link(dve.tensor_tensor(seen[:, :], seen[:, :], chosen[:, r, :], ALU.add))
                            link(dve.tensor_tensor(mine[:, :, :, :], hot[:, :, :, :],
                                                   place[:, :, :].unsqueeze(1).to_broadcast([P, 2, PAIR, EXPERTS]), ALU.mult))
                            link(dve.tensor_reduce(slot[:, :, :], mine[:, :, :, :], AX.X, ALU.add))
                            row_free(dve, g1)
                            link(dve.tensor_copy(index[:, g1.par, :, :], slot[:, :, :]))
                            wait(dve, token_ready, g1, 1, 1)
                            link(dve.tensor_copy(row[:, g1.par, :, :, D + 1],
                                                 numbers[:, g1.par, :].unsqueeze(2).to_broadcast([P, PAIR, 2])))
                            wait(dve, exps_ready, g1, 1, 1)
                            link(dve.reciprocal(total[:, :], total[:, :]))
                            link(dve.tensor_tensor(row[:, g1.par, :, :, D], exps[:, :, 0:2],
                                                   total[:, :].unsqueeze(2).to_broadcast([P, PAIR, 2]), ALU.mult))
                            while done[0] < ROUTE_STEPS:
                                dve.sem_inc(route_step, 1)
                                done[0] += 1
                            dve.sem_inc(index_ready, 1)
                        if g0:
                            dve.wait_ge(x_loaded[g0.par], (g0.n + (2 - g0.par)) * 8)
                            row_free(dve, g0)
                            wait(dve, xt_done, g0, 1, -1)
                            for r in range(PAIR):
                                column = bass.ds(g0.n * PAIR + r, 1)
                                last = dve.tensor_scalar(row[:, g0.par, r, 0, 0:D], x_t[:, g0.par, r, :], mean[:, column],
                                                         rstd[:, column], ALU.subtract, ALU.mult)
                            last.then_inc(xn_ready, 1)
                    pipeline(dve, pairs, 2, step)

                @block.gpsimd
                def _(pool):
                    pool.wait_ge(r_loaded, 16 * 8)
                    pool.wait_ge(prepared, 1)

                    def step(at):
                        g0, g1 = at(0), at(1)
                        if g1:
                            wait(pool, twin_ready, g1, 1, 1)
                            wait(pool, index_ready, g1, 1, 1)
                        if g0:
                            pool.tensor_tensor(numbers[:, g0.par, :], token_no[:, bass.ds(g0.n * PAIR, PAIR)],
                                               nothing[:, :], ALU.add).then_inc(token_ready, 1)
                        if g1:
                            for r in range(PAIR):
                                for k in range(2):
                                    pool.indirect_dma_start(
                                        xg, bass.IndirectOffsetOnAxis(ap=index[:, g1.par, k, r:r + 1], axis=0),
                                        row[:, g1.par, r, k, :], None).then_inc(scattered[g1.par], 16)
                    pipeline(pool, pairs, 2, step)
                    for par in range(2):
                        pool.wait_ge(scattered[par], 16 * 2 * PAIR * (pairs // 2))

            plan_tiles(nc, route, sb, ps, sem, w_dram, base, seen, ones, pad_row, tile_expert, tile_row, tiles, part)

        with ExitStack() as work:
            x_t = sb("e_x_t", [P, 2, WIDE], where=work)
            y, y_s = sb("e_y", [P, 2, D], where=work), sb("e_y_s", [P, 2, D], where=work)
            share, number = sb("e_share", [P, 2], where=work), sb("e_number", [P, 2], where=work)
            token = sb("e_token", [P, 2], I32, where=work)
            xT = sb("e_xT", [P, 2, DC, P], where=work)
            h = sb("e_h", [P, HID], where=work)
            h_b, hT = sb("e_h_b", [P, HC, P], where=work), sb("e_hT", [P, HC, P], where=work)
            x_ps, y_ps = ps("e_x", [P, 512], work), ps("e_y", [P, 512], work)
            h_ps, ht_ps = ps("e_h", [P, 2, 512], work), ps("e_ht", [P, 2, 4, P], work)
            x_loaded = [sem("e_x_loaded0"), sem("e_x_loaded1")]
            added = sem.kept("e_added")
            share_ready, scaled = sem("e_share_ready"), sem("e_scaled")
            xt_done, xT_ready, h_done, h_ready, ht_done, hb_ready, hT_ready, y_done, y_ready = (
                sem(f"e_{n}") for n in ("xt_done", "xT_ready", "h_done", "h_ready", "ht_done", "hb_ready",
                                        "hT_ready", "y_done", "y_ready"))

            def expert_of(eng, t):
                column = tile_expert[0:1, t.n:t.n + 1] if t.known() else tile_expert[0:1, bass.ds(t.n, 1)]
                return eng.value_load(column, min_val=0, max_val=EXPERTS - 1)

            with nc.Block() as block:
                @block.sync
                def _(sp):
                    for e in range(EXPERTS):
                        first = sp.value_load(pad_row[0:1, e:e + 1], min_val=0, max_val=EXPERTS * part - P)
                        sp.dma_start(xg[bass.ds(first, P)], padding[:, :]).then_inc(padded, 16)
                    sp.wait_ge(padded, 16 * (EXPERTS + 1))

                    def step(at):
                        t = at(0)
                        if t:
                            column = tile_row[0:1, t.n:t.n + 1] if t.known() else tile_row[0:1, bass.ds(t.n, 1)]
                            first = sp.value_load(column, min_val=0, max_val=EXPERTS * (part + P) - P)
                            wait(sp, xt_done, t, 1, -1)
                            wait(sp, share_ready, t, 1, -1)
                            sp.dma_start(x_t[:, t.par, :], xg[bass.ds(first, P)]).then_inc(x_loaded[t.par], 16)
                    pipeline(sp, tiles, 1, step)

                @block.tensor
                def _(pe):
                    def h_transpose(t, j):
                        wait(pe, h_ready, t, 2, j + 1)
                        wait(pe, hb_ready, t, 2, j - 1)
                        for c in range(4):
                            col = P * (4 * j + c)
                            last = pe.transpose(ht_ps[:, j, c, :], h[:, col:col + P], ident[:, :])
                        last.then_inc(ht_done, 1)

                    pe.wait_ge(w1_loaded, 16 * pairs)
                    pe.wait_ge(w2_loaded, 16 * pairs)

                    def step(at):
                        t0, t1 = at(0), at(1)
                        if t1:
                            h_transpose(t1, 0)
                        if t0:
                            pe.wait_ge(x_loaded[t0.par], (t0.n + (2 - t0.par)) * 8)
                            wait(pe, xT_ready, t0, 1, 0)
                            for c in range(DC):
                                last = pe.transpose(x_ps[:, P * c:P * c + P], x_t[:, t0.par, P * c:P * c + P], ident[:, :])
                            last.then_inc(xt_done, 1)
                        if t1:
                            h_transpose(t1, 1)
                        if t0:
                            e0 = expert_of(pe, t0)
                            wait(pe, xT_ready, t0, 1, 1)
                            for j in range(2):
                                wait(pe, h_ready, t0, 2, j - 1)
                                for c in range(DC):
                                    last = pe.matmul(h_ps[:, j, :], xT[:, t0.par, c, :],
                                                     w1[:, bass.ds(e0, 1), c, 512 * j:512 * j + 512].rearrange("p a n -> p (a n)"),
                                                     start=(c == 0), stop=(c == DC - 1))
                                last.then_inc(h_done, 1)
                        if t1:
                            e1 = expert_of(pe, t1)
                            wait(pe, hT_ready, t1, 2, 2)
                            wait(pe, y_ready, t1, 1, 0)
                            for c in range(HC):
                                last = pe.matmul(y_ps[:, 0:D], hT[:, c, :],
                                                 w2[:, bass.ds(e1, 1), c, :].rearrange("p a n -> p (a n)"),
                                                 start=(c == 0), stop=(c == HC - 1))
                            last.then_inc(y_done, 1)
                    pipeline(pe, tiles, 2, step)

                @block.scalar
                def _(act):
                    def step(at):
                        t0, t1 = at(0), at(1)
                        if t0:
                            wait(act, xt_done, t0, 1, 1)
                            wait(act, h_done, t0, 2, -2)
                            act.copy(xT[:, t0.par, :, :], x_ps[:, 0:D].rearrange("p (c t) -> p c t", c=DC))\
                               .then_inc(xT_ready, 1)
                        if t1:
                            for j in range(2):
                                wait(act, hb_ready, t1, 2, j + 1)
                                wait(act, y_done, t1, 1, 0)
                                act.activation(hT[:, 4 * j:4 * j + 4, :], h_b[:, 4 * j:4 * j + 4, :], ACT.Relu)\
                                   .then_inc(hT_ready, 1)
                        if t0:
                            for j in range(2):
                                wait(act, h_done, t0, 2, j + 1)
                                wait(act, ht_done, t0, 2, 0)
                                act.copy(h[:, 512 * j:512 * j + 512], h_ps[:, j, :]).then_inc(h_ready, 1)
                    pipeline(act, tiles, 2, step)

                @block.vector
                def _(dve):
                    dve.wait_ge(b_loaded, 32)

                    def step(at):
                        t0, t1 = at(0), at(1)
                        if t0:
                            dve.wait_ge(x_loaded[t0.par], (t0.n + (2 - t0.par)) * 8)
                            wait(dve, scaled, t0, 1, -1)
                            dve.tensor_copy(share[:, t0.par:t0.par + 1], x_t[:, t0.par, D:D + 1])
                            dve.tensor_copy(number[:, t0.par:t0.par + 1], x_t[:, t0.par, D + 1:WIDE]).then_inc(share_ready, 1)
                        if t1:
                            e1 = expert_of(dve, t1)
                            for j in range(2):
                                wait(dve, ht_done, t1, 2, j + 1)
                                wait(dve, hT_ready, t1, 2, j - 1)
                                dve.tensor_tensor(h_b[:, 4 * j:4 * j + 4, :], ht_ps[:, j, :, :],
                                                  b1[:, bass.ds(e1 * HC + 4 * j, 4)].unsqueeze(2).to_broadcast([P, 4, P]),
                                                  ALU.add).then_inc(hb_ready, 1)
                            wait(dve, added, t1, 16, -16)
                            wait(dve, share_ready, t1, 1, 1)
                            dve.tensor_copy(token[:, t1.par:t1.par + 1], number[:, t1.par:t1.par + 1])
                            wait(dve, scaled, t1, 1, -1)
                            wait(dve, y_done, t1, 1, 1)
                            dve.tensor_tensor(y[:, t1.par, :], y_ps[:, 0:D], b2[:, bass.ds(e1 * D, D)], ALU.add)\
                                .then_inc(y_ready, 1)
                    pipeline(dve, tiles, 2, step)

                @block.gpsimd
                def _(pool):
                    pool.wait_ge(out_begun, 16 * (pairs + 1))

                    def step(at):
                        t1, t2 = at(1), at(2)
                        if t2:
                            wait(pool, scaled, t2, 1, 1)
                            wait(pool, added, t2, 16, 0)
                        if t1:
                            wait(pool, share_ready, t1, 1, 1)
                            wait(pool, y_ready, t1, 1, 1)
                            pool.tensor_tensor(y_s[:, t1.par, :], y[:, t1.par, :],
                                               share[:, t1.par:t1.par + 1].to_broadcast([P, D]), ALU.mult)\
                                .then_inc(scaled, 1)
                        if t2:
                            pool.indirect_dma_start(
                                x_out.rearrange("b p d -> (b p) d"),
                                bass.IndirectOffsetOnAxis(ap=token[:, t2.par:t2.par + 1], axis=0),
                                y_s[:, t2.par, :], None, compute_op=ALU.add).then_inc(added, 16)
                    pipeline(pool, tiles, 3, step)
                    pool.wait_ge(added, 16 * tiles)
        sem.clear()


def plan_tiles(nc, where, sb, ps, sem, w_dram, base, seen, ones, pad_row, tile_expert, tile_row, tiles, part):
    tile_no = sb("tile_no", [1, tiles], where=where)
    counts, n_tiles, end_a, end_b, pad = (sb(n, [P, EXPERTS], where=where) for n in (
        "counts", "n_tiles", "end_a", "end_b", "pad"))
    passed, weighed = (sb(n, [1, tiles, EXPERTS], where=where) for n in ("passed", "weighed"))
    number, started, number_7 = (sb(n, [1, tiles], where=where) for n in ("number", "started", "number_7"))
    count_ps = ps("count", [P, 512], where)
    loaded, plan_step, counted = (sem(f"plan_{n}") for n in ("loaded", "step", "counted"))
    shape = [1, tiles, EXPERTS]

    with nc.Block() as block:
        @block.sync
        def _(sp):
            sp.dma_start(tile_no[:, :], w_dram["tile_no"]).then_inc(loaded, 16)

        @block.tensor
        def _(pe):
            pe.matmul(count_ps[:, 0:EXPERTS], ones[:, :], seen[:, :], start=True, stop=True).then_inc(counted, 1)

        @block.vector
        def _(dve):
            link = chained(dve, plan_step)
            dve.wait_ge(loaded, 16)
            dve.wait_ge(counted, 1)
            link(dve.tensor_copy(counts[:, :], count_ps[:, 0:EXPERTS]))
            link(dve.tensor_tensor(pad[:, :], counts[:, :], base[:, :], ALU.add))
            link(dve.tensor_copy(pad_row[:, :], pad[0:1, :]))
            link(dve.tensor_scalar(n_tiles[:, :], counts[:, :], 1.0 / P, (P - 1) / P - 0.5 + 0.5 / P, ALU.mult, ALU.add))
            link(dve.tensor_scalar(n_tiles[:, :], n_tiles[:, :], ROUNDER, ROUNDER, ALU.add, ALU.subtract))
            link(dve.tensor_copy(end_a[:, :], n_tiles[:, :]))
            end, other, shift = end_a, end_b, 1
            while shift < EXPERTS:
                link(dve.tensor_copy(other[:, 0:shift], end[:, 0:shift]))
                link(dve.tensor_tensor(other[:, shift:], end[:, shift:], end[:, :EXPERTS - shift], ALU.add))
                end, other, shift = other, end, 2 * shift
            link(dve.tensor_tensor(passed[:, :, :], end[0:1, :].unsqueeze(1).to_broadcast(shape),
                                   tile_no[:, :].unsqueeze(2).to_broadcast(shape), ALU.is_le))
            link(dve.tensor_reduce(number[:, :], passed[:, :, :], AX.X, ALU.add))
            link(dve.tensor_tensor(weighed[:, :, :], passed[:, :, :], n_tiles[0:1, :].unsqueeze(1).to_broadcast(shape), ALU.mult))
            link(dve.tensor_reduce(started[:, :], weighed[:, :, :], AX.X, ALU.add))
            link(dve.tensor_scalar(number_7[:, :], number[:, :], float(EXPERTS - 1), None, ALU.min))
            link(dve.tensor_copy(tile_expert[:, :], number_7[:, :]))
            link(dve.tensor_tensor(started[:, :], tile_no[:, :], started[:, :], ALU.subtract))
            link(dve.tensor_scalar(started[:, :], started[:, :], float(P), None, ALU.mult))
            link(dve.scalar_tensor_tensor(out=started[:, :], in0=number[:, :], scalar=float(part), in1=started[:, :],
                                          op0=ALU.mult, op1=ALU.add))
            link(dve.tensor_copy(tile_row[:, :], started[:, :]))


RES = float(1.0 / np.sqrt(2.0))
CHUNK = 64
HC = HID // P
RMS_EPS = 1e-6
Q_EPS = float(np.finfo(np.float32).eps)


def mixer(nc, x_in, x_out, stats, mean, rstd, scale, ident, w_dram, count=NB):
    name = "mix"
    with ExitStack() as ctx:
        def sb(n, shape, dt=F32):
            return ctx.enter_context(nc.sbuf_tensor(f"{name}_{n}", shape, dt))

        def ps(n, shape):
            return ctx.enter_context(nc.psum_tensor(f"{name}_{n}", shape, F32))

        sem = Semaphores(nc, ctx, name)

        w_in = sb("w_in", [P, DC, 5 * D])
        w_out = sb("w_out", [P, DC, D])
        w_fc = sb("w_fc", [P, DC, HID])
        w_pr = sb("w_pr", [P, HC, D])
        norm1, norm2 = sb("norm1", [P, DC]), sb("norm2", [P, DC])
        x_t, x_again, x_ln, h_n, x_1, x_s, h2_n, x_o, junk = (
            sb(n, [P, 2, D]) for n in ("x_t", "x_again", "x_ln", "h_n", "x_1", "x_s", "h2_n", "x_o", "junk"))
        hT, h2T, vT, kT, uT, aT, gT, prefix, inv_prefix, accT, memT, zT, yT = (
            sb(n, [P, 2, DC, P]) for n in ("hT", "h2T", "vT", "kT", "uT", "aT", "gT", "prefix", "inv_prefix",
                                           "accT", "memT", "zT", "yT"))
        q_t, q_sq, q_n = (sb(n, [P, 2, D]) for n in ("q_t", "q_sq", "q_n"))
        q_ms, q_r = sb("q_ms", [P, 2, HEADS]), sb("q_r", [P, 2, HEADS])
        x_ms, x_r = sb("x_ms", [P, 2]), sb("x_r", [P, 2])
        ones, consts = sb("ones", [P, CHUNK]), sb("consts", [P, 4])
        t_fc = sb("t_fc", [P, 2, 512])
        sT = sb("sT", [P, 2, HC, P])
        f_ps = [ps("f0", [P, 512]), ps("f1", [P, 512])]
        kv_ps, ag_ps, q_ps, t_ps, o_ps, m_ps = (ps(n, [P, 512]) for n in ("kv", "ag", "q", "t", "o", "m"))

        loaded_w, folded, const_ready = sem("loaded_w"), sem("folded"), sem("const_ready")
        x_loaded = [sem("x_loaded0"), sem("x_loaded1")]
        again_loaded = [sem("again_loaded0"), sem("again_loaded1")]
        stored = [sem.kept("stored0"), sem.kept("stored1")]
        h_ready, tx_done, hT_ready = sem("h_ready"), sem("tx_done"), sem("hT_ready")
        q_done, q_copied, qsq_ready, qms_ready, qr_ready, qn_ready, qt_done = (
            sem(n) for n in ("q_done", "q_copied", "qsq_ready", "qms_ready", "qr_ready", "qn_ready", "qt_done"))
        kv_done, kv_ready, ag_done, ag_ready, u_ready = (
            sem(n) for n in ("kv_done", "kv_ready", "ag_done", "ag_ready", "u_ready"))
        scan_step, y_ready, out_done, x1_ready, ms_ready, xr_ready, xs_ready = (
            sem(n) for n in ("scan_step", "y_ready", "out_done", "x1_ready", "ms_ready", "xr_ready", "xs_ready"))
        h2_ready, h2t_done, h2T_ready = sem("h2_ready"), sem("h2t_done"), sem("h2T_ready")
        fc_done, tanh_ready, s_ready, pr_done, xo_ready = (
            sem(n) for n in ("fc_done", "tanh_ready", "s_ready", "pr_done", "xo_ready"))
        half_ready, xr_step, clip_step, qr_step = (sem(n) for n in ("half_ready", "xr_step", "clip_step", "qr_step"))
        z_ready, gated = sem("z_ready"), sem("gated")
        ctx.callback(sem.clear)
        block = ctx.enter_context(nc.Block())

        def loaded(eng, sems, b):
            eng.wait_ge(sems[b.par], (b.n + (2 - b.par)) * 8)

        @block.sync
        def _(sp):
            for dst, key in ((w_in, "w_in"), (w_out, "w_out"), (w_fc, "w_fc"), (w_pr, "w_pr")):
                sp.dma_start(dst[:, :, :], w_dram[key]).then_inc(loaded_w, 16)
            for dst, key in ((norm1, "norm1"), (norm2, "norm2")):
                sp.dma_start(dst[:, :], w_dram[key]).then_inc(loaded_w, 16)

            def step(at):
                b0, b1, b3 = at(0), at(1), at(3)
                if b0:
                    wait(sp, h_ready, b0, 1, -1)
                    sp.dma_start(x_t[:, b0.par, :], x_in[b0.n]).then_inc(x_loaded[b0.par], 16)
                if b1:
                    wait(sp, xs_ready, b1, 1, -1)
                    sp.dma_start(x_again[:, b1.par, :], x_in[b1.n]).then_inc(again_loaded[b1.par], 16)
                if b3:
                    wait(sp, xo_ready, b3, 1, 1)
                    sp.dma_start(x_out[b3.n], x_o[:, b3.par, :]).then_inc(stored[b3.par], 16)
            pipeline(sp, count, 4, step)
            for par in range(2):
                sp.wait_ge(stored[par], 16 * (count // 2))

        @block.tensor
        def _(pe):
            pe.wait_ge(folded, 2)

            def transposes(src, b, done):
                for c in range(DC):
                    last = pe.transpose(t_ps[:, P * c:P * c + P], src[:, b.par, P * c:P * c + P], ident[:, :])
                last.then_inc(done, 1)

            def channels(b, bank, part0, parts, done):
                for m in range(parts * DC):
                    col = part0 * D + P * m
                    for c in range(DC):
                        last = pe.matmul(bank[:, P * m:P * m + P], w_in[:, c, col:col + P],
                                         hT[:, b.par, c, :], start=(c == 0), stop=(c == DC - 1))
                last.then_inc(done, 1)

            def hidden(b, j):
                wait(pe, h2T_ready, b, 1, 1)
                wait(pe, s_ready, b, 2, j - 1)
                for m in range(4):
                    for c in range(DC):
                        last = pe.matmul(f_ps[j][:, P * m:P * m + P],
                                         w_fc[:, c, 512 * j + P * m:512 * j + P * m + P],
                                         h2T[:, b.par, c, :], start=(c == 0), stop=(c == DC - 1))
                last.then_inc(fc_done, 1)

            def project(b, j):
                wait(pe, s_ready, b, 2, j + 1)
                if j == 0:
                    wait(pe, xo_ready, b, 1, 0)
                for c in range(4 * j, 4 * j + 4):
                    last = pe.matmul(m_ps[:, 0:D], sT[:, b.par, c, :], w_pr[:, c, :],
                                     start=(c == 0), stop=(c == HC - 1))
                if j == 1:
                    last.then_inc(pr_done, 1)

            def step(at):
                b0, b1, b2, b3 = at(0), at(1), at(2), at(3)
                if b3:
                    project(b3, 0)
                if b2:
                    wait(pe, h2_ready, b2, 1, 1)
                    wait(pe, z_ready, b2, 1, 1)
                    transposes(h2_n, b2, h2t_done)
                if b3:
                    project(b3, 1)
                if b0:
                    wait(pe, h_ready, b0, 1, 1)
                    if b2:
                        wait(pe, h2T_ready, b2, 1, 1)
                    transposes(h_n, b0, tx_done)
                if b2:
                    hidden(b2, 0)
                if b1:
                    wait(pe, qn_ready, b1, 1, 1)
                    if b0:
                        wait(pe, hT_ready, b0, 1, 1)
                    transposes(q_n, b1, qt_done)
                if b2:
                    hidden(b2, 1)
                if b0:
                    wait(pe, hT_ready, b0, 1, 1)
                    wait(pe, q_copied, b0, 1, 0)
                    for c in range(DC):
                        last = pe.matmul(q_ps[:, 0:D], hT[:, b0.par, c, :], w_in[:, c, 0:D],
                                         start=(c == 0), stop=(c == DC - 1))
                    last.then_inc(q_done, 1)
                    wait(pe, kv_ready, b0, 1, 0)
                    channels(b0, kv_ps, 1, 2, kv_done)
                if b1:
                    wait(pe, y_ready, b1, 1, 1)
                    wait(pe, x1_ready, b1, 1, 0)
                    for c in range(DC):
                        last = pe.matmul(o_ps[:, 0:D], yT[:, b1.par, c, :], w_out[:, c, :],
                                         start=(c == 0), stop=(c == DC - 1))
                    last.then_inc(out_done, 1)
                if b0:
                    wait(pe, ag_ready, b0, 1, 0)
                    channels(b0, ag_ps, 3, 2, ag_done)
            pipeline(pe, count, 4, step)

        @block.scalar
        def _(act):
            def step(at):
                b0, b1, b2 = at(0), at(1), at(2)
                if b2:
                    wait(act, h2t_done, b2, 1, 1)
                    wait(act, fc_done, b2, 2, -2)
                    act.copy(h2T[:, b2.par, :, :], t_ps[:, 0:D].rearrange("p (c t) -> p c t", c=DC))\
                       .then_inc(h2T_ready, 1)
                if b0:
                    wait(act, tx_done, b0, 1, 1)
                    wait(act, ag_done, b0, 1, -1)
                    act.copy(hT[:, b0.par, :, :], t_ps[:, 0:D].rearrange("p (c t) -> p c t", c=DC))\
                       .then_inc(hT_ready, 1)
                if b2:
                    for j in range(2):
                        wait(act, fc_done, b2, 2, j + 1)
                        wait(act, s_ready, b2, 2, j - 1)
                        act.activation(t_fc[:, j, :], f_ps[j][:, :], ACT.Tanh, scale=0.5).then_inc(tanh_ready, 1)
                if b0:
                    wait(act, q_done, b0, 1, 1)
                    wait(act, qn_ready, b0, 1, -1)
                    act.copy(q_t[:, b0.par, :], q_ps[:, 0:D]).then_inc(q_copied, 1)
                    wait(act, kv_done, b0, 1, 1)
                    wait(act, u_ready, b0, 1, -1)
                    wait(act, y_ready, b0, 1, -1)
                    act.activation(kT[:, b0.par, :, :], kv_ps[:, 0:D].rearrange("p (c t) -> p c t", c=DC), ACT.Tanh)
                    act.copy(vT[:, b0.par, :, :], kv_ps[:, D:2 * D].rearrange("p (c t) -> p c t", c=DC))\
                       .then_inc(kv_ready, 1)
                if b1:
                    wait(act, x1_ready, b1, 1, 1)
                    wait(act, xr_ready, b1, 1, -1)
                    act.activation(junk[:, b1.par, :], x_1[:, b1.par, :], ACT.Square, scale=D ** -0.5,
                                   accum_out=x_ms[:, b1.par:b1.par + 1]).then_inc(ms_ready, 1)
                if b0:
                    wait(act, ag_done, b0, 1, 1)
                    wait(act, scan_step, b0, 9, 1 - 18)
                    act.activation(aT[:, b0.par, :, :], ag_ps[:, 0:D].rearrange("p (c t) -> p c t", c=DC),
                                   ACT.Tanh, bias=one_col[:, :], scale=0.5)
                    act.activation(gT[:, b0.par, :, :], ag_ps[:, D:2 * D].rearrange("p (c t) -> p c t", c=DC),
                                   ACT.Tanh, scale=0.5).then_inc(ag_ready, 1)
            one_col = ones[:, 0:1]
            act.wait_ge(const_ready, 1)
            pipeline(act, count, 3, step)

        @block.vector
        def _(dve):
            dve.memset(ones[:, :], 1.0).then_inc(const_ready, 1)
            dve.wait_ge(loaded_w, 16 * 6)
            for c in range(DC):
                dve.tensor_scalar(w_in[:, c, :], w_in[:, c, :], norm1[:, c:c + 1], None, ALU.mult)
                last = dve.tensor_scalar(w_fc[:, c, :], w_fc[:, c, :], norm2[:, c:c + 1], None, ALU.mult)
                last.then_inc(folded, 1)
            dve.wait_ge(folded, 2)
            STEPS = 9

            def step(at):
                b0, b1, b2, b3 = at(0), at(1), at(2), at(3)
                if b0:
                    loaded(dve, x_loaded, b0)
                    wait(dve, tx_done, b0, 1, -1)
                    dve.tensor_scalar(h_n[:, b0.par, :], x_t[:, b0.par, :], mean[:, bass.ds(b0.n, 1)],
                                      scale[:, bass.ds(b0.n, 1)], ALU.subtract, ALU.mult)
                    dve.tensor_scalar(x_ln[:, b0.par, :], x_t[:, b0.par, :], mean[:, bass.ds(b0.n, 1)],
                                      rstd[:, bass.ds(b0.n, 1)], ALU.subtract, ALU.mult).then_inc(h_ready, 1)
                if b1:
                    wait(dve, ag_ready, b1, 1, 1)
                    dve.tensor_scalar(aT[:, b1.par, :, :], aT[:, b1.par, :, :], 0.5, 0.5, ALU.mult, ALU.add)\
                       .then_inc(clip_step, 1)
                    wait(dve, clip_step, b1, 2, 1)
                    dve.tensor_scalar(aT[:, b1.par, :, :], aT[:, b1.par, :, :], 0.9995, 0.6, ALU.min, ALU.max)\
                       .then_inc(clip_step, 1)
                    wait(dve, clip_step, b1, 2, 2)
                    for c in range(DC):
                        for s in range(P // CHUNK):
                            part = slice(CHUNK * s, CHUNK * s + CHUNK)
                            last = dve.tensor_tensor_scan(prefix[:, b1.par, c, part], aT[:, b1.par, c, part],
                                                          ones[:, :], 1.0, ALU.mult, ALU.mult)
                    last.then_inc(scan_step, 1)
                    wait(dve, scan_step, b1, STEPS, 1)
                    dve.tensor_scalar(inv_prefix[:, b1.par, :, :], prefix[:, b1.par, :, :], 1e-6, None, ALU.max)\
                       .then_inc(scan_step, 1)
                    wait(dve, scan_step, b1, STEPS, 2)
                    dve.reciprocal(inv_prefix[:, b1.par, :, :], inv_prefix[:, b1.par, :, :]).then_inc(scan_step, 1)
                    wait(dve, qr_ready, b1, 1, 1)
                    wait(dve, qt_done, b1, 1, -1)
                    dve.tensor_tensor(q_n[:, b1.par, :].rearrange("p (h d) -> p h d", h=HEADS),
                                      q_t[:, b1.par, :].rearrange("p (h d) -> p h d", h=HEADS),
                                      q_r[:, b1.par, :].unsqueeze(2).to_broadcast([P, HEADS, HD]),
                                      ALU.mult).then_inc(qn_ready, 1)
                    wait(dve, scan_step, b1, STEPS, 3)
                    wait(dve, u_ready, b1, 1, 1)
                    dve.tensor_tensor(inv_prefix[:, b1.par, :, :], inv_prefix[:, b1.par, :, :],
                                      uT[:, b1.par, :, :], ALU.mult).then_inc(scan_step, 1)
                    wait(dve, scan_step, b1, STEPS, 4)
                if b3:
                    wait(dve, pr_done, b3, 1, 1)
                    wait(dve, xs_ready, b3, 1, 1)
                    if not b3.known() or b3.n >= 2:
                        dve.wait_ge(stored[b3.par], (b3.n - b3.par) * 8)
                    dve.scalar_tensor_tensor(out=x_o[:, b3.par, :], in0=m_ps[:, 0:D], scalar=0.5 * RES,
                                             in1=x_s[:, b3.par, :], op0=ALU.mult, op1=ALU.add)\
                       .then_inc(xo_ready, 1)
                    wait(dve, xo_ready, b3, 1, 1)
                    dve.bn_stats(stats[:, b3.n, :], x_o[:, b3.par, :])
                if b1:
                    for s in range(P // CHUNK):
                        part = slice(CHUNK * s, CHUNK * s + CHUNK)
                        for c in range(DC):
                            first = 0.0 if s == 0 else memT[:, b1.par, c, CHUNK * s - 1:CHUNK * s]
                            last = dve.tensor_tensor_scan(accT[:, b1.par, c, part], ones[:, :],
                                                          inv_prefix[:, b1.par, c, part], first,
                                                          ALU.mult, ALU.add)
                        last.then_inc(scan_step, 1)
                        wait(dve, scan_step, b1, STEPS, 5 + 2 * s)
                        dve.tensor_tensor(memT[:, b1.par, :, part], accT[:, b1.par, :, part],
                                          prefix[:, b1.par, :, part], ALU.mult).then_inc(scan_step, 1)
                        wait(dve, scan_step, b1, STEPS, 6 + 2 * s)
                    wait(dve, qt_done, b1, 1, 1)
                    dve.tensor_tensor(zT[:, b1.par, :, :], t_ps[:, 0:D].rearrange("p (c t) -> p c t", c=DC),
                                      memT[:, b1.par, :, :], ALU.mult).then_inc(z_ready, 1)
                    wait(dve, z_ready, b1, 1, 1)
                    dve.tensor_tensor(zT[:, b1.par, :, :], zT[:, b1.par, :, :], vT[:, b1.par, :, :],
                                      ALU.subtract).then_inc(scan_step, 1)
                    wait(dve, scan_step, b1, STEPS, 9)
                    wait(dve, out_done, b1, 1, -1)
                    dve.scalar_tensor_tensor(out=zT[:, b1.par, :, :], in0=gT[:, b1.par, :, :], scalar=1.0,
                                             in1=zT[:, b1.par, :, :], op0=ALU.add, op1=ALU.mult)\
                       .then_inc(gated, 1)
                    wait(dve, gated, b1, 1, 1)
                    dve.scalar_tensor_tensor(out=yT[:, b1.par, :, :], in0=zT[:, b1.par, :, :], scalar=0.5,
                                             in1=vT[:, b1.par, :, :], op0=ALU.mult, op1=ALU.add)\
                       .then_inc(y_ready, 1)
                if b2:
                    for j in range(2):
                        wait(dve, tanh_ready, b2, 2, j + 1)
                        wait(dve, pr_done, b2, 1, -1)
                        dve.scalar_tensor_tensor(
                            out=sT[:, b2.par, 4 * j:4 * j + 4, :].rearrange("p c t -> p (c t)"),
                            in0=t_fc[:, j, :], scalar=1.0, in1=f_ps[j][:, :],
                            op0=ALU.add, op1=ALU.mult).then_inc(s_ready, 1)
                if b1:
                    wait(dve, out_done, b1, 1, 1)
                    wait(dve, xs_ready, b1, 1, -1)
                    wait(dve, ms_ready, b1, 1, -1)
                    dve.scalar_tensor_tensor(out=x_1[:, b1.par, :], in0=o_ps[:, 0:D], scalar=RES,
                                             in1=x_ln[:, b1.par, :], op0=ALU.mult, op1=ALU.add)\
                       .then_inc(x1_ready, 1)
                if b0:
                    wait(dve, q_copied, b0, 1, 1)
                    dve.tensor_tensor(q_sq[:, b0.par, :], q_t[:, b0.par, :], q_t[:, b0.par, :], ALU.mult)\
                       .then_inc(qsq_ready, 1)
                    wait(dve, qsq_ready, b0, 1, 1)
                    wait(dve, qr_ready, b0, 1, -1)
                    dve.tensor_reduce(q_ms[:, b0.par, :], q_sq[:, b0.par, :].rearrange("p (h d) -> p h d", h=HEADS),
                                      AX.X, ALU.add).then_inc(qms_ready, 1)
                if b1:
                    wait(dve, xr_ready, b1, 1, 1)
                    wait(dve, h2t_done, b1, 1, -1)
                    dve.tensor_scalar(h2_n[:, b1.par, :], x_1[:, b1.par, :], x_r[:, b1.par:b1.par + 1],
                                      None, ALU.mult).then_inc(h2_ready, 1)
            pipeline(dve, count, 4, step)

        @block.gpsimd
        def _(pool):
            for i, value in enumerate((-0.5, RMS_EPS, 1.0 / HD, Q_EPS)):
                pool.memset(consts[:, i:i + 1], value).then_inc(half_ready, 1)
            pool.wait_ge(half_ready, 4)

            def step(at):
                b0, b1, b2 = at(0), at(1), at(2)
                if b0:
                    wait(pool, kv_ready, b0, 1, 1)
                    wait(pool, scan_step, b0, 9, 4 - 18)
                    pool.tensor_tensor(uT[:, b0.par, :, :], kT[:, b0.par, :, :], vT[:, b0.par, :, :],
                                       ALU.mult).then_inc(u_ready, 1)
                if b1:
                    wait(pool, ms_ready, b1, 1, 1)
                    wait(pool, h2_ready, b1, 1, -1)
                    pool.tensor_tensor(x_r[:, b1.par:b1.par + 1], x_ms[:, b1.par:b1.par + 1], consts[:, 1:2],
                                       ALU.add).then_inc(xr_step, 1)
                    wait(pool, xr_step, b1, 1, 1)
                    pool.tensor_tensor(x_r[:, b1.par:b1.par + 1], x_r[:, b1.par:b1.par + 1], consts[:, 0:1],
                                       ALU.pow).then_inc(xr_ready, 1)
                    wait(pool, x1_ready, b1, 1, 1)
                    loaded(pool, again_loaded, b1)
                    wait(pool, xo_ready, b1, 1, -1)
                    pool.tensor_tensor(x_s[:, b1.par, :], x_1[:, b1.par, :], x_again[:, b1.par, :], ALU.add)\
                        .then_inc(xs_ready, 1)
                if b0:
                    wait(pool, qms_ready, b0, 1, 1)
                    wait(pool, qn_ready, b0, 1, -1)
                    pool.tensor_tensor(q_r[:, b0.par, :], q_ms[:, b0.par, :],
                                       consts[:, 2:3].to_broadcast([P, HEADS]), ALU.mult).then_inc(qr_step, 1)
                    wait(pool, qr_step, b0, 2, 1)
                    pool.tensor_tensor(q_r[:, b0.par, :], q_r[:, b0.par, :],
                                       consts[:, 3:4].to_broadcast([P, HEADS]), ALU.add).then_inc(qr_step, 1)
                    wait(pool, qr_step, b0, 2, 2)
                    pool.tensor_tensor(q_r[:, b0.par, :], q_r[:, b0.par, :],
                                       consts[:, 0:1].to_broadcast([P, HEADS]), ALU.pow)\
                        .then_inc(qr_ready, 1)
            pipeline(pool, count, 3, step)


def cross_values(nc, x_in, x_out, ctx_in, stats, mean, rstd, ident, w_dram, count=NB):
    name = "xv"
    with ExitStack() as ctx:
        def sb(n, shape, dt=F32):
            return ctx.enter_context(nc.sbuf_tensor(f"{name}_{n}", shape, dt))

        def ps(n):
            return ctx.enter_context(nc.psum_tensor(f"{name}_ps_{n}", [P, 512], F32))

        sem = Semaphores(nc, ctx, name)

        w_vk, w_lk, w_vv, w_lv = (sb(n, [P, DC, D]) for n in ("w_vk", "w_lk", "w_vv", "w_lv"))
        b_vk, b_lk = sb("b_vk", [P, DC]), sb("b_lk", [P, DC])
        b_vv, b_lv = sb("b_vv", [P, D]), sb("b_lv", [P, D])
        x_t, c_t, x_r, xn, vv, lv, x_o = (sb(n, [P, 2, D]) for n in ("x_t", "c_t", "x_r", "xn", "vv", "lv", "x_o"))
        srcT = sb("srcT", [P, 2, 2 * DC, P])
        vkT, lkT = sb("vkT", [P, 2, DC, P]), sb("lkT", [P, 2, DC, P])
        attn, attnT = sb("attn", [P, 2, P]), sb("attnT", [P, 2, P])
        neg_max, total, inv = sb("neg_max", [P, 2]), sb("total", [P, 2]), sb("inv", [P, 2])
        t_ps, vk_ps, lk_ps, vv_ps, s_ps, at_ps, l_ps, o_ps = (ps(n) for n in ("t", "vk", "lk", "vv", "s", "at", "l", "o"))
        loaded_w = sem("loaded_w")
        x_loaded, c_loaded, r_loaded = ([sem(f"{n}{i}") for i in range(2)] for n in ("x_loaded", "c_loaded", "r_loaded"))
        stored = [sem.kept("stored0"), sem.kept("stored1")]
        xn_ready, t_done, srcT_ready, vk_done, vk_ready, lk_done, lk_ready, vv_done, vv_ready = (
            sem(n) for n in ("xn_ready", "t_done", "srcT_ready", "vk_done", "vk_ready", "lk_done", "lk_ready",
                             "vv_done", "vv_ready"))
        s_done, max_ready, exp_ready, inv_ready, attn_ready, at_done, attnT_ready = (
            sem(n) for n in ("s_done", "max_ready", "exp_ready", "inv_ready", "attn_ready", "at_done", "attnT_ready"))
        l_done, lv_ready, out_done, xo_ready = (sem(n) for n in ("l_done", "lv_ready", "out_done", "xo_ready"))
        ctx.callback(sem.clear)
        block = ctx.enter_context(nc.Block())

        def loaded(eng, sems, b):
            eng.wait_ge(sems[b.par], (b.n + (2 - b.par)) * 8)

        @block.sync
        def _(sp):
            for dst, key in ((w_vk, "w_vk"), (w_lk, "w_lk"), (w_vv, "w_vv"), (w_lv, "w_lv")):
                sp.dma_start(dst[:, :, :], w_dram[key]).then_inc(loaded_w, 16)
            for dst, key in ((b_vk, "b_vk"), (b_lk, "b_lk"), (b_vv, "b_vv"), (b_lv, "b_lv")):
                sp.dma_start(dst[:, :], w_dram[key]).then_inc(loaded_w, 16)

            def step(at):
                b = at(0)
                if b:
                    wait(sp, xn_ready, b, 1, -1)
                    sp.dma_start(x_t[:, b.par, :], x_in[b.n]).then_inc(x_loaded[b.par], 16)
                    wait(sp, t_done, b, 1, -1)
                    sp.dma_start(c_t[:, b.par, :], ctx_in[b.n]).then_inc(c_loaded[b.par], 16)
                    wait(sp, xo_ready, b, 1, -1)
                    sp.dma_start(x_r[:, b.par, :], x_in[b.n]).then_inc(r_loaded[b.par], 16)
            pipeline(sp, count, 1, step)
            for par in range(2):
                sp.wait_ge(stored[par], 16 * (count // 2))

        @block.tensor
        def _(pe):
            pe.wait_ge(loaded_w, 16 * 8)

            def channels(b, bank, w, chunk0, done):
                for m in range(DC):
                    for c in range(DC):
                        last = pe.matmul(bank[:, P * m:P * m + P], w[:, c, P * m:P * m + P],
                                         srcT[:, b.par, chunk0 + c, :], start=(c == 0), stop=(c == DC - 1))
                last.then_inc(done, 1)

            def step(at):
                b0, b1, b2 = at(0), at(1), at(2)
                if b2:
                    wait(pe, lv_ready, b2, 1, 1)
                    wait(pe, attnT_ready, b2, 1, 1)
                    wait(pe, xo_ready, b2, 1, 0)
                    pe.matmul(o_ps[:, 0:D], attnT[:, b2.par, :], lv[:, b2.par, :], start=True, stop=True)\
                      .then_inc(out_done, 1)
                if b1:
                    wait(pe, vk_ready, b1, 1, 1)
                    wait(pe, lk_ready, b1, 1, 1)
                    wait(pe, exp_ready, b1, 1, 0)
                    for c in range(DC):
                        last = pe.matmul(s_ps[:, 0:P], vkT[:, b1.par, c, :], lkT[:, b1.par, c, :],
                                         start=(c == 0), stop=(c == DC - 1))
                    last.then_inc(s_done, 1)
                if b0:
                    wait(pe, xn_ready, b0, 1, 1)
                    loaded(pe, c_loaded, b0)
                    wait(pe, srcT_ready, b0, 1, 0)
                    for k in range(2 * DC):
                        src = xn if k < DC else c_t
                        last = pe.transpose(t_ps[:, P * k:P * k + P],
                                            src[:, b0.par, P * (k % DC):P * (k % DC) + P], ident[:, :])
                    last.then_inc(t_done, 1)
                if b1:
                    wait(pe, lv_ready, b1, 1, 0)
                    for c in range(DC):
                        pe.matmul(l_ps[:, 0:D], srcT[:, b1.par, DC + c, :], w_lv[:, c, :], start=(c == 0), stop=False)
                if b0:
                    wait(pe, srcT_ready, b0, 1, 1)
                    wait(pe, vk_ready, b0, 1, 0)
                    channels(b0, vk_ps, w_vk, 0, vk_done)
                if b1:
                    wait(pe, attn_ready, b1, 1, 1)
                    wait(pe, attnT_ready, b1, 1, 0)
                    pe.transpose(at_ps[:, 0:P], attn[:, b1.par, :], ident[:, :]).then_inc(at_done, 1)
                    wait(pe, vv_ready, b1, 1, 1)
                    pe.matmul(l_ps[:, 0:D], attn[:, b1.par, :], vv[:, b1.par, :], start=False, stop=True)\
                      .then_inc(l_done, 1)
                if b0:
                    wait(pe, lk_ready, b0, 1, 0)
                    channels(b0, lk_ps, w_lk, DC, lk_done)
                    wait(pe, vv_ready, b0, 1, 0)
                    for c in range(DC):
                        last = pe.matmul(vv_ps[:, 0:D], srcT[:, b0.par, c, :], w_vv[:, c, :],
                                         start=(c == 0), stop=(c == DC - 1))
                    last.then_inc(vv_done, 1)
            pipeline(pe, count, 3, step)

        @block.scalar
        def _(act):
            def step(at):
                b0, b1 = at(0), at(1)
                if b1:
                    wait(act, max_ready, b1, 1, 1)
                    wait(act, at_done, b1, 1, -1)
                    wait(act, l_done, b1, 1, -1)
                    act.activation(attn[:, b1.par, :], s_ps[:, 0:P], ACT.Exp, bias=neg_max[:, b1.par:b1.par + 1],
                                   scale=D ** -0.5, accum_out=total[:, b1.par:b1.par + 1]).then_inc(exp_ready, 1)
                if b0:
                    wait(act, t_done, b0, 1, 1)
                    wait(act, vv_done, b0, 1, -1)
                    wait(act, l_done, b0, 1, -1)
                    act.copy(srcT[:, b0.par, :, :], t_ps[:, :].rearrange("p (c t) -> p c t", c=2 * DC))\
                       .then_inc(srcT_ready, 1)
                if b1:
                    wait(act, at_done, b1, 1, 1)
                    wait(act, out_done, b1, 1, -1)
                    act.copy(attnT[:, b1.par, :], at_ps[:, 0:P]).then_inc(attnT_ready, 1)
            pipeline(act, count, 2, step)

        @block.vector
        def _(dve):
            dve.wait_ge(loaded_w, 16 * 8)

            def step(at):
                b0, b1, b2 = at(0), at(1), at(2)
                if b0:
                    loaded(dve, x_loaded, b0)
                    wait(dve, t_done, b0, 1, -1)
                    dve.tensor_scalar(xn[:, b0.par, :], x_t[:, b0.par, :], mean[:, bass.ds(b0.n, 1)],
                                      rstd[:, bass.ds(b0.n, 1)], ALU.subtract, ALU.mult).then_inc(xn_ready, 1)
                if b1:
                    wait(dve, s_done, b1, 1, 1)
                    wait(dve, exp_ready, b1, 1, -1)
                    dve.tensor_reduce(neg_max[:, b1.par:b1.par + 1], s_ps[:, 0:P], AX.X, ALU.max, negate=True)\
                       .then_inc(inv_ready, 1)
                    wait(dve, inv_ready, b1, 2, 1)
                    dve.tensor_scalar(neg_max[:, b1.par:b1.par + 1], neg_max[:, b1.par:b1.par + 1], D ** -0.5, None,
                                      ALU.mult).then_inc(max_ready, 1)
                if b2:
                    wait(dve, out_done, b2, 1, 1)
                    loaded(dve, r_loaded, b2)
                    if not b2.known() or b2.n >= 2:
                        dve.wait_ge(stored[b2.par], (b2.n - b2.par) * 8)
                    dve.tensor_tensor(x_o[:, b2.par, :], o_ps[:, 0:D], x_r[:, b2.par, :], ALU.add)\
                       .then_inc(xo_ready, 1)
                    wait(dve, xo_ready, b2, 1, 1)
                    dve.bn_stats(stats[:, b2.n, :], x_o[:, b2.par, :])
                if b1:
                    wait(dve, exp_ready, b1, 1, 1)
                    dve.reciprocal(inv[:, b1.par:b1.par + 1], total[:, b1.par:b1.par + 1]).then_inc(inv_ready, 1)
                    wait(dve, inv_ready, b1, 2, 2)
                    dve.tensor_scalar(attn[:, b1.par, :], attn[:, b1.par, :], inv[:, b1.par:b1.par + 1], None,
                                      ALU.mult).then_inc(attn_ready, 1)
                if b0:
                    wait(dve, vk_done, b0, 1, 1)
                    wait(dve, s_done, b0, 1, -1)
                    dve.tensor_tensor(vkT[:, b0.par, :, :], vk_ps[:, 0:D].rearrange("p (c t) -> p c t", c=DC),
                                      b_vk[:, :].unsqueeze(2).to_broadcast([P, DC, P]), ALU.add)\
                       .then_inc(vk_ready, 1)
                if b1:
                    wait(dve, l_done, b1, 1, 1)
                    wait(dve, out_done, b1, 1, -1)
                    dve.tensor_tensor(lv[:, b1.par, :], l_ps[:, 0:D], b_lv[:, :], ALU.add).then_inc(lv_ready, 1)
                if b0:
                    wait(dve, lk_done, b0, 1, 1)
                    dve.tensor_tensor(lkT[:, b0.par, :, :], lk_ps[:, 0:D].rearrange("p (c t) -> p c t", c=DC),
                                      b_lk[:, :].unsqueeze(2).to_broadcast([P, DC, P]), ALU.add)\
                       .then_inc(lk_ready, 1)
                    wait(dve, vv_done, b0, 1, 1)
                    wait(dve, l_done, b0, 1, -1)
                    dve.tensor_tensor(vv[:, b0.par, :], vv_ps[:, 0:D], b_vv[:, :], ALU.add).then_inc(vv_ready, 1)
            pipeline(dve, count, 3, step)

        @block.gpsimd
        def _(pool):
            def step(at):
                b2 = at(2)
                if b2:
                    wait(pool, xo_ready, b2, 1, 1)
                    pool.dma_start(x_out[b2.n], x_o[:, b2.par, :]).then_inc(stored[b2.par], 16)
            pipeline(pool, count, 3, step)


MAGIC = 12582912.0
TAPS = 3


def quantised_ffn(nc, x_in, x_out, mean, rstd, ident, ident_b, w_dram, count=NB):
    name = "qf"
    with ExitStack() as ctx:
        def sb(n, shape, dt=F32):
            return ctx.enter_context(nc.sbuf_tensor(f"{name}_{n}", shape, dt))

        def ps(n, shape, dt=F32):
            return ctx.enter_context(nc.psum_tensor(f"{name}_ps_{n}", shape, dt))

        sem = Semaphores(nc, ctx, name)

        w1, w2 = sb("w1", [P, DC * HID]), sb("w2", [P, HC * D])
        w1_q, w2_q = sb("w1_q", [P, DC, HID], BF16), sb("w2_q", [P, HC, D], BF16)
        conv_w = sb("conv_w", [P, TAPS, HC])
        diag = sb("diag", [P, TAPS, HC, P])
        bias = sb("bias", [1, HID])
        bias_p = sb("bias_p", [1, 3, HID], BF16)
        bias3 = sb("bias3", [3, HID], BF16)
        ones3 = sb("ones3", [3, P], BF16)
        ones = sb("ones", [P, P])
        w_sum, w_mean, w_inv, factor = sb("w_sum", [P, 2]), sb("w_mean", [P, 2]), sb("w_inv", [P, 2]), sb("factor", [P, 2])
        x_t, x_r, xn, rounded, x_o = (sb(n, [P, 2, D]) for n in ("x_t", "x_r", "xn", "rounded", "x_o"))
        q1 = sb("q1", [P, 2, D])
        q1T = sb("q1T", [P, 2, DC, P], BF16)
        peak1, step1, inv1, fac1 = (sb(n, [P, 2]) for n in ("peak1", "step1", "inv1", "fac1"))
        peak2, step2, inv2, fac2 = (sb(n, [P, 2]) for n in ("peak2", "step2", "inv2", "fac2"))
        fac_row = sb("fac_row", [P, 2, P])
        h_pad = sb("h_pad", [P, 2, HC, P + 2])
        t_h = sb("t_h", [P, 2, 512])
        sT = sb("sT", [P, HC, P])
        rounded2 = sb("rounded2", [P, HID])
        q2 = sb("q2", [P, 2, HID], BF16)
        q2T = sb("q2T", [P, HC, P], BF16)
        h_ps, z_ps, st_ps = ps("h", [P, 2, 512]), ps("z", [P, 2, 512]), ps("st", [P, 2, 512])
        q2_ps = ps("q2", [P, HC, P], BF16)
        m_ps = ps("m", [P, 512])
        f_ps, q1_ps, o_ps = m_ps[:, 0:P], m_ps[:, P:P + D], m_ps[:, 0:D]

        loaded_w, w_step, sums_ready, sum_done, weights_ready, bias_ready, bias_stacked, pads_ready = (
            sem(n) for n in ("loaded_w", "w_step", "sums_ready", "sum_done", "weights_ready", "bias_ready",
                             "bias_stacked", "pads_ready"))
        x_loaded, r_loaded = ([sem(f"{n}{i}") for i in range(2)] for n in ("x_loaded", "r_loaded"))
        stored = [sem.kept("stored0"), sem.kept("stored1")]
        small, xn_ready, round1_ready, q1_ready, q1t_done, q1T_ready, fac1_ready, f_ready = (
            sem(n) for n in ("small", "xn_ready", "round1_ready", "q1_ready", "q1t_done", "q1T_ready", "fac1_ready",
                             "f_ready"))
        h_done, h_ready, z_done, tanh_ready, s_ready, st_done, small2, round2_ready, q2_ready = (
            sem(n) for n in ("h_done", "h_ready", "z_done", "tanh_ready", "s_ready", "st_done", "small2",
                             "round2_ready", "q2_ready"))
        scaled1, scaled2 = sem("scaled1"), sem("scaled2")
        q2t_done, q2T_ready, o_done, xo_ready = (sem(n) for n in ("q2t_done", "q2T_ready", "o_done", "xo_ready"))
        block = ctx.enter_context(nc.Block())

        def loaded(eng, sems, b):
            eng.wait_ge(sems[b.par], (b.n + (2 - b.par)) * 8)

        @block.sync
        def _(sp):
            sp.dma_start(w1[:, :], w_dram["w1"]).then_inc(loaded_w, 16)
            sp.dma_start(w2[:, :], w_dram["w2"]).then_inc(loaded_w, 16)
            sp.dma_start(conv_w[:, :, :], w_dram["conv_w"]).then_inc(loaded_w, 16)
            sp.dma_start(bias[:, :], w_dram["conv_b"]).then_inc(loaded_w, 16)
            sp.wait_ge(bias_ready, 1)
            for part in range(3):
                sp.dma_start(bias3[part:part + 1, :], bias_p[:, part, :]).then_inc(bias_stacked, 16)

            def step(at):
                b0, b2, b3 = at(0), at(2), at(3)
                if b0:
                    wait(sp, xn_ready, b0, 1, -1)
                    sp.dma_start(x_t[:, b0.par, :], x_in[b0.n]).then_inc(x_loaded[b0.par], 16)
                if b2:
                    wait(sp, xo_ready, b2, 1, -1)
                    sp.dma_start(x_r[:, b2.par, :], x_in[b2.n]).then_inc(r_loaded[b2.par], 16)
                if b3:
                    wait(sp, xo_ready, b3, 1, 1)
                    sp.dma_start(x_out[b3.n], x_o[:, b3.par, :]).then_inc(stored[b3.par], 16)
            pipeline(sp, count, 4, step)
            for par in range(2):
                sp.wait_ge(stored[par], 16 * (count // 2))

        @block.tensor
        def _(pe):
            pe.wait_ge(sums_ready, 1)
            pe.matmul(m_ps[:, 0:2], ones[:, :], w_sum[:, :], start=True, stop=True).then_inc(sum_done, 1)
            pe.wait_ge(weights_ready, 1)
            pe.wait_ge(bias_stacked, 48)

            def convolve(b, j):
                wait(pe, h_ready, b, 2, j + 1)
                wait(pe, s_ready, b, 2, j - 1)
                for c in range(4 * j, 4 * j + 4):
                    out = z_ps[:, j, P * (c % 4):P * (c % 4) + P]
                    for tap in range(TAPS):
                        pe.matmul(out, diag[:, tap, c, :], h_pad[:, b.par, c, tap:tap + P],
                                  start=(tap == 0), stop=False)
                    last = pe.matmul(out, bias3[:, P * c:P * c + P], ones3[:, :], start=False, stop=True)
                last.then_inc(z_done, 1)

            def silu_transpose(b, j):
                wait(pe, s_ready, b, 2, j + 1)
                if j == 0:
                    wait(pe, round2_ready, b, 1, 0)
                for c in range(4 * j, 4 * j + 4):
                    last = pe.transpose(st_ps[:, j, P * (c % 4):P * (c % 4) + P], sT[:, c, :], ident[:, :])
                if j == 1:
                    last.then_inc(st_done, 1)

            def step(at):
                b0, b1, b2 = at(0), at(1), at(2)
                if b1:
                    convolve(b1, 0)
                    convolve(b1, 1)
                if b2:
                    wait(pe, q2_ready, b2, 1, 1)
                    wait(pe, q2T_ready, b2, 1, 0)
                    for c in range(HC):
                        last = pe.transpose(q2_ps[:, c, :], q2[:, b2.par, P * c:P * c + P], ident_b[:, :])
                    last.then_inc(q2t_done, 1)
                if b1:
                    silu_transpose(b1, 0)
                if b0:
                    wait(pe, q1_ready, b0, 1, 1)
                    wait(pe, fac1_ready, b0, 1, 1)
                    wait(pe, xo_ready, b0, 1, -2)
                    for c in range(DC):
                        pe.transpose(q1_ps[:, P * c:P * c + P], q1[:, b0.par, P * c:P * c + P], ident[:, :])
                    pe.transpose(f_ps, fac1[:, b0.par:b0.par + 1].to_broadcast([P, P]), ident[:, :])\
                      .then_inc(q1t_done, 1)
                if b1:
                    silu_transpose(b1, 1)
                if b0:
                    wait(pe, q1T_ready, b0, 1, 1)
                    for j in range(2):
                        wait(pe, h_ready, b0, 2, j - 1)
                        for m in range(4 * j, 4 * j + 4):
                            for c in range(DC):
                                last = pe.matmul(h_ps[:, j, P * (m % 4):P * (m % 4) + P], w1_q[:, c, P * m:P * m + P],
                                                 q1T[:, b0.par, c, :], start=(c == 0), stop=(c == DC - 1))
                        last.then_inc(h_done, 1)
                if b2:
                    wait(pe, q2T_ready, b2, 1, 1)
                    wait(pe, xo_ready, b2, 1, 0)
                    if b0:
                        wait(pe, f_ready, b0, 1, 1)
                    for c in range(HC):
                        last = pe.matmul(o_ps, q2T[:, c, :], w2_q[:, c, :], start=(c == 0), stop=(c == HC - 1))
                    last.then_inc(o_done, 1)
            pipeline(pe, count, 3, step)

        @block.scalar
        def _(act):
            def silu_tanh(b, j):
                wait(act, z_done, b, 2, j + 1)
                wait(act, s_ready, b, 2, j - 1)
                act.activation(t_h[:, j, :], z_ps[:, j, :], ACT.Tanh, scale=0.5).then_inc(tanh_ready, 1)

            def step(at):
                b0, b1, b2 = at(0), at(1), at(2)
                if b1:
                    silu_tanh(b1, 0)
                if b2:
                    wait(act, round2_ready, b2, 1, 1)
                    wait(act, q2t_done, b2, 1, -1)
                    act.activation(q2[:, b2.par, :], rounded2[:, :], ACT.Copy, bias=-MAGIC, scale=1.0)\
                       .then_inc(q2_ready, 1)
                if b1:
                    silu_tanh(b1, 1)
                if b0:
                    wait(act, round1_ready, b0, 1, 1)
                    wait(act, q1t_done, b0, 1, -1)
                    act.activation(q1[:, b0.par, :], rounded[:, b0.par, :], ACT.Copy, bias=-MAGIC, scale=1.0)\
                       .then_inc(q1_ready, 1)
                    wait(act, q1t_done, b0, 1, 1)
                    wait(act, h_done, b0, 2, -2)
                    act.copy(q1T[:, b0.par, :, :], q1_ps.rearrange("p (c t) -> p c t", c=DC)).then_inc(q1T_ready, 1)
                    wait(act, h_ready, b0, 2, -2)
                    act.copy(fac_row[:, b0.par, :], f_ps).then_inc(f_ready, 1)
                if b2:
                    wait(act, q2t_done, b2, 1, 1)
                    wait(act, o_done, b2, 1, 0)
                    act.copy(q2T[:, :, :], q2_ps[:, :, :]).then_inc(q2T_ready, 1)
            pipeline(act, count, 3, step)

        @block.vector
        def _(dve):
            done = [0]

            def link(instruction):
                done[0] += 1
                instruction.then_inc(w_step, 1)
                dve.wait_ge(w_step, done[0])

            link(dve.memset(ones[:, :], 1.0))
            link(dve.memset(ones3[:, :], 1.0))
            link(dve.memset(h_pad[:, :, :, :], 0.0))
            dve.wait_ge(loaded_w, 16 * 4)
            for part in range(3):
                link(dve.tensor_copy(bias_p[:, part, :], bias[:, :]))
                if part < 2:
                    link(dve.tensor_tensor(bias[:, :], bias[:, :], bias_p[:, part, :], ALU.subtract))
            dve.sem_inc(bias_ready, 1)
            link(dve.tensor_tensor(diag[:, :, :, :].rearrange("p a c t -> p (a c) t"),
                                   ident[:, :].unsqueeze(1).to_broadcast([P, TAPS * HC, P]),
                                   conv_w[:, :, :].rearrange("p a c -> p (a c)").unsqueeze(2).to_broadcast([P, TAPS * HC, P]),
                                   ALU.mult))
            link(dve.tensor_reduce(w_sum[:, 0:1], w1[:, :], AX.X, ALU.add, apply_absolute_value=True))
            link(dve.tensor_reduce(w_sum[:, 1:2], w2[:, :], AX.X, ALU.add, apply_absolute_value=True))
            dve.sem_inc(sums_ready, 1)
            dve.wait_ge(sum_done, 1)
            link(dve.tensor_scalar(w_mean[:, :], m_ps[:, 0:2], 1.0 / (D * HID), 1e-5, ALU.mult, ALU.max))
            link(dve.reciprocal(w_inv[:, :], w_mean[:, :]))
            for i, (w, w_q) in enumerate(((w1, w1_q), (w2, w2_q))):
                link(dve.tensor_scalar(w[:, :], w[:, :], w_inv[:, i:i + 1], None, ALU.mult))
                link(dve.tensor_scalar(w[:, :], w[:, :], MAGIC, MAGIC, ALU.add, ALU.subtract))
                link(dve.tensor_scalar(w_q[:, :, :].rearrange("p a b -> p (a b)"), w[:, :], 1.0, -1.0, ALU.min, ALU.max))
            link(dve.tensor_copy(factor[:, 0:1], w_mean[:, 0:1]))
            link(dve.tensor_scalar(factor[:, 1:2], w_mean[:, 1:2], 0.5, None, ALU.mult))
            dve.sem_inc(weights_ready, 1)

            def scales(src, par, floor, peak, stp, inv, fac, factor_col, sem_, b):
                dve.tensor_reduce(peak[:, par:par + 1], src, AX.X if len(src.shape) == 2 else AX.XY, ALU.max,
                                  apply_absolute_value=True).then_inc(sem_, 1)
                wait(dve, sem_, b, 3, 1)
                dve.tensor_scalar(stp[:, par:par + 1], peak[:, par:par + 1], floor, 1.0 / 127.0, ALU.max, ALU.mult)\
                   .then_inc(sem_, 1)
                wait(dve, sem_, b, 3, 2)
                dve.reciprocal(inv[:, par:par + 1], stp[:, par:par + 1]).then_inc(sem_, 1)
                return dve.tensor_scalar(fac[:, par:par + 1], stp[:, par:par + 1], factor[:, factor_col:factor_col + 1],
                                         None, ALU.mult)

            def silu(b, j):
                wait(dve, tanh_ready, b, 2, j + 1)
                wait(dve, st_done, b, 1, 0)
                dve.scalar_tensor_tensor(
                    out=sT[:, 4 * j:4 * j + 4, :].rearrange("p c t -> p (c t)"), in0=t_h[:, j, :],
                    scalar=1.0, in1=z_ps[:, j, :], op0=ALU.add, op1=ALU.mult).then_inc(s_ready, 1)

            def step(at):
                b0, b1, b2, b3 = at(0), at(1), at(2), at(3)
                if b1:
                    wait(dve, f_ready, b1, 1, 1)
                    wait(dve, z_done, b1, 2, -2)
                    for j in range(2):
                        wait(dve, h_done, b1, 2, j + 1)
                        dve.tensor_tensor(h_pad[:, b1.par, 4 * j:4 * j + 4, 1:P + 1],
                                          h_ps[:, j, :].rearrange("p (c t) -> p c t", c=4),
                                          fac_row[:, b1.par, :].unsqueeze(1).to_broadcast([P, 4, P]),
                                          ALU.mult).then_inc(h_ready, 1)
                if b2:
                    wait(dve, st_done, b2, 1, 1)
                    scales(st_ps[:, :, :], b2.par, 2e-5, peak2, step2, inv2, fac2, 1, small2, b2)
                    wait(dve, small2, b2, 3, 3)
                    wait(dve, q2_ready, b2, 1, 0)
                    dve.tensor_scalar(rounded2[:, :], st_ps[:, :, :].rearrange("p a b -> p (a b)"),
                                      inv2[:, b2.par:b2.par + 1], MAGIC, ALU.mult, ALU.add).then_inc(scaled2, 1)
                    wait(dve, scaled2, b2, 1, 1)
                    dve.tensor_scalar(rounded2[:, :], rounded2[:, :], MAGIC + 127.0, MAGIC - 128.0,
                                      ALU.min, ALU.max).then_inc(round2_ready, 1)
                if b3:
                    wait(dve, o_done, b3, 1, 1)
                    loaded(dve, r_loaded, b3)
                    if not b3.known() or b3.n >= 2:
                        dve.wait_ge(stored[b3.par], (b3.n - b3.par) * 8)
                    dve.scalar_tensor_tensor(out=x_o[:, b3.par, :], in0=o_ps, scalar=fac2[:, b3.par:b3.par + 1],
                                             in1=x_r[:, b3.par, :], op0=ALU.mult, op1=ALU.add).then_inc(xo_ready, 1)
                if b1:
                    silu(b1, 0)
                if b0:
                    loaded(dve, x_loaded, b0)
                    dve.tensor_scalar(xn[:, b0.par, :], x_t[:, b0.par, :], mean[:, bass.ds(b0.n, 1)],
                                      rstd[:, bass.ds(b0.n, 1)], ALU.subtract, ALU.mult).then_inc(xn_ready, 1)
                    wait(dve, xn_ready, b0, 1, 1)
                    wait(dve, q1t_done, b0, 1, -1)
                    scales(xn[:, b0.par, :], b0.par, 1e-5, peak1, step1, inv1, fac1, 0, small, b0)\
                        .then_inc(fac1_ready, 1)
                    wait(dve, small, b0, 3, 3)
                    dve.tensor_scalar(xn[:, b0.par, :], xn[:, b0.par, :], inv1[:, b0.par:b0.par + 1], MAGIC,
                                      ALU.mult, ALU.add).then_inc(scaled1, 1)
                    wait(dve, scaled1, b0, 1, 1)
                    wait(dve, q1_ready, b0, 1, -1)
                    dve.tensor_scalar(rounded[:, b0.par, :], xn[:, b0.par, :], MAGIC + 127.0, MAGIC - 128.0,
                                      ALU.min, ALU.max).then_inc(round1_ready, 1)
                if b1:
                    silu(b1, 1)
            pipeline(dve, count, 4, step)


def decoder(nc, ins, scratch, x_out):
    with ExitStack() as ctx:
        def sb(n, shape, dt=F32):
            return ctx.enter_context(nc.sbuf_tensor(n, shape, dt))

        ident, ident_b = sb("ident", [P, P]), sb("ident_b", [P, P], BF16)
        mean, rstd, rms_scale = sb("mean", [P, NB]), sb("rstd", [P, NB]), sb("rms_scale", [P, NB])
        stats = sb("stats", [P, NB, 6])
        consts_loaded = ctx.enter_context(nc.semaphore("consts_loaded"))
        with nc.Block() as block:
            @block.sync
            def _(sp):
                sp.dma_start(ident[:, :], ins["ident"]).then_inc(consts_loaded, 16)
                sp.dma_start(ident_b[:, :], ins["ident_b"]).then_inc(consts_loaded, 16)
                sp.wait_ge(consts_loaded, 32)

        def part(prefix):
            return {n[len(prefix):]: ap for n, ap in {**ins, **scratch}.items() if n.startswith(prefix)}

        x = [ins["x"]] + [scratch[f"x{i}"] for i in range(1, 6)] + [x_out]

        latent_weights(nc, part("latent_"), part("self_"))
        alibi_rows(nc, ins["q_pos"], ins["k_pos"], ins["slope_rows"], scratch["alibi_q"], scratch["alibi_k"])
        first_statistics(nc, x[0], stats)
        norm_scales(nc, "norm0", stats, mean, rstd)
        attention(nc, "self", False, x[0], x[1], None, None, None, stats, mean, rstd, ident, ident_b, part("self_"), None)
        norm_scales(nc, "norm1", stats, mean, rstd)
        attention(nc, "cross", True, x[1], x[2], ins["ctx"], ins["mask"],
                  dict(q=scratch["alibi_q"], k=scratch["alibi_k"], slopes=ins["slope_parts"]),
                  stats, mean, rstd, ident, ident_b, part("cross_"), None)
        norm_scales(nc, "norm2", stats, mean, rstd)
        experts_ffn(nc, x[2], x[3], mean, rstd, ident, part("moe_"), scratch["sorted_x"])
        first_statistics(nc, x[3], stats, name="joined")
        norm_scales(nc, "norm3", stats, mean, rstd, rms_scale=rms_scale)
        mixer(nc, x[3], x[4], stats, mean, rstd, rms_scale, ident, part("mix_"))
        norm_scales(nc, "norm4", stats, mean, rstd)
        cross_values(nc, x[4], x[5], ins["ctx"], stats, mean, rstd, ident, part("vis_"))
        norm_scales(nc, "norm5", stats, mean, rstd)
        quantised_ffn(nc, x[5], x[6], mean, rstd, ident, ident_b, part("q_"))


def by_chunks(w):
    return w.reshape(w.shape[0] // P, P, w.shape[1]).transpose(1, 0, 2)


def column(v):
    return v.reshape(-1, P).T


def rows(v):
    return np.broadcast_to(v.reshape(-1), (P, v.size))


def kernel(**inputs):
    import concourse.bacc as bacc
    import ml_dtypes
    from concourse.bass_utils import run_bass_kernel_spmd

    inp = {name: np.asarray(a) for name, a in inputs.items()}
    bf16 = ml_dtypes.bfloat16

    slope = np.asarray([(2.0 ** (-8.0 / HEADS)) ** i for i in range(1, HEADS + 1)], np.float32)
    slope_parts, rest = [], slope
    for _ in range(3):
        slope_parts.append(rest.astype(bf16))
        rest = rest - slope_parts[-1].astype(np.float32)
    negated = np.stack([np.repeat(-part, P) for part in slope_parts])
    head_mask = (np.arange(P)[:, None] // HD == np.arange(P // HD)[None, :]).astype(np.float32)
    tiles = expert_tiles(NB)
    zeros = np.zeros(D, np.float32)
    padding = np.zeros((P, WIDE), np.float32)
    padding[:, D + 1] = NB * P + np.arange(P)

    lay = {
        "x": inp["x"], "ctx": inp["ctx_1024"], "mask": inp["mask_BxSxS2_if1"],
        "q_pos": inp["itok_BxS_8_8191"], "k_pos": inp["itok_BxS2_1_8191"],
        "ident": np.eye(P, dtype=np.float32), "ident_b": np.eye(P, dtype=np.float32).astype(bf16),
        "slope_rows": np.broadcast_to(slope, (NB, HEADS)), "slope_parts": np.tile(negated, (3, 1)),

        "latent_down": inp["L0_attn_Wl"].T,
        "latent_up": np.concatenate([inp["L0_attn_Wk"], inp["L0_attn_Wv"]], 1),
        "latent_bl": inp["L0_attn_bl"].reshape(LATENT, 1),
        "latent_bk": column(inp["L0_attn_bk"]), "latent_bv": rows(inp["L0_attn_bv"]),
        "self_wq": by_chunks(inp["L0_attn_Wq"]), "self_wo": by_chunks(inp["L0_attn_Wo"]),
        "self_bq": column(inp["L0_attn_bq"]), "self_bo": rows(inp["L0_attn_bo"]), "self_head_mask": head_mask,

        "cross_wq": by_chunks(inp["L0_xattn_W_q"].T), "cross_wk": by_chunks(inp["L0_xattn_W_k"].T),
        "cross_wv": by_chunks(inp["L0_xattn_W_v"].T), "cross_wo": by_chunks(inp["L0_xattn_W_o"].T),
        "cross_bq": column(zeros), "cross_bk": column(zeros), "cross_bv": rows(zeros), "cross_bo": rows(zeros),
        "cross_head_mask": head_mask,

        "moe_wr": by_chunks(inp["L0_ffn_Wr"]), "moe_br": rows(inp["L0_ffn_br"]),
        "moe_w1": inp["L0_ffn_W1"].reshape(EXPERTS, DC, P, HID).transpose(2, 0, 1, 3),
        "moe_w2": inp["L0_ffn_W2"].reshape(EXPERTS, HC, P, D).transpose(2, 0, 1, 3),
        "moe_b1": inp["L0_ffn_b1"].reshape(EXPERTS * HC, P).T, "moe_b2": rows(inp["L0_ffn_b2"]),
        "moe_falling": rows(np.arange(EXPERTS, 0, -1).astype(np.float32)),
        "moe_before": np.triu(np.ones((P, P), np.float32), 1), "moe_ones": np.ones((P, P), np.float32),
        "moe_tile_no": np.arange(tiles, dtype=np.float32)[None],
        "moe_base": rows(np.arange(EXPERTS, dtype=np.float32) * expert_rows(NB)),
        "moe_token_no": np.arange(NB * P, dtype=np.float32).reshape(NB, P).T, "moe_padding": padding,

        "mix_w_in": by_chunks(inp["L1_attn_in_proj_w"].T), "mix_w_out": by_chunks(inp["L1_attn_out_proj_w"].T),
        "mix_w_fc": by_chunks(inp["L1_attn_fc_w"].T), "mix_w_pr": by_chunks(inp["L1_attn_proj_w"].T),
        "mix_norm1": column(inp["L1_attn_norm1_w"]), "mix_norm2": column(inp["L1_attn_norm2_w"]),

        "vis_w_vk": by_chunks(inp["L1_xattn_W_vk"].T), "vis_w_lk": by_chunks(inp["L1_xattn_W_lk"].T),
        "vis_w_vv": by_chunks(inp["L1_xattn_W_vv"].T), "vis_w_lv": by_chunks(inp["L1_xattn_W_lv"].T),
        "vis_b_vk": column(inp["L1_xattn_b_vk"]), "vis_b_lk": column(inp["L1_xattn_b_lk"]),
        "vis_b_vv": rows(inp["L1_xattn_b_vv"]), "vis_b_lv": rows(inp["L1_xattn_b_lv"]),

        "q_w1": by_chunks(inp["L1_ffn_w1"].T).reshape(P, -1), "q_w2": by_chunks(inp["L1_ffn_w2"].T).reshape(P, -1),
        "q_conv_w": inp["L1_ffn_conv_w"].reshape(HC, P, 3).transpose(1, 2, 0),
        "q_conv_b": inp["L1_ffn_conv_b"].reshape(1, HID),
    }

    nc = bacc.Bacc("TRN2", target_bir_lowering=False, num_devices=1)
    arrays, ins = {}, {}
    for name, a in lay.items():
        arrays[f"in_{name}"] = np.ascontiguousarray(a)
        ins[name] = nc.dram_tensor(f"in_{name}", list(a.shape), mybir.dt.from_np(a.dtype), kind="ExternalInput").ap()

    def internal(name, shape, dt=F32):
        return nc.dram_tensor(f"dram_{name}", shape, dt, kind="Internal").ap()

    scratch = {f"x{i}": internal(f"x{i}", [NB + (i == 3), P, D]) for i in range(1, 6)}
    scratch["self_wk"], scratch["self_wv"] = internal("self_wk", [P, DC, D]), internal("self_wv", [P, DC, D])
    scratch["self_bk"], scratch["self_bv"] = internal("self_bk", [P, DC]), internal("self_bv", [P, D])
    scratch["alibi_q"], scratch["alibi_k"] = internal("alibi_q", [12, NB, P], BF16), internal("alibi_k", [NB, 3, HEADS * P], BF16)
    scratch["sorted_x"] = internal("sorted_x", [sorted_rows(NB), WIDE])
    x_out = nc.dram_tensor("x_out", [NB, P, D], F32, kind="ExternalOutput").ap()
    decoder(nc, ins, scratch, x_out)
    return run_bass_kernel_spmd(nc, [arrays], core_ids=[0]).results[0]["x_out"]
```

```python
from contextlib import ExitStack

import numpy as np

import concourse.bass as bass
from concourse import mybir

F32, BF16, I32, U32 = mybir.dt.float32, mybir.dt.bfloat16, mybir.dt.int32, mybir.dt.uint32
ALU = mybir.AluOpType
ACT = mybir.ActivationFunctionType
AX = mybir.AxisListType

P = 128
NB = 32
D = 256
DC = D // P
HEADS = 16
HD = D // HEADS
LATENT = D // 4
QUADS = HEADS // 4
LN_EPS = 1e-5


class Semaphores:

    def __init__(self, nc, ctx, name):
        self.nc, self.ctx, self.name, self.cleared = nc, ctx, name, []

    def __call__(self, n):
        s = self.ctx.enter_context(self.nc.semaphore(f"{self.name}_{n}"))
        self.cleared.append(s)
        return s

    def kept(self, n):
        return self.nc.alloc_semaphore(f"{self.name}_{n}")

    def clear(self):
        with self.nc.Block() as block:
            @block.gpsimd
            def _(pool):
                numbers = sorted(s.num for s in self.cleared)
                first = 0
                for i, number in enumerate(numbers):
                    if i + 1 == len(numbers) or numbers[i + 1] != number + 1:
                        pool.sem_clear(range(numbers[first], number + 1))
                        first = i + 1


class Weights:

    def __init__(self, nc, ctx, name, dram, keys):
        self.dram = {key: dram[key] for key in keys}
        self.tiles = {key: ctx.enter_context(nc.sbuf_tensor(f"{name}_{key}", list(dram[key].shape), F32)) for key in keys}
        self.loaded = nc.alloc_semaphore(f"{name}_weights_loaded")

    def __getitem__(self, key):
        return self.tiles[key]

    def start(self, eng):
        for key, tile in self.tiles.items():
            eng.dma_start(tile[(slice(None),) * len(tile.shape)], self.dram[key]).then_inc(self.loaded, 16)

    def wait(self, eng):
        eng.wait_ge(self.loaded, 16 * len(self.tiles))


class Batch:

    def __init__(self, number, parity):
        self.n, self.par = number, parity

    def known(self):
        return isinstance(self.n, int)


def wait(eng, sem, batch, per_batch, done):
    value = batch.n * per_batch + done if per_batch != 1 else batch.n + done
    if batch.known() and value <= 0:
        return
    eng.wait_ge(sem, value)


def pipeline(eng, count, depth, step):
    lag = depth - 1
    start = (lag + 3) // 2 * 2

    def one(t, parity):
        def at(k):
            if isinstance(t, int):
                return Batch(t - k, (t - k) % 2) if 0 <= t - k < count else None
            return Batch(t - k if k else t, (parity - k) % 2)
        step(at)

    end = start + (count - start) // 2 * 2
    for t in range(start):
        one(t, t % 2)
    with eng.Fori(start, end - 1, 2) as i:
        one(i, 0)
        one(i + 1, 1)
    for t in range(end, count + lag):
        one(t, t % 2)


def chained(eng, sem):
    count = [0]

    def link(instruction):
        count[0] += 1
        instruction.then_inc(sem, 1)
        eng.wait_ge(sem, count[0])
    return link


def first_statistics(nc, ctx, block, x_in, stats, count=NB, name="first"):
    per, buffers = 4, 4
    x_a = ctx.enter_context(nc.sbuf_tensor(f"{name}_x", [P, buffers, per, D], F32))
    loaded = [nc.alloc_semaphore(f"{name}_loaded{i}") for i in range(buffers)]
    done = nc.alloc_semaphore(f"{name}_done")

    @block.sync
    def _(sp):
        for g in range(count // per):
            if g >= buffers:
                sp.wait_ge(done, per * (g - buffers + 1))
            sp.dma_start(x_a[:, g % buffers, :, :], x_in[per * g:per * g + per].rearrange("b t d -> t b d"))\
              .then_inc(loaded[g % buffers], 16)

    @block.vector
    def _(dve):
        for g in range(count // per):
            dve.wait_ge(loaded[g % buffers], 16 * (g // buffers + 1))
            for i in range(per):
                dve.bn_stats(stats[:, per * g + i, :], x_a[:, g % buffers, i, :]).then_inc(done, 1)


def norm_scales(nc, name, stats, mean, rstd, rms_scale=None, rms_eps=1e-6, ahead=(), count=NB):
    with ExitStack() as ctx:
        def sb(n):
            return ctx.enter_context(nc.sbuf_tensor(f"{name}_{n}", [P, count], F32))
        diff, var, root, tmp = sb("diff"), sb("var"), sb("root"), sb("tmp")
        dve_step = nc.alloc_semaphore(f"{name}_dve_step")
        var_ready = nc.alloc_semaphore(f"{name}_var_ready")
        root_ready = nc.alloc_semaphore(f"{name}_root_ready")
        block = ctx.enter_context(nc.Block())
        rounds = 1 if rms_scale is None else 2

        @block.vector
        def _(dve):
            link = chained(dve, dve_step)

            def tt(out, a, b, op):
                link(dve.tensor_tensor(out, a, b, op))

            def inverse_root(out, turn):
                link(dve.tensor_copy(tmp[:, :], var[:, :]))
                dve.sem_inc(var_ready, 1)
                dve.wait_ge(root_ready, turn)
                link(dve.reciprocal(out, root[:, :]))
                tt(tmp[:, :], out, out, ALU.mult)
                tt(tmp[:, :], tmp[:, :], var[:, :], ALU.mult)
                link(dve.tensor_scalar(tmp[:, :], tmp[:, :], -0.5, 1.5, ALU.mult, ALU.add))
                tt(out, out, tmp[:, :], ALU.mult)

            tt(mean[:, :], stats[:, :, 1], stats[:, :, 4], ALU.add)
            link(dve.tensor_scalar(mean[:, :], mean[:, :], 0.5, None, ALU.mult))
            tt(diff[:, :], stats[:, :, 1], stats[:, :, 4], ALU.subtract)
            tt(diff[:, :], diff[:, :], diff[:, :], ALU.mult)
            link(dve.tensor_scalar(diff[:, :], diff[:, :], 0.25, LN_EPS, ALU.mult, ALU.add))
            tt(var[:, :], stats[:, :, 2], stats[:, :, 5], ALU.add)
            link(dve.tensor_scalar(var[:, :], var[:, :], 1.0 / D, None, ALU.mult))
            if rms_scale is not None:
                tt(rms_scale[:, :], var[:, :], diff[:, :], ALU.add)
                link(dve.tensor_scalar(rms_scale[:, :], rms_scale[:, :], -LN_EPS, None, ALU.add))
            tt(var[:, :], var[:, :], diff[:, :], ALU.add)
            inverse_root(rstd[:, :], 1)
            if rms_scale is not None:
                tt(tmp[:, :], rstd[:, :], rstd[:, :], ALU.mult)
                tt(var[:, :], rms_scale[:, :], tmp[:, :], ALU.mult)
                link(dve.tensor_scalar(var[:, :], var[:, :], rms_eps, None, ALU.add))
                inverse_root(rms_scale[:, :], 2)
                tt(rms_scale[:, :], rms_scale[:, :], rstd[:, :], ALU.mult)

        @block.scalar
        def _(act):
            for weights_ahead in ahead:
                weights_ahead.start(act)
            for turn in range(rounds):
                act.wait_ge(var_ready, turn + 1)
                act.activation(root[:, :], var[:, :], ACT.Sqrt).then_inc(root_ready, 1)


def alibi_rows(nc, ctx, block, q_pos, k_pos, slope_bc, q_rows, k_rows, count=NB):
    def sb(n, shape, dt):
        return ctx.enter_context(nc.sbuf_tensor(f"alibi_{n}", shape, dt))
    ints = sb("ints", [count, 2, P], I32)
    pos = sb("pos", [count, 2, P], F32)
    slope = sb("slope", [count, HEADS], F32)
    prod = sb("prod", [count, HEADS, P], F32)
    parts = sb("parts", [count, 3, HEADS, P], BF16)
    q_parts = sb("q_parts", [count, 4, P], BF16)
    loaded, step, stored = (nc.alloc_semaphore(f"alibi_{n}") for n in ("loaded", "step", "stored"))
    parts_ready = nc.alloc_semaphore("alibi_parts_ready")

    @block.scalar
    def _(act):
        act.dma_start(ints[:, 0, :], q_pos).then_inc(loaded, 16)
        act.dma_start(ints[:, 1, :], k_pos).then_inc(loaded, 16)
        act.dma_start(slope[:, :], slope_bc).then_inc(loaded, 16)
        act.wait_ge(parts_ready, 1)
        for row in range(12):
            a = 3 if row < 3 else (row - 3) // 3
            act.dma_start(q_rows[row], q_parts[:, a, :]).then_inc(stored, 16)
        act.dma_start(k_rows.rearrange("b a n -> b (a n)"),
                     parts[:, :, :, :].rearrange("b a h t -> b (a h t)")).then_inc(stored, 16)
        act.wait_ge(stored, 16 * 13)

    @block.vector
    def _(dve):
        link = chained(dve, step)
        dve.wait_ge(loaded, 48)
        link(dve.tensor_copy(pos[:, :, :], ints[:, :, :]))
        link(dve.memset(q_parts[:, 3, :], 1.0))
        link(dve.tensor_tensor(prod[:, :, :], pos[:, 1, :].unsqueeze(1).to_broadcast([count, HEADS, P]),
                               slope[:, :].unsqueeze(2).to_broadcast([count, HEADS, P]), ALU.mult))
        for part in range(3):
            link(dve.tensor_copy(parts[:, part, :, :], prod[:, :, :]))
            link(dve.tensor_copy(q_parts[:, part, :], pos[:, 0, :]))
            if part < 2:
                link(dve.tensor_tensor(prod[:, :, :], prod[:, :, :], parts[:, part, :, :], ALU.subtract))
                link(dve.tensor_tensor(pos[:, 0, :], pos[:, 0, :], q_parts[:, part, :], ALU.subtract))
        dve.sem_inc(parts_ready, 1)


def latent_weights(nc, ctx, block, w_in, w_out):
    def sb(n, shape):
        return ctx.enter_context(nc.sbuf_tensor(f"latent_{n}", shape, F32))

    def sem(n):
        return nc.alloc_semaphore(f"latent_{n}")

    down, up = sb("down", [LATENT, D]), sb("up", [LATENT, 2 * D])
    bl, bl_rows = sb("bl", [LATENT, 1]), sb("bl_rows", [LATENT, P])
    bk, bv = sb("bk", [P, DC]), sb("bv", [P, D])
    both = sb("both", [P, DC, 2 * D])
    w_ps = ctx.enter_context(nc.psum_tensor("latent_w_ps", [P, DC, 2 * D], F32))
    v_ps = ctx.enter_context(nc.psum_tensor("latent_v_ps", [P, 2 * D], F32))
    k_ps = ctx.enter_context(nc.psum_tensor("latent_k_ps", [P, 2 * D], F32))
    loaded, rows_ready, done, ready, stored = (sem(n) for n in ("loaded", "rows_ready", "done", "ready", "stored"))

    @block.gpsimd
    def _(pool):
        for dst, key in ((down, "down"), (up, "up"), (bl, "bl"), (bk, "bk"), (bv, "bv")):
            pool.dma_start(dst[:, :], w_in[key]).then_inc(loaded, 16)
        pool.wait_ge(ready, 3)
        pool.dma_start(w_out["wk"], both[:, :, 0:D]).then_inc(stored, 16)
        pool.dma_start(w_out["wv"], both[:, :, D:2 * D]).then_inc(stored, 16)
        pool.dma_start(w_out["bk"], bk[:, :]).then_inc(stored, 16)
        pool.dma_start(w_out["bv"], bv[:, :]).then_inc(stored, 16)
        pool.wait_ge(stored, 64)

    @block.tensor
    def _(pe):
        pe.wait_ge(loaded, 80)
        for c in range(DC):
            pe.matmul(w_ps[:, c, :], down[:, P * c:P * c + P], up[:, :], start=True, stop=True)
        for c in range(DC):
            pe.matmul(k_ps[:, c:c + 1], up[:, P * c:P * c + P], bl[:, :], start=True, stop=True)
        pe.wait_ge(rows_ready, 1)
        pe.matmul(v_ps[:, 0:D], bl_rows[:, :], up[:, D:2 * D], start=True, stop=True).then_inc(done, 1)

    @block.vector
    def _(dve):
        dve.wait_ge(loaded, 80)
        dve.tensor_copy(bl_rows[:, :], bl[:, :].to_broadcast([LATENT, P])).then_inc(rows_ready, 1)
        dve.wait_ge(done, 1)
        dve.tensor_copy(both[:, :, :], w_ps[:, :, :]).then_inc(ready, 1)
        dve.tensor_tensor(bk[:, :], k_ps[:, 0:DC], bk[:, :], ALU.add).then_inc(ready, 1)
        dve.tensor_tensor(bv[:, :], v_ps[:, 0:D], bv[:, :], ALU.add).then_inc(ready, 1)


ATTENTION_WEIGHTS = ("wq", "wk", "wv", "wo", "bq", "bk", "bv", "bo", "head_mask")


def attention(nc, name, cross, x_in, x_out, ctx_in, mask_in, alibi, stats, mean, rstd, ident,
              ident_b, weights, ahead=(), count=NB):
    with ExitStack() as ctx:
        def sb(n, shape, dt=F32):
            return ctx.enter_context(nc.sbuf_tensor(f"{name}_{n}", shape, dt))

        def ps(n, shape):
            return ctx.enter_context(nc.psum_tensor(f"{name}_{n}", shape, F32))

        sem = Semaphores(nc, ctx, name)

        wq, wk, wv, wo, bq, bk, bv, bo, head_mask = (
            weights[key] for key in ATTENTION_WEIGHTS)
        x_t, x_r, xn, o_n, x_o = (sb(n, [P, 2, D]) for n in ("x_t", "x_r", "xn", "o_n", "x_o"))
        xnT, o_nT, qT, kT = (sb(n, [P, 2, DC, P]) for n in ("xnT", "o_nT", "qT", "kT"))
        k_diag = sb("k_diag", [P, 2, HEADS, P])
        v_pad = sb("v_pad", [P, 2, HEADS, 32])
        probs = sb("probs", [P, QUADS, 4, P])
        probsT = sb("probsT", [P, 2, 4, P])
        oT = sb("oT", [P, QUADS, P])
        neg_max, sums, inv = (sb(n, [P, 2, HEADS]) for n in ("neg_max", "sums", "inv"))
        s_ps = ps("scores", [P, QUADS, 4, P])
        o_ps = ps("o_ps", [P, QUADS, P])
        b_ps = ps("b_ps", [P, 512])
        p_ps = [ps("p0", [P, 512]), ps("p1", [P, 512])]

        alibi_loaded, scaled = sem("alibi_loaded"), sem("scaled")
        x_loaded = [sem("x_loaded0"), sem("x_loaded1")]
        r_loaded = [sem("r_loaded0"), sem("r_loaded1")]
        xn_ready, xt_done, xnT_ready = sem("xn_ready"), sem("xt_done"), sem("xnT_ready")
        q_done, k_done, v_done = sem("q_done"), sem("k_done"), sem("v_done")
        q_ready, k_ready, v_ready, diag_ready = sem("q_ready"), sem("k_ready"), sem("v_ready"), sem("diag_ready")
        s_done, max_ready, exp_ready = sem("s_done"), sem("max_ready"), sem("exp_ready")
        pt_done, pt_ready, pv_done = sem("pt_done"), sem("pt_ready"), sem("pv_done")
        oT_ready, back_done, on_ready, inv_ready = sem("oT_ready"), sem("back_done"), sem("on_ready"), sem("inv_ready")
        ont_done, onT_ready, wo_done = sem("ont_done"), sem("onT_ready"), sem("wo_done")
        r_biased, xo_ready, stat_ready = sem("r_biased"), sem("xo_ready"), sem("stat_ready")
        stored = [sem.kept("stored0"), sem.kept("stored1")]
        if cross:
            c_t = sb("c_t", [P, 2, D])
            cT = sb("cT", [P, 2, DC, P])
            mask_t = sb("mask_t", [P, 2, P], I32)
            mask_b = sb("mask_b", [P, 2, P], BF16)
            rows_k = sb("rows_k", [12, 2, HEADS * P], BF16)
            rows_q = sb("rows_q", [12, NB, P], BF16)
            c_loaded = [sem("c_loaded0"), sem("c_loaded1")]
            m_loaded = [sem("m_loaded0"), sem("m_loaded1")]
            k_rows_loaded = [sem("k_rows0"), sem("k_rows1")]
            ct_done, cT_ready, mask_ready = sem("ct_done"), sem("cT_ready"), sem("mask_ready")
        ctx.callback(sem.clear)
        block = ctx.enter_context(nc.Block())

        @block.sync
        def _(sp):
            if cross:
                sp.dma_start(rows_q[:, :, :], alibi["q"]).then_inc(alibi_loaded, 16)
                for par in range(2):
                    sp.dma_start(rows_k[3:12, par, :], alibi["slopes"]).then_inc(alibi_loaded, 16)

            def step(at):
                b = at(0)
                if b:
                    wait(sp, xn_ready, b, 1, -1)
                    sp.dma_start(x_t[:, b.par, :], x_in[b.n]).then_inc(x_loaded[b.par], 16)
                    if cross:
                        wait(sp, ct_done, b, 1, -1)
                        sp.dma_start(c_t[:, b.par, :], ctx_in[b.n]).then_inc(c_loaded[b.par], 16)
                        wait(sp, mask_ready, b, 1, -1)
                        sp.dma_start(mask_t[:, b.par, :], mask_in[b.n]).then_inc(m_loaded[b.par], 16)
                        wait(sp, s_done, b, QUADS, -QUADS)
                        sp.dma_start(rows_k[0:3, b.par, :], alibi["k"][b.n]).then_inc(k_rows_loaded[b.par], 16)
                    wait(sp, xo_ready, b, 1, -1)
                    sp.dma_start(x_r[:, b.par, :], x_in[b.n]).then_inc(r_loaded[b.par], 16)
            pipeline(sp, count, 1, step)
            for par in range(2):
                sp.wait_ge(stored[par], 16 * (count // 2))

        def loaded(eng, sems, b):
            eng.wait_ge(sems[b.par], (b.n + (2 - b.par)) * 8)

        @block.tensor
        def _(pe):
            pe.wait_ge(scaled, 1)
            if cross:
                pe.wait_ge(alibi_loaded, 16 * 3)

            def scores(b, j):
                if j == 0:
                    wait(pe, q_ready, b, 1, 1)
                    wait(pe, diag_ready, b, 1, 1)
                    if cross:
                        wait(pe, mask_ready, b, 1, 1)
                        loaded(pe, k_rows_loaded, b)
                wait(pe, pt_ready, b, QUADS, j - 3)
                last = pe.matmul(s_ps[:, j, :, :], qT[:, b.par, j // 2, :],
                                 k_diag[:, b.par, 4 * j:4 * j + 4, :], start=True, stop=not cross)
                if cross:
                    pe.matmul(s_ps[:, j, :, :], ident_b[:, :],
                              mask_b[:, b.par, :].unsqueeze(1).to_broadcast([P, 4, P]), start=False, stop=False)
                    last = pe.matmul(s_ps[:, j, :, :], rows_q[:, b.n, :],
                                     rows_k[:, b.par, 512 * j:512 * j + 512].rearrange("p (a c) -> p a c", a=4),
                                     start=False, stop=True)
                last.then_inc(s_done, 1)

            def back(b):
                wait(pe, oT_ready, b, 1, 1)
                wait(pe, xo_ready, b, 1, 0)
                for j in range(QUADS):
                    last = pe.transpose(b_ps[:, P * j:P * j + P], oT[:, j, :], ident[:, :])
                last.then_inc(back_done, 1)

            def x_transpose(b):
                wait(pe, xn_ready, b, 1, 1)
                wait(pe, v_ready, b, 1, 0)
                for c in range(DC):
                    last = pe.transpose(p_ps[0][:, P * c:P * c + P], xn[:, b.par, P * c:P * c + P], ident[:, :])
                last.then_inc(xt_done, 1)
                if cross:
                    loaded(pe, c_loaded, b)
                    wait(pe, k_ready, b, 1, 0)
                    for c in range(DC):
                        last = pe.transpose(p_ps[1][:, P * c:P * c + P], c_t[:, b.par, P * c:P * c + P], ident[:, :])
                    last.then_inc(ct_done, 1)

            def on_transpose(b):
                wait(pe, on_ready, b, 1, 1)
                for c in range(DC):
                    last = pe.transpose(b_ps[:, P * c:P * c + P], o_n[:, b.par, P * c:P * c + P], ident[:, :])
                last.then_inc(ont_done, 1)

            def probs_transpose(b, j):
                wait(pe, exp_ready, b, QUADS, j + 1)
                for i in range(4):
                    last = pe.transpose(s_ps[:, j, i, :], probs[:, j, i, :], ident[:, :])
                last.then_inc(pt_done, 1)

            def project(b, w, src, bank, done):
                for m in range(DC):
                    for c in range(DC):
                        last = pe.matmul(p_ps[bank][:, P * m:P * m + P], w[:, c, P * m:P * m + P],
                                         src[:, b.par, c, :], start=(c == 0), stop=(c == DC - 1))
                last.then_inc(done, 1)

            def values(b, j):
                if j == 0:
                    wait(pe, v_ready, b, 1, 1)
                    wait(pe, oT_ready, b, 1, 0)
                wait(pe, pt_ready, b, QUADS, j + 1)
                for i in range(4):
                    last = pe.matmul(o_ps[32 * i:32 * i + 32, j, :], v_pad[:, b.par, 4 * j + i, :],
                                     probsT[:, j % 2, i, :], start=True, stop=True)
                last.then_inc(pv_done, 1)

            def step(at):
                b0, b1, b2 = at(0), at(1), at(2)
                src = cT if cross else xnT
                if b1:
                    scores(b1, 0)
                    scores(b1, 1)
                if b2:
                    back(b2)
                if b1:
                    scores(b1, 2)
                if b0:
                    x_transpose(b0)
                if b1:
                    scores(b1, 3)
                if b2:
                    on_transpose(b2)
                if b1:
                    probs_transpose(b1, 0)
                if b0:
                    if cross:
                        wait(pe, cT_ready, b0, 1, 1)
                    else:
                        wait(pe, xnT_ready, b0, 1, 1)
                        wait(pe, k_ready, b0, 1, 0)
                    project(b0, wk, src, 1, k_done)
                if b1:
                    probs_transpose(b1, 1)
                    values(b1, 0)
                if b0:
                    wait(pe, xnT_ready, b0, 1, 1)
                    project(b0, wq, xnT, 0, q_done)
                if b1:
                    probs_transpose(b1, 2)
                    values(b1, 1)
                if b2:
                    wait(pe, onT_ready, b2, 1, 1)
                    for c in range(DC):
                        last = pe.matmul(b_ps[:, 0:D], o_nT[:, b2.par, c, :], wo[:, c, :],
                                         start=(c == 0), stop=(c == DC - 1))
                    last.then_inc(wo_done, 1)
                if b1:
                    probs_transpose(b1, 3)
                    values(b1, 2)
                if b0:
                    wait(pe, q_ready, b0, 1, 1)
                    for c in range(DC):
                        last = pe.matmul(p_ps[0][:, 0:D], src[:, b0.par, c, :], wv[:, c, :],
                                         start=(c == 0), stop=(c == DC - 1))
                    last.then_inc(v_done, 1)
                if b1:
                    values(b1, 3)
            pipeline(pe, count, 3, step)

        @block.scalar
        def _(act):
            for weights_ahead in ahead:
                weights_ahead.start(act)

            def exps(b, j):
                wait(act, max_ready, b, QUADS, j + 1)
                wait(act, pt_done, b, QUADS, j - 3)
                if j == 0:
                    wait(act, on_ready, b, 1, -1)
                for i in range(4):
                    h = 4 * j + i
                    last = act.activation(probs[:, j, i, :], s_ps[:, j, i, :], ACT.Exp,
                                          bias=neg_max[:, b.par, h:h + 1], scale=1.0,
                                          accum_out=sums[:, b.par, h:h + 1])
                last.then_inc(exp_ready, 1)

            def step(at):
                b0, b1, b2 = at(0), at(1), at(2)
                if b2:
                    wait(act, pv_done, b2, QUADS, QUADS)
                    act.copy(oT[:, :, :], o_ps[:, :, :]).then_inc(oT_ready, 1)
                if b1:
                    exps(b1, 0)
                if b0:
                    wait(act, xt_done, b0, 1, 1)
                    wait(act, v_done if not cross else q_done, b0, 1, -1)
                    act.copy(xnT[:, b0.par, :, :], p_ps[0][:, 0:D].rearrange("p (c t) -> p c t", c=DC))\
                       .then_inc(xnT_ready, 1)
                    if cross:
                        wait(act, ct_done, b0, 1, 1)
                        wait(act, v_done, b0, 1, -1)
                        act.copy(cT[:, b0.par, :, :], p_ps[1][:, 0:D].rearrange("p (c t) -> p c t", c=DC))\
                           .then_inc(cT_ready, 1)
                if b1:
                    exps(b1, 1)
                if b2:
                    wait(act, ont_done, b2, 1, 1)
                    wait(act, wo_done, b2, 1, -1)
                    act.copy(o_nT[:, b2.par, :, :], b_ps[:, 0:D].rearrange("p (c t) -> p c t", c=DC))\
                       .then_inc(onT_ready, 1)
                if b1:
                    exps(b1, 2)
                    exps(b1, 3)
            pipeline(act, count, 3, step)

        @block.vector
        def _(dve):
            dve.memset(v_pad[:, :, :, :], 0.0)
            weights.wait(dve)
            dve.tensor_scalar(wq[:, :, :], wq[:, :, :], HD ** -0.5, None, ALU.mult)
            dve.tensor_scalar(bq[:, :], bq[:, :], HD ** -0.5, None, ALU.mult).then_inc(scaled, 1)
            dve.wait_ge(scaled, 1)

            def maxima(b, j):
                wait(dve, s_done, b, QUADS, j + 1)
                if j == 0:
                    wait(dve, exp_ready, b, QUADS, -QUADS)
                dve.tensor_reduce(neg_max[:, b.par, 4 * j:4 * j + 4], s_ps[:, j, :, :], AX.X, ALU.max,
                                  negate=True).then_inc(max_ready, 1)

            def probsT_copy(b, j):
                wait(dve, pt_done, b, QUADS, j + 1)
                wait(dve, pv_done, b, QUADS, j - 1)
                dve.tensor_copy(probsT[:, j % 2, :, :], s_ps[:, j, :, :]).then_inc(pt_ready, 1)

            def step(at):
                b0, b1, b2 = at(0), at(1), at(2)
                if b0:
                    loaded(dve, x_loaded, b0)
                    wait(dve, xt_done, b0, 1, -1)
                    dve.tensor_scalar(xn[:, b0.par, :], x_t[:, b0.par, :], mean[:, bass.ds(b0.n, 1)],
                                      rstd[:, bass.ds(b0.n, 1)], ALU.subtract, ALU.mult).then_inc(xn_ready, 1)
                    if cross:
                        loaded(dve, m_loaded, b0)
                        wait(dve, s_done, b0, QUADS, -QUADS)
                        dve.tensor_scalar(mask_b[:, b0.par, :], mask_t[:, b0.par, :], 0.0, -3.0e38,
                                          ALU.is_equal, ALU.mult).then_inc(mask_ready, 1)
                if b1:
                    maxima(b1, 0)
                if b2:
                    src = sums
                    wait(dve, exp_ready, b2, QUADS, QUADS)
                    if cross:
                        dve.tensor_scalar(sums[:, b2.par, :], sums[:, b2.par, :], 1.0, None, ALU.add)\
                           .then_inc(inv_ready, 1)
                        wait(dve, inv_ready, b2, 2, 1)
                    dve.reciprocal(inv[:, b2.par, :], sums[:, b2.par, :]).then_inc(inv_ready, 1)
                    wait(dve, inv_ready, b2, 1 + cross, 1 + cross)
                    wait(dve, back_done, b2, 1, 1)
                    wait(dve, ont_done, b2, 1, -1)
                    dve.tensor_tensor(o_n[:, b2.par, :].rearrange("p (h d) -> p h d", h=HEADS),
                                      b_ps[:, :].rearrange("p (h d) -> p h d", h=HEADS)[:, :, 0:HD],
                                      inv[:, b2.par, :].unsqueeze(2).to_broadcast([P, HEADS, HD]),
                                      ALU.mult).then_inc(on_ready, 1)
                if b1:
                    maxima(b1, 1)
                    maxima(b1, 2)
                    maxima(b1, 3)
                    probsT_copy(b1, 0)
                if b0:
                    wait(dve, k_done, b0, 1, 1)
                    wait(dve, diag_ready, b0, 1, -1)
                    dve.tensor_tensor(kT[:, b0.par, :, :], p_ps[1][:, 0:D].rearrange("p (c t) -> p c t", c=DC),
                                      bk[:, :].unsqueeze(2).to_broadcast([P, DC, P]), ALU.add)\
                       .then_inc(k_ready, 1)
                if b1:
                    probsT_copy(b1, 1)
                if b0:
                    wait(dve, q_done, b0, 1, 1)
                    wait(dve, s_done, b0, QUADS, -QUADS)
                    dve.tensor_tensor(qT[:, b0.par, :, :], p_ps[0][:, 0:D].rearrange("p (c t) -> p c t", c=DC),
                                      bq[:, :].unsqueeze(2).to_broadcast([P, DC, P]), ALU.add)\
                       .then_inc(q_ready, 1)
                if b1:
                    probsT_copy(b1, 2)
                if b2:
                    wait(dve, wo_done, b2, 1, 1)
                    wait(dve, r_biased, b2, 1, 1)
                    if not b2.known() or b2.n >= 2:
                        dve.wait_ge(stored[b2.par], (b2.n - b2.par) * 8)
                    dve.tensor_tensor(x_o[:, b2.par, :], b_ps[:, 0:D], x_r[:, b2.par, :], ALU.add)\
                       .then_inc(xo_ready, 1)
                    wait(dve, xo_ready, b2, 1, 1)
                    dve.bn_stats(stats[:, b2.n, :], x_o[:, b2.par, :]).then_inc(stat_ready, 1)
                if b1:
                    probsT_copy(b1, 3)
                if b0:
                    wait(dve, v_done, b0, 1, 1)
                    wait(dve, pv_done, b0, QUADS, -QUADS)
                    dve.tensor_tensor(v_pad[:, b0.par, :, 0:HD], p_ps[0][:, 0:D].rearrange("p (h d) -> p h d", h=HEADS),
                                      bv[:, :].rearrange("p (h d) -> p h d", h=HEADS), ALU.add)\
                       .then_inc(v_ready, 1)
            pipeline(dve, count, 3, step)

        @block.gpsimd
        def _(pool):
            weights.wait(pool)

            def step(at):
                b0, b1, b2 = at(0), at(1), at(2)
                if b2:
                    loaded(pool, r_loaded, b2)
                    pool.tensor_tensor(x_r[:, b2.par, :], x_r[:, b2.par, :], bo[:, :], ALU.add)\
                        .then_inc(r_biased, 1)
                if b0:
                    wait(pool, k_ready, b0, 1, 1)
                    wait(pool, s_done, b0, QUADS, -QUADS)
                    for c in range(DC):
                        last = pool.tensor_tensor(
                            k_diag[:, b0.par, 8 * c:8 * c + 8, :],
                            kT[:, b0.par, c, :].unsqueeze(1).to_broadcast([P, 8, P]),
                            head_mask[:, :].unsqueeze(2).to_broadcast([P, 8, P]), ALU.mult)
                    last.then_inc(diag_ready, 1)
                if b2:
                    wait(pool, xo_ready, b2, 1, 1)
                    pool.dma_start(x_out[b2.n], x_o[:, b2.par, :]).then_inc(stored[b2.par], 16)
            pipeline(pool, count, 3, step)


HID = 1024
HC = HID // P
EXPERTS = 8
NEG_INF = -1.0e9
ROUNDER = 12582912.0
GROUP = 4
WIDE = D + 2
ROUTE_STEPS = 24


def expert_tiles(count):
    return 2 * count + EXPERTS - 1


def expert_rows(count):
    return (count + 1) * P


def sorted_rows(count):
    return EXPERTS * expert_rows(count) + EXPERTS * P


def experts_ffn(nc, x, mean, rstd, ident, w_dram, xg, ahead=(), count=NB):
    name = "moe"
    tiles, groups, part = expert_tiles(count), count // GROUP, expert_rows(count)
    with ExitStack() as ctx:
        def sb(n, shape, dt=F32, where=None):
            return (where or ctx).enter_context(nc.sbuf_tensor(f"{name}_{n}", shape, dt))

        def ps(n, shape, where):
            return where.enter_context(nc.psum_tensor(f"{name}_ps_{n}", shape, F32))

        sem = Semaphores(nc, ctx, name)

        w1, w2 = sb("w1", [P, EXPERTS, DC, HID]), sb("w2", [P, EXPERTS, HC, D])
        b1 = sb("b1", [P, EXPERTS * HC])
        tile_expert, tile_row = sb("tile_expert", [1, tiles], I32), sb("tile_row", [1, tiles], I32)
        pad_row = sb("pad_row", [1, EXPERTS], I32)
        seen = sb("seen", [P, EXPERTS], BF16)
        padding = sb("padding", [P, WIDE])
        ones = sb("ones", [P, P], BF16)
        w1_loaded, w2_loaded, b_loaded, r_loaded = sem("w1_loaded"), sem("w2_loaded"), sem("b_loaded"), sem("r_loaded")
        spare_ready, padded = sem("spare_ready"), sem("padded")

        with ExitStack() as route:
            wr, br, falling = (sb(n, shape, where=route) for n, shape in (
                ("wr", [P, DC, EXPERTS]), ("br", [P, EXPERTS]), ("falling", [P, EXPERTS])))
            before, base = sb("before", [P, P], BF16, where=route), sb("base", [P, EXPERTS], where=route)
            token_no = sb("token_no", [P, count], where=route)
            nothing, numbers = sb("nothing", [P, GROUP], where=route), sb("numbers", [P, 2, GROUP], where=route)
            xn = sb("xn", [P, 2, GROUP, D], where=route)
            row = sb("row", [P, 2, GROUP, 2, WIDE], where=route)
            xnT = sb("xnT", [P, 2, GROUP, DC, P], where=route)
            shape = [P, GROUP, EXPERTS]
            logits, equal, rest, place = (sb(n, shape, where=route) for n in ("logits", "equal", "rest", "place"))
            chosen = sb("chosen", shape, BF16, where=route)
            hot, mine = (sb(n, [P, 2, GROUP, EXPERTS], where=route) for n in ("hot", "mine"))
            tops, exps = (sb(n, [P, GROUP, EXPERTS], where=route) for n in ("tops", "exps"))
            key, low, total = (sb(n, [P, GROUP], where=route) for n in ("key", "low", "total"))
            slot = sb("slot", [P, 2, GROUP], where=route)
            index = sb("index", [P, 2, 2, GROUP], I32, where=route)
            xt_ps, l_ps = ps("xt", [P, 2, GROUP * D], route), ps("l", [P, 2, 512], route)
            rank_ps = ps("rank", [P, 512], route)
            x_loaded = [sem("x_loaded0"), sem("x_loaded1")]
            scattered = [sem.kept("scattered0"), sem.kept("scattered1")]
            prepared, xn_ready, rows_ready, xt_done, xnT_ready, l_done = (
                sem(n) for n in ("prepared", "xn_ready", "rows_ready", "xt_done", "xnT_ready", "l_done"))
            route_step, chosen_ready, rank_done, low_ready, exps_ready, index_ready, token_ready = (
                sem(n) for n in ("route_step", "chosen_ready", "rank_done", "low_ready", "exps_ready",
                                 "index_ready", "token_ready"))

            def row_free(eng, g):
                if not g.known() or g.n >= 2:
                    eng.wait_ge(scattered[g.par], (g.n - g.par) * 8 * 2 * GROUP)

            with nc.Block() as block:
                @block.sync
                def _(sp):
                    for dst, key_ in ((br, "br"), (falling, "falling"), (before, "before"), (base, "base"),
                                      (ones, "ones"), (token_no, "token_no"), (padding, "padding")):
                        sp.dma_start(dst[:, :], w_dram[key_]).then_inc(r_loaded, 16)
                    sp.dma_start(wr[:, :, :], w_dram["wr"]).then_inc(r_loaded, 16)

                    def step(at):
                        g = at(0)
                        if g:
                            wait(sp, rows_ready, g, 1, -1)
                            wait(sp, xt_done, g, 1, -1)
                            sp.dma_start(xn[:, g.par, :, :],
                                         x[0:count].rearrange("(g r) p d -> g p r d", r=GROUP)[g.n]).then_inc(x_loaded[g.par], 16)
                    pipeline(sp, groups, 1, step)

                @block.tensor
                def _(pe):
                    pe.wait_ge(r_loaded, 16 * 8)
                    pe.wait_ge(prepared, 1)

                    def step(at):
                        g0, g1 = at(0), at(1)
                        if g1:
                            wait(pe, chosen_ready, g1, 1, 1)
                            for r in range(GROUP):
                                out = rank_ps[:, EXPERTS * r:EXPERTS * r + EXPERTS]
                                pe.matmul(out, before[:, :], chosen[:, r, :], start=True, stop=False)
                                for earlier in range(r):
                                    pe.matmul(out, ones[:, :], chosen[:, earlier, :], start=False, stop=False)
                                last = pe.matmul(out, ones[:, :], seen[:, :], start=False, stop=True)
                            last.then_inc(rank_done, 1)
                        if g0:
                            wait(pe, xn_ready, g0, 1, 1)
                            wait(pe, xnT_ready, g0, 1, -1)
                            for r in range(GROUP):
                                for c in range(DC):
                                    col = P * (DC * r + c)
                                    last = pe.transpose(xt_ps[:, g0.par, col:col + P], xn[:, g0.par, r, P * c:P * c + P],
                                                        ident[:, :])
                            last.then_inc(xt_done, 1)
                            wait(pe, xnT_ready, g0, 1, 1)
                            for r in range(GROUP):
                                for c in range(DC):
                                    last = pe.matmul(l_ps[:, g0.par, EXPERTS * r:EXPERTS * r + EXPERTS],
                                                     xnT[:, g0.par, r, c, :], wr[:, c, :], start=(c == 0), stop=(c == DC - 1))
                            last.then_inc(l_done, 1)
                    pipeline(pe, groups, 2, step)

                @block.scalar
                def _(act):
                    act.dma_start(b1[:, :], w_dram["b1"]).then_inc(b_loaded, 16)
                    act.wait_ge(r_loaded, 16 * 8)
                    act.dma_start(x[count], padding[:, 0:D]).then_inc(spare_ready, 16)
                    act.dma_start(xg[EXPERTS * part:EXPERTS * (part + P)].rearrange("(t p) w -> p t w", p=P),
                                  padding[:, :].unsqueeze(1).to_broadcast([P, EXPERTS, WIDE])).then_inc(padded, 16)
                    loads = [(w[:, :, :, :].rearrange("p a b c -> p (a b c)").rearrange("p (g n) -> p g n", g=groups),
                              w_dram[key_].rearrange("p a b c -> p (a b c)").rearrange("p (g n) -> p g n", g=groups), done)
                             for w, key_, done in ((w1, "w1", w1_loaded), (w2, "w2", w2_loaded))]

                    def step(at):
                        g0, g1 = at(0), at(1)
                        if g0:
                            here = slice(g0.n, g0.n + 1) if g0.known() else bass.ds(g0.n, 1)
                            for w_sb, w_in, done in loads:
                                act.dma_start(w_sb[:, here, :], w_in[:, here, :]).then_inc(done, 16)
                        if g1:
                            wait(act, xn_ready, g1, 1, 1)
                            row_free(act, g1)
                            for k in range(2):
                                last = act.copy(row[:, g1.par, :, k, 0:D], xn[:, g1.par, :, :])
                            last.then_inc(rows_ready, 1)
                            wait(act, low_ready, g1, 1, 1)
                            for r in range(GROUP):
                                last = act.activation(exps[:, r, :], tops[:, r, :], ACT.Exp, bias=low[:, r:r + 1], scale=1.0,
                                                      accum_out=total[:, r:r + 1])
                            last.then_inc(exps_ready, 1)
                        if g0:
                            wait(act, xt_done, g0, 1, 1)
                            wait(act, l_done, g0, 1, -1)
                            act.copy(xnT[:, g0.par, :, :, :].rearrange("p r c t -> p (r c t)"), xt_ps[:, g0.par, :])                               .then_inc(xnT_ready, 1)
                    pipeline(act, groups, 2, step)

                @block.vector
                def _(dve):
                    dve.memset(seen[:, :], 0.0)
                    dve.memset(tops[:, :, :], NEG_INF)
                    dve.memset(nothing[:, :], 0.0).then_inc(prepared, 1)
                    dve.wait_ge(prepared, 1)
                    dve.wait_ge(r_loaded, 16 * 8)
                    experts = falling[:, :].unsqueeze(1).to_broadcast(shape)

                    def over_experts(t):
                        return t.unsqueeze(2).to_broadcast(shape)

                    def normalise(g):
                        if not g:
                            return
                        dve.wait_ge(x_loaded[g.par], (g.n + (2 - g.par)) * 8)
                        for r in range(GROUP):
                            column = bass.ds(g.n * GROUP + r, 1)
                            last = dve.tensor_scalar(xn[:, g.par, r, :], xn[:, g.par, r, :], mean[:, column],
                                                     rstd[:, column], ALU.subtract, ALU.mult)
                        last.then_inc(xn_ready, 1)

                    def step(at):
                        g0, g1 = at(0), at(1)
                        if g1:
                            done = [0]

                            def link(instruction):
                                done[0] += 1
                                instruction.then_inc(route_step, 1)
                                wait(dve, route_step, g1, ROUTE_STEPS, done[0])

                            def largest(scores, k):
                                top = tops[:, :, k]
                                link(dve.tensor_reduce(top, scores[:, :, :], AX.X, ALU.max))
                                link(dve.tensor_tensor(equal[:, :, :], scores[:, :, :], over_experts(top), ALU.is_equal))
                                link(dve.tensor_tensor(equal[:, :, :], equal[:, :, :], experts, ALU.mult))
                                link(dve.tensor_reduce(key[:, :], equal[:, :, :], AX.X, ALU.max))
                                link(dve.tensor_tensor(hot[:, k, :, :], experts, over_experts(key[:, :]), ALU.is_equal))

                            wait(dve, l_done, g1, 1, 1)
                            wait(dve, exps_ready, g1, 1, 0)
                            link(dve.tensor_tensor(logits[:, :, :],
                                                   l_ps[:, g1.par, 0:GROUP * EXPERTS].rearrange("p (r e) -> p r e", r=GROUP),
                                                   br[:, :].unsqueeze(1).to_broadcast(shape), ALU.add))
                            largest(logits, 0)
                            link(dve.scalar_tensor_tensor(out=rest[:, :, :], in0=hot[:, 0, :, :], scalar=-3.0e38,
                                                          in1=logits[:, :, :], op0=ALU.mult, op1=ALU.add))
                            largest(rest, 1)
                            dve.tensor_tensor(chosen[:, :, :], hot[:, 0, :, :], hot[:, 1, :, :], ALU.add)\
                                .then_inc(chosen_ready, 1)
                            dve.tensor_scalar(low[:, :], tops[:, :, 0], NEG_INF, -1.0, ALU.max, ALU.mult)\
                                .then_inc(low_ready, 1)
                            normalise(g0)
                            wait(dve, rank_done, g1, 1, 1)
                            link(dve.tensor_tensor(place[:, :, :],
                                                   rank_ps[:, 0:GROUP * EXPERTS].rearrange("p (r e) -> p r e", r=GROUP),
                                                   base[:, :].unsqueeze(1).to_broadcast(shape), ALU.add))
                            for r in range(GROUP):
                                link(dve.tensor_tensor(seen[:, :], seen[:, :], chosen[:, r, :], ALU.add))
                            link(dve.tensor_tensor(mine[:, :, :, :], hot[:, :, :, :],
                                                   place[:, :, :].unsqueeze(1).to_broadcast([P, 2, GROUP, EXPERTS]), ALU.mult))
                            link(dve.tensor_reduce(slot[:, :, :], mine[:, :, :, :], AX.X, ALU.add))
                            row_free(dve, g1)
                            link(dve.tensor_copy(index[:, g1.par, :, :], slot[:, :, :]))
                            wait(dve, token_ready, g1, 1, 1)
                            link(dve.tensor_copy(row[:, g1.par, :, :, D + 1],
                                                 numbers[:, g1.par, :].unsqueeze(2).to_broadcast([P, GROUP, 2])))
                            wait(dve, exps_ready, g1, 1, 1)
                            link(dve.reciprocal(total[:, :], total[:, :]))
                            link(dve.tensor_tensor(row[:, g1.par, :, :, D], exps[:, :, 0:2],
                                                   total[:, :].unsqueeze(2).to_broadcast([P, GROUP, 2]), ALU.mult))
                            while done[0] < ROUTE_STEPS:
                                dve.sem_inc(route_step, 1)
                                done[0] += 1
                            dve.sem_inc(index_ready, 1)
                        else:
                            normalise(g0)
                    pipeline(dve, groups, 2, step)

                @block.gpsimd
                def _(pool):
                    pool.wait_ge(r_loaded, 16 * 8)
                    pool.wait_ge(prepared, 1)

                    def step(at):
                        g0, g1 = at(0), at(1)
                        if g1:
                            wait(pool, rows_ready, g1, 1, 1)
                            wait(pool, index_ready, g1, 1, 1)
                        if g0:
                            pool.tensor_tensor(numbers[:, g0.par, :], token_no[:, bass.ds(g0.n * GROUP, GROUP)],
                                               nothing[:, :], ALU.add).then_inc(token_ready, 1)
                        if g1:
                            for r in range(GROUP):
                                for k in range(2):
                                    pool.indirect_dma_start(
                                        xg, bass.IndirectOffsetOnAxis(ap=index[:, g1.par, k, r:r + 1], axis=0),
                                        row[:, g1.par, r, k, :], None).then_inc(scattered[g1.par], 16)
                    pipeline(pool, groups, 2, step)
                    for par in range(2):
                        pool.wait_ge(scattered[par], 16 * 2 * GROUP * (groups // 2))

            plan_tiles(nc, route, sb, ps, sem, w_dram, base, seen, ones, pad_row, tile_expert, tile_row, tiles, part)

        with ExitStack() as work:
            b2 = sb("b2", [P, EXPERTS * D], where=work)
            x_t = sb("e_x_t", [P, 2, WIDE], where=work)
            y, y_s = sb("e_y", [P, 2, D], where=work), sb("e_y_s", [P, 2, D], where=work)
            share, number = sb("e_share", [P, 2], where=work), sb("e_number", [P, 2], where=work)
            token = sb("e_token", [P, 2], I32, where=work)
            xT = sb("e_xT", [P, 2, DC, P], where=work)
            h = sb("e_h", [P, HID], where=work)
            h_b, hT = sb("e_h_b", [P, HC, P], where=work), sb("e_hT", [P, HC, P], where=work)
            x_ps, y_ps = ps("e_x", [P, 512], work), ps("e_y", [P, 512], work)
            h_ps, ht_ps = ps("e_h", [P, 2, 512], work), ps("e_ht", [P, 2, 4, P], work)
            x_loaded = [sem("e_x_loaded0"), sem("e_x_loaded1")]
            added = sem.kept("e_added")
            share_ready, scaled = sem("e_share_ready"), sem("e_scaled")
            xt_done, xT_ready, h_done, h_ready, ht_done, hb_ready, hT_ready, y_done, y_ready = (
                sem(f"e_{n}") for n in ("xt_done", "xT_ready", "h_done", "h_ready", "ht_done", "hb_ready",
                                        "hT_ready", "y_done", "y_ready"))

            def expert_of(eng, t):
                column = tile_expert[0:1, t.n:t.n + 1] if t.known() else tile_expert[0:1, bass.ds(t.n, 1)]
                return eng.value_load(column, min_val=0, max_val=EXPERTS - 1)

            with nc.Block() as block:
                @block.sync
                def _(sp):
                    for e in range(EXPERTS):
                        first = sp.value_load(pad_row[0:1, e:e + 1], min_val=0, max_val=EXPERTS * part - P)
                        sp.dma_start(xg[bass.ds(first, P)], padding[:, :]).then_inc(padded, 16)
                    sp.wait_ge(padded, 16 * (EXPERTS + 1))

                    def step(at):
                        t = at(0)
                        if t:
                            column = tile_row[0:1, t.n:t.n + 1] if t.known() else tile_row[0:1, bass.ds(t.n, 1)]
                            first = sp.value_load(column, min_val=0, max_val=EXPERTS * (part + P) - P)
                            wait(sp, xt_done, t, 1, -1)
                            wait(sp, share_ready, t, 1, -1)
                            sp.dma_start(x_t[:, t.par, :], xg[bass.ds(first, P)]).then_inc(x_loaded[t.par], 16)
                    pipeline(sp, tiles, 1, step)

                @block.tensor
                def _(pe):
                    def h_transpose(t, j):
                        wait(pe, h_ready, t, 2, j + 1)
                        wait(pe, hb_ready, t, 2, j - 1)
                        for c in range(4):
                            col = P * (4 * j + c)
                            last = pe.transpose(ht_ps[:, j, c, :], h[:, col:col + P], ident[:, :])
                        last.then_inc(ht_done, 1)

                    pe.wait_ge(w1_loaded, 16 * groups)
                    pe.wait_ge(w2_loaded, 16 * groups)

                    def step(at):
                        t0, t1 = at(0), at(1)
                        if t0:
                            e0 = expert_of(pe, t0)
                        if t0:
                            pe.wait_ge(x_loaded[t0.par], (t0.n + (2 - t0.par)) * 8)
                            wait(pe, xT_ready, t0, 1, 0)
                            for c in range(DC):
                                last = pe.transpose(x_ps[:, P * c:P * c + P], x_t[:, t0.par, P * c:P * c + P], ident[:, :])
                            last.then_inc(xt_done, 1)
                        if t1:
                            h_transpose(t1, 0)
                        if t1:
                            h_transpose(t1, 1)
                        if t0:
                            wait(pe, xT_ready, t0, 1, 1)
                            for j in range(2):
                                wait(pe, h_ready, t0, 2, j - 1)
                                for c in range(DC):
                                    last = pe.matmul(h_ps[:, j, :], xT[:, t0.par, c, :],
                                                     w1[:, bass.ds(e0, 1), c, 512 * j:512 * j + 512].rearrange("p a n -> p (a n)"),
                                                     start=(c == 0), stop=(c == DC - 1))
                                last.then_inc(h_done, 1)
                        if t1:
                            e1 = expert_of(pe, t1)
                            wait(pe, hT_ready, t1, 2, 2)
                            wait(pe, y_ready, t1, 1, 0)
                            for c in range(HC):
                                last = pe.matmul(y_ps[:, 0:D], hT[:, c, :],
                                                 w2[:, bass.ds(e1, 1), c, :].rearrange("p a n -> p (a n)"),
                                                 start=(c == 0), stop=(c == HC - 1))
                            last.then_inc(y_done, 1)
                    pipeline(pe, tiles, 2, step)

                @block.scalar
                def _(act):
                    act.dma_start(b2[:, :], w_dram["b2"]).then_inc(b_loaded, 16)
                    for weights_ahead in ahead:
                        weights_ahead.start(act)

                    def step(at):
                        t0, t1 = at(0), at(1)
                        if t0:
                            wait(act, xt_done, t0, 1, 1)
                            wait(act, h_done, t0, 2, -2)
                            act.copy(xT[:, t0.par, :, :], x_ps[:, 0:D].rearrange("p (c t) -> p c t", c=DC))\
                               .then_inc(xT_ready, 1)
                        if t1:
                            for j in range(2):
                                wait(act, hb_ready, t1, 2, j + 1)
                                wait(act, y_done, t1, 1, 0)
                                act.activation(hT[:, 4 * j:4 * j + 4, :], h_b[:, 4 * j:4 * j + 4, :], ACT.Relu)\
                                   .then_inc(hT_ready, 1)
                        if t0:
                            for j in range(2):
                                wait(act, h_done, t0, 2, j + 1)
                                wait(act, ht_done, t0, 2, 0)
                                act.copy(h[:, 512 * j:512 * j + 512], h_ps[:, j, :]).then_inc(h_ready, 1)
                    pipeline(act, tiles, 2, step)

                @block.vector
                def _(dve):
                    dve.wait_ge(b_loaded, 32)

                    def step(at):
                        t0, t1 = at(0), at(1)
                        if t0:
                            dve.wait_ge(x_loaded[t0.par], (t0.n + (2 - t0.par)) * 8)
                            wait(dve, scaled, t0, 1, -1)
                            dve.tensor_copy(share[:, t0.par:t0.par + 1], x_t[:, t0.par, D:D + 1])
                            dve.tensor_copy(number[:, t0.par:t0.par + 1], x_t[:, t0.par, D + 1:WIDE]).then_inc(share_ready, 1)
                        if t1:
                            e1 = expert_of(dve, t1)
                            for j in range(2):
                                wait(dve, ht_done, t1, 2, j + 1)
                                wait(dve, hT_ready, t1, 2, j - 1)
                                dve.tensor_tensor(h_b[:, 4 * j:4 * j + 4, :], ht_ps[:, j, :, :],
                                                  b1[:, bass.ds(e1 * HC + 4 * j, 4)].unsqueeze(2).to_broadcast([P, 4, P]),
                                                  ALU.add).then_inc(hb_ready, 1)
                            wait(dve, added, t1, 16, -16)
                            wait(dve, share_ready, t1, 1, 1)
                            dve.tensor_copy(token[:, t1.par:t1.par + 1], number[:, t1.par:t1.par + 1])
                            wait(dve, scaled, t1, 1, -1)
                            wait(dve, y_done, t1, 1, 1)
                            dve.tensor_tensor(y[:, t1.par, :], y_ps[:, 0:D], b2[:, bass.ds(e1 * D, D)], ALU.add)\
                                .then_inc(y_ready, 1)
                    pipeline(dve, tiles, 2, step)

                @block.gpsimd
                def _(pool):
                    pool.wait_ge(spare_ready, 16)

                    def step(at):
                        t1, t2 = at(1), at(2)
                        if t2:
                            wait(pool, scaled, t2, 1, 1)
                            wait(pool, added, t2, 16, 0)
                        if t1:
                            wait(pool, share_ready, t1, 1, 1)
                            wait(pool, y_ready, t1, 1, 1)
                            pool.tensor_tensor(y_s[:, t1.par, :], y[:, t1.par, :],
                                               share[:, t1.par:t1.par + 1].to_broadcast([P, D]), ALU.mult)\
                                .then_inc(scaled, 1)
                        if t2:
                            pool.indirect_dma_start(
                                x.rearrange("b p d -> (b p) d"),
                                bass.IndirectOffsetOnAxis(ap=token[:, t2.par:t2.par + 1], axis=0),
                                y_s[:, t2.par, :], None, compute_op=ALU.add).then_inc(added, 16)
                    pipeline(pool, tiles, 3, step)
                    pool.wait_ge(added, 16 * tiles)
        sem.clear()


def plan_tiles(nc, where, sb, ps, sem, w_dram, base, seen, ones, pad_row, tile_expert, tile_row, tiles, part):
    tile_no = sb("tile_no", [1, tiles], where=where)
    counts, n_tiles, end_a, end_b, pad = (sb(n, [P, EXPERTS], where=where) for n in (
        "counts", "n_tiles", "end_a", "end_b", "pad"))
    passed, weighed = (sb(n, [1, tiles, EXPERTS], where=where) for n in ("passed", "weighed"))
    number, started, number_7 = (sb(n, [1, tiles], where=where) for n in ("number", "started", "number_7"))
    count_ps = ps("count", [P, 512], where)
    loaded, plan_step, counted = (sem(f"plan_{n}") for n in ("loaded", "step", "counted"))
    shape = [1, tiles, EXPERTS]

    with nc.Block() as block:
        @block.sync
        def _(sp):
            sp.dma_start(tile_no[:, :], w_dram["tile_no"]).then_inc(loaded, 16)

        @block.tensor
        def _(pe):
            pe.matmul(count_ps[:, 0:EXPERTS], ones[:, :], seen[:, :], start=True, stop=True).then_inc(counted, 1)

        @block.vector
        def _(dve):
            link = chained(dve, plan_step)
            dve.wait_ge(loaded, 16)
            dve.wait_ge(counted, 1)
            link(dve.tensor_copy(counts[:, :], count_ps[:, 0:EXPERTS]))
            link(dve.tensor_tensor(pad[:, :], counts[:, :], base[:, :], ALU.add))
            link(dve.tensor_copy(pad_row[:, :], pad[0:1, :]))
            link(dve.tensor_scalar(n_tiles[:, :], counts[:, :], 1.0 / P, (P - 1) / P - 0.5 + 0.5 / P, ALU.mult, ALU.add))
            link(dve.tensor_scalar(n_tiles[:, :], n_tiles[:, :], ROUNDER, ROUNDER, ALU.add, ALU.subtract))
            link(dve.tensor_copy(end_a[:, :], n_tiles[:, :]))
            end, other, shift = end_a, end_b, 1
            while shift < EXPERTS:
                link(dve.tensor_copy(other[:, 0:shift], end[:, 0:shift]))
                link(dve.tensor_tensor(other[:, shift:], end[:, shift:], end[:, :EXPERTS - shift], ALU.add))
                end, other, shift = other, end, 2 * shift
            link(dve.tensor_tensor(passed[:, :, :], end[0:1, :].unsqueeze(1).to_broadcast(shape),
                                   tile_no[:, :].unsqueeze(2).to_broadcast(shape), ALU.is_le))
            link(dve.tensor_reduce(number[:, :], passed[:, :, :], AX.X, ALU.add))
            link(dve.tensor_tensor(weighed[:, :, :], passed[:, :, :], n_tiles[0:1, :].unsqueeze(1).to_broadcast(shape), ALU.mult))
            link(dve.tensor_reduce(started[:, :], weighed[:, :, :], AX.X, ALU.add))
            link(dve.tensor_scalar(number_7[:, :], number[:, :], float(EXPERTS - 1), None, ALU.min))
            link(dve.tensor_copy(tile_expert[:, :], number_7[:, :]))
            link(dve.tensor_tensor(started[:, :], tile_no[:, :], started[:, :], ALU.subtract))
            link(dve.tensor_scalar(started[:, :], started[:, :], float(P), None, ALU.mult))
            link(dve.scalar_tensor_tensor(out=started[:, :], in0=number[:, :], scalar=float(part), in1=started[:, :],
                                          op0=ALU.mult, op1=ALU.add))
            link(dve.tensor_copy(tile_row[:, :], started[:, :]))


RES = float(1.0 / np.sqrt(2.0))
CHUNK = 64
RMS_EPS = 1e-6
Q_EPS = float(np.finfo(np.float32).eps)


def mixer(nc, x_in, x_out, stats, mean, rstd, scale, ident, weights, ahead=(), count=NB):
    name = "mix"
    with ExitStack() as ctx:
        def sb(n, shape, dt=F32):
            return ctx.enter_context(nc.sbuf_tensor(f"{name}_{n}", shape, dt))

        def ps(n, shape):
            return ctx.enter_context(nc.psum_tensor(f"{name}_{n}", shape, F32))

        sem = Semaphores(nc, ctx, name)

        w_in, w_out, w_fc, w_pr, norm1, norm2 = (
            weights[key] for key in ("w_in", "w_out", "w_fc", "w_pr", "norm1", "norm2"))
        x_t, x_again, x_ln, h_n, x_1, x_s, h2_n, x_o, junk = (
            sb(n, [P, 2, D]) for n in ("x_t", "x_again", "x_ln", "h_n", "x_1", "x_s", "h2_n", "x_o", "junk"))
        hT, h2T, vT, kT, uT, aT, gT, prefix, inv_prefix, accT, memT, zT, yT = (
            sb(n, [P, 2, DC, P]) for n in ("hT", "h2T", "vT", "kT", "uT", "aT", "gT", "prefix", "inv_prefix",
                                           "accT", "memT", "zT", "yT"))
        q_t, q_sq, q_n = (sb(n, [P, 2, D]) for n in ("q_t", "q_sq", "q_n"))
        q_ms, q_r = sb("q_ms", [P, 2, HEADS]), sb("q_r", [P, 2, HEADS])
        x_ms, x_r = sb("x_ms", [P, 2]), sb("x_r", [P, 2])
        ones, consts = sb("ones", [P, CHUNK]), sb("consts", [P, 4])
        t_fc = sb("t_fc", [P, 2, 512])
        sT = sb("sT", [P, 2, HC, P])
        f_ps = [ps("f0", [P, 512]), ps("f1", [P, 512])]
        kv_ps, ag_ps, q_ps, t_ps, o_ps, m_ps = (ps(n, [P, 512]) for n in ("kv", "ag", "q", "t", "o", "m"))

        folded, const_ready = sem("folded"), sem("const_ready")
        x_loaded = [sem("x_loaded0"), sem("x_loaded1")]
        again_loaded = [sem("again_loaded0"), sem("again_loaded1")]
        stored = [sem.kept("stored0"), sem.kept("stored1")]
        h_ready, tx_done, hT_ready = sem("h_ready"), sem("tx_done"), sem("hT_ready")
        q_done, q_copied, qsq_ready, qms_ready, qr_ready, qn_ready, qt_done = (
            sem(n) for n in ("q_done", "q_copied", "qsq_ready", "qms_ready", "qr_ready", "qn_ready", "qt_done"))
        kv_done, kv_ready, ag_done, ag_ready, u_ready = (
            sem(n) for n in ("kv_done", "kv_ready", "ag_done", "ag_ready", "u_ready"))
        scan_step, y_ready, out_done, x1_ready, ms_ready, xr_ready, xs_ready = (
            sem(n) for n in ("scan_step", "y_ready", "out_done", "x1_ready", "ms_ready", "xr_ready", "xs_ready"))
        h2_ready, h2t_done, h2T_ready = sem("h2_ready"), sem("h2t_done"), sem("h2T_ready")
        fc_done, tanh_ready, s_ready, pr_done, xo_ready = (
            sem(n) for n in ("fc_done", "tanh_ready", "s_ready", "pr_done", "xo_ready"))
        half_ready, xr_step, clip_step, qr_step = (sem(n) for n in ("half_ready", "xr_step", "clip_step", "qr_step"))
        z_ready, gated = sem("z_ready"), sem("gated")
        ctx.callback(sem.clear)
        block = ctx.enter_context(nc.Block())

        def loaded(eng, sems, b):
            eng.wait_ge(sems[b.par], (b.n + (2 - b.par)) * 8)

        @block.sync
        def _(sp):

            def step(at):
                b0, b1, b3 = at(0), at(1), at(3)
                if b0:
                    wait(sp, h_ready, b0, 1, -1)
                    sp.dma_start(x_t[:, b0.par, :], x_in[b0.n]).then_inc(x_loaded[b0.par], 16)
                if b1:
                    wait(sp, xs_ready, b1, 1, -1)
                    sp.dma_start(x_again[:, b1.par, :], x_in[b1.n]).then_inc(again_loaded[b1.par], 16)
                if b3:
                    wait(sp, xo_ready, b3, 1, 1)
                    sp.dma_start(x_out[b3.n], x_o[:, b3.par, :]).then_inc(stored[b3.par], 16)
            pipeline(sp, count, 4, step)
            for par in range(2):
                sp.wait_ge(stored[par], 16 * (count // 2))

        @block.tensor
        def _(pe):
            pe.wait_ge(folded, 2)

            def transposes(src, b, done):
                for c in range(DC):
                    last = pe.transpose(t_ps[:, P * c:P * c + P], src[:, b.par, P * c:P * c + P], ident[:, :])
                last.then_inc(done, 1)

            def channels(b, bank, part0, parts, done):
                for m in range(parts * DC):
                    col = part0 * D + P * m
                    for c in range(DC):
                        last = pe.matmul(bank[:, P * m:P * m + P], w_in[:, c, col:col + P],
                                         hT[:, b.par, c, :], start=(c == 0), stop=(c == DC - 1))
                last.then_inc(done, 1)

            def hidden(b, j):
                wait(pe, h2T_ready, b, 1, 1)
                wait(pe, s_ready, b, 2, j - 1)
                for m in range(4):
                    for c in range(DC):
                        last = pe.matmul(f_ps[j][:, P * m:P * m + P],
                                         w_fc[:, c, 512 * j + P * m:512 * j + P * m + P],
                                         h2T[:, b.par, c, :], start=(c == 0), stop=(c == DC - 1))
                last.then_inc(fc_done, 1)

            def project(b, j):
                wait(pe, s_ready, b, 2, j + 1)
                if j == 0:
                    wait(pe, xo_ready, b, 1, 0)
                for c in range(4 * j, 4 * j + 4):
                    last = pe.matmul(m_ps[:, 0:D], sT[:, b.par, c, :], w_pr[:, c, :],
                                     start=(c == 0), stop=(c == HC - 1))
                if j == 1:
                    last.then_inc(pr_done, 1)

            def step(at):
                b0, b1, b2, b3 = at(0), at(1), at(2), at(3)
                if b3:
                    project(b3, 0)
                if b2:
                    wait(pe, h2_ready, b2, 1, 1)
                    wait(pe, z_ready, b2, 1, 1)
                    transposes(h2_n, b2, h2t_done)
                if b3:
                    project(b3, 1)
                if b0:
                    wait(pe, h_ready, b0, 1, 1)
                    if b2:
                        wait(pe, h2T_ready, b2, 1, 1)
                    transposes(h_n, b0, tx_done)
                if b2:
                    hidden(b2, 0)
                if b1:
                    wait(pe, qn_ready, b1, 1, 1)
                    if b0:
                        wait(pe, hT_ready, b0, 1, 1)
                    transposes(q_n, b1, qt_done)
                if b2:
                    hidden(b2, 1)
                if b0:
                    wait(pe, hT_ready, b0, 1, 1)
                    wait(pe, q_copied, b0, 1, 0)
                    for c in range(DC):
                        last = pe.matmul(q_ps[:, 0:D], hT[:, b0.par, c, :], w_in[:, c, 0:D],
                                         start=(c == 0), stop=(c == DC - 1))
                    last.then_inc(q_done, 1)
                    wait(pe, kv_ready, b0, 1, 0)
                    channels(b0, kv_ps, 1, 2, kv_done)
                if b1:
                    wait(pe, y_ready, b1, 1, 1)
                    wait(pe, x1_ready, b1, 1, 0)
                    for c in range(DC):
                        last = pe.matmul(o_ps[:, 0:D], yT[:, b1.par, c, :], w_out[:, c, :],
                                         start=(c == 0), stop=(c == DC - 1))
                    last.then_inc(out_done, 1)
                if b0:
                    wait(pe, ag_ready, b0, 1, 0)
                    channels(b0, ag_ps, 3, 2, ag_done)
            pipeline(pe, count, 4, step)

        @block.scalar
        def _(act):
            for weights_ahead in ahead:
                weights_ahead.start(act)

            def step(at):
                b0, b1, b2 = at(0), at(1), at(2)
                if b2:
                    wait(act, h2t_done, b2, 1, 1)
                    wait(act, fc_done, b2, 2, -2)
                    act.copy(h2T[:, b2.par, :, :], t_ps[:, 0:D].rearrange("p (c t) -> p c t", c=DC))\
                       .then_inc(h2T_ready, 1)
                if b0:
                    wait(act, tx_done, b0, 1, 1)
                    wait(act, ag_done, b0, 1, -1)
                    act.copy(hT[:, b0.par, :, :], t_ps[:, 0:D].rearrange("p (c t) -> p c t", c=DC))\
                       .then_inc(hT_ready, 1)
                if b2:
                    for j in range(2):
                        wait(act, fc_done, b2, 2, j + 1)
                        wait(act, s_ready, b2, 2, j - 1)
                        act.activation(t_fc[:, j, :], f_ps[j][:, :], ACT.Tanh, scale=0.5).then_inc(tanh_ready, 1)
                if b0:
                    wait(act, q_done, b0, 1, 1)
                    wait(act, qn_ready, b0, 1, -1)
                    act.copy(q_t[:, b0.par, :], q_ps[:, 0:D]).then_inc(q_copied, 1)
                    wait(act, kv_done, b0, 1, 1)
                    wait(act, u_ready, b0, 1, -1)
                    wait(act, y_ready, b0, 1, -1)
                    act.activation(kT[:, b0.par, :, :], kv_ps[:, 0:D].rearrange("p (c t) -> p c t", c=DC), ACT.Tanh)
                    act.copy(vT[:, b0.par, :, :], kv_ps[:, D:2 * D].rearrange("p (c t) -> p c t", c=DC))\
                       .then_inc(kv_ready, 1)
                if b1:
                    wait(act, x1_ready, b1, 1, 1)
                    wait(act, xr_ready, b1, 1, -1)
                    act.activation(junk[:, b1.par, :], x_1[:, b1.par, :], ACT.Square, scale=D ** -0.5,
                                   accum_out=x_ms[:, b1.par:b1.par + 1]).then_inc(ms_ready, 1)
                if b0:
                    wait(act, ag_done, b0, 1, 1)
                    wait(act, scan_step, b0, 9, 1 - 18)
                    act.activation(aT[:, b0.par, :, :], ag_ps[:, 0:D].rearrange("p (c t) -> p c t", c=DC),
                                   ACT.Tanh, bias=one_col[:, :], scale=0.5)
                    act.activation(gT[:, b0.par, :, :], ag_ps[:, D:2 * D].rearrange("p (c t) -> p c t", c=DC),
                                   ACT.Tanh, scale=0.5).then_inc(ag_ready, 1)
            one_col = ones[:, 0:1]
            act.wait_ge(const_ready, 1)
            pipeline(act, count, 3, step)

        @block.vector
        def _(dve):
            dve.memset(ones[:, :], 1.0).then_inc(const_ready, 1)
            weights.wait(dve)
            for c in range(DC):
                dve.tensor_scalar(w_in[:, c, :], w_in[:, c, :], norm1[:, c:c + 1], None, ALU.mult)
                last = dve.tensor_scalar(w_fc[:, c, :], w_fc[:, c, :], norm2[:, c:c + 1], None, ALU.mult)
                last.then_inc(folded, 1)
            dve.wait_ge(folded, 2)
            STEPS = 9

            def step(at):
                b0, b1, b2, b3 = at(0), at(1), at(2), at(3)
                if b0:
                    loaded(dve, x_loaded, b0)
                    wait(dve, tx_done, b0, 1, -1)
                    dve.tensor_scalar(h_n[:, b0.par, :], x_t[:, b0.par, :], mean[:, bass.ds(b0.n, 1)],
                                      scale[:, bass.ds(b0.n, 1)], ALU.subtract, ALU.mult)
                    dve.tensor_scalar(x_ln[:, b0.par, :], x_t[:, b0.par, :], mean[:, bass.ds(b0.n, 1)],
                                      rstd[:, bass.ds(b0.n, 1)], ALU.subtract, ALU.mult).then_inc(h_ready, 1)
                if b1:
                    wait(dve, ag_ready, b1, 1, 1)
                    dve.tensor_scalar(aT[:, b1.par, :, :], aT[:, b1.par, :, :], 0.5, 0.5, ALU.mult, ALU.add)\
                       .then_inc(clip_step, 1)
                    wait(dve, clip_step, b1, 2, 1)
                    dve.tensor_scalar(aT[:, b1.par, :, :], aT[:, b1.par, :, :], 0.9995, 0.6, ALU.min, ALU.max)\
                       .then_inc(clip_step, 1)
                    wait(dve, clip_step, b1, 2, 2)
                    for c in range(DC):
                        for s in range(P // CHUNK):
                            part = slice(CHUNK * s, CHUNK * s + CHUNK)
                            last = dve.tensor_tensor_scan(prefix[:, b1.par, c, part], aT[:, b1.par, c, part],
                                                          ones[:, :], 1.0, ALU.mult, ALU.mult)
                    last.then_inc(scan_step, 1)
                    wait(dve, scan_step, b1, STEPS, 1)
                    dve.tensor_scalar(inv_prefix[:, b1.par, :, :], prefix[:, b1.par, :, :], 1e-6, None, ALU.max)\
                       .then_inc(scan_step, 1)
                    wait(dve, scan_step, b1, STEPS, 2)
                    dve.reciprocal(inv_prefix[:, b1.par, :, :], inv_prefix[:, b1.par, :, :]).then_inc(scan_step, 1)
                    wait(dve, qr_ready, b1, 1, 1)
                    wait(dve, qt_done, b1, 1, -1)
                    dve.tensor_tensor(q_n[:, b1.par, :].rearrange("p (h d) -> p h d", h=HEADS),
                                      q_t[:, b1.par, :].rearrange("p (h d) -> p h d", h=HEADS),
                                      q_r[:, b1.par, :].unsqueeze(2).to_broadcast([P, HEADS, HD]),
                                      ALU.mult).then_inc(qn_ready, 1)
                    wait(dve, scan_step, b1, STEPS, 3)
                    wait(dve, u_ready, b1, 1, 1)
                    dve.tensor_tensor(inv_prefix[:, b1.par, :, :], inv_prefix[:, b1.par, :, :],
                                      uT[:, b1.par, :, :], ALU.mult).then_inc(scan_step, 1)
                    wait(dve, scan_step, b1, STEPS, 4)
                if b3:
                    wait(dve, pr_done, b3, 1, 1)
                    wait(dve, xs_ready, b3, 1, 1)
                    if not b3.known() or b3.n >= 2:
                        dve.wait_ge(stored[b3.par], (b3.n - b3.par) * 8)
                    dve.scalar_tensor_tensor(out=x_o[:, b3.par, :], in0=m_ps[:, 0:D], scalar=0.5 * RES,
                                             in1=x_s[:, b3.par, :], op0=ALU.mult, op1=ALU.add)\
                       .then_inc(xo_ready, 1)
                    wait(dve, xo_ready, b3, 1, 1)
                    dve.bn_stats(stats[:, b3.n, :], x_o[:, b3.par, :])
                if b1:
                    for s in range(P // CHUNK):
                        part = slice(CHUNK * s, CHUNK * s + CHUNK)
                        for c in range(DC):
                            first = 0.0 if s == 0 else memT[:, b1.par, c, CHUNK * s - 1:CHUNK * s]
                            last = dve.tensor_tensor_scan(accT[:, b1.par, c, part], ones[:, :],
                                                          inv_prefix[:, b1.par, c, part], first,
                                                          ALU.mult, ALU.add)
                        last.then_inc(scan_step, 1)
                        wait(dve, scan_step, b1, STEPS, 5 + 2 * s)
                        dve.tensor_tensor(memT[:, b1.par, :, part], accT[:, b1.par, :, part],
                                          prefix[:, b1.par, :, part], ALU.mult).then_inc(scan_step, 1)
                        wait(dve, scan_step, b1, STEPS, 6 + 2 * s)
                    wait(dve, qt_done, b1, 1, 1)
                    dve.tensor_tensor(zT[:, b1.par, :, :], t_ps[:, 0:D].rearrange("p (c t) -> p c t", c=DC),
                                      memT[:, b1.par, :, :], ALU.mult).then_inc(z_ready, 1)
                    wait(dve, z_ready, b1, 1, 1)
                    dve.tensor_tensor(zT[:, b1.par, :, :], zT[:, b1.par, :, :], vT[:, b1.par, :, :],
                                      ALU.subtract).then_inc(scan_step, 1)
                    wait(dve, scan_step, b1, STEPS, 9)
                    wait(dve, out_done, b1, 1, -1)
                    dve.scalar_tensor_tensor(out=zT[:, b1.par, :, :], in0=gT[:, b1.par, :, :], scalar=1.0,
                                             in1=zT[:, b1.par, :, :], op0=ALU.add, op1=ALU.mult)\
                       .then_inc(gated, 1)
                    wait(dve, gated, b1, 1, 1)
                    dve.scalar_tensor_tensor(out=yT[:, b1.par, :, :], in0=zT[:, b1.par, :, :], scalar=0.5,
                                             in1=vT[:, b1.par, :, :], op0=ALU.mult, op1=ALU.add)\
                       .then_inc(y_ready, 1)
                if b2:
                    for j in range(2):
                        wait(dve, tanh_ready, b2, 2, j + 1)
                        wait(dve, pr_done, b2, 1, -1)
                        dve.scalar_tensor_tensor(
                            out=sT[:, b2.par, 4 * j:4 * j + 4, :].rearrange("p c t -> p (c t)"),
                            in0=t_fc[:, j, :], scalar=1.0, in1=f_ps[j][:, :],
                            op0=ALU.add, op1=ALU.mult).then_inc(s_ready, 1)
                if b1:
                    wait(dve, out_done, b1, 1, 1)
                    wait(dve, xs_ready, b1, 1, -1)
                    wait(dve, ms_ready, b1, 1, -1)
                    dve.scalar_tensor_tensor(out=x_1[:, b1.par, :], in0=o_ps[:, 0:D], scalar=RES,
                                             in1=x_ln[:, b1.par, :], op0=ALU.mult, op1=ALU.add)\
                       .then_inc(x1_ready, 1)
                if b0:
                    wait(dve, q_copied, b0, 1, 1)
                    dve.tensor_tensor(q_sq[:, b0.par, :], q_t[:, b0.par, :], q_t[:, b0.par, :], ALU.mult)\
                       .then_inc(qsq_ready, 1)
                    wait(dve, qsq_ready, b0, 1, 1)
                    wait(dve, qr_ready, b0, 1, -1)
                    dve.tensor_reduce(q_ms[:, b0.par, :], q_sq[:, b0.par, :].rearrange("p (h d) -> p h d", h=HEADS),
                                      AX.X, ALU.add).then_inc(qms_ready, 1)
                if b1:
                    wait(dve, xr_ready, b1, 1, 1)
                    wait(dve, h2t_done, b1, 1, -1)
                    dve.tensor_scalar(h2_n[:, b1.par, :], x_1[:, b1.par, :], x_r[:, b1.par:b1.par + 1],
                                      None, ALU.mult).then_inc(h2_ready, 1)
            pipeline(dve, count, 4, step)

        @block.gpsimd
        def _(pool):
            for i, value in enumerate((-0.5, RMS_EPS, 1.0 / HD, Q_EPS)):
                pool.memset(consts[:, i:i + 1], value).then_inc(half_ready, 1)
            pool.wait_ge(half_ready, 4)

            def step(at):
                b0, b1, b2 = at(0), at(1), at(2)
                if b0:
                    wait(pool, kv_ready, b0, 1, 1)
                    wait(pool, scan_step, b0, 9, 4 - 18)
                    pool.tensor_tensor(uT[:, b0.par, :, :], kT[:, b0.par, :, :], vT[:, b0.par, :, :],
                                       ALU.mult).then_inc(u_ready, 1)
                if b1:
                    wait(pool, ms_ready, b1, 1, 1)
                    wait(pool, h2_ready, b1, 1, -1)
                    pool.tensor_tensor(x_r[:, b1.par:b1.par + 1], x_ms[:, b1.par:b1.par + 1], consts[:, 1:2],
                                       ALU.add).then_inc(xr_step, 1)
                    wait(pool, xr_step, b1, 1, 1)
                    pool.tensor_tensor(x_r[:, b1.par:b1.par + 1], x_r[:, b1.par:b1.par + 1], consts[:, 0:1],
                                       ALU.pow).then_inc(xr_ready, 1)
                    wait(pool, x1_ready, b1, 1, 1)
                    loaded(pool, again_loaded, b1)
                    wait(pool, xo_ready, b1, 1, -1)
                    pool.tensor_tensor(x_s[:, b1.par, :], x_1[:, b1.par, :], x_again[:, b1.par, :], ALU.add)\
                        .then_inc(xs_ready, 1)
                if b0:
                    wait(pool, qms_ready, b0, 1, 1)
                    wait(pool, qn_ready, b0, 1, -1)
                    pool.tensor_tensor(q_r[:, b0.par, :], q_ms[:, b0.par, :],
                                       consts[:, 2:3].to_broadcast([P, HEADS]), ALU.mult).then_inc(qr_step, 1)
                    wait(pool, qr_step, b0, 2, 1)
                    pool.tensor_tensor(q_r[:, b0.par, :], q_r[:, b0.par, :],
                                       consts[:, 3:4].to_broadcast([P, HEADS]), ALU.add).then_inc(qr_step, 1)
                    wait(pool, qr_step, b0, 2, 2)
                    pool.tensor_tensor(q_r[:, b0.par, :], q_r[:, b0.par, :],
                                       consts[:, 0:1].to_broadcast([P, HEADS]), ALU.pow)\
                        .then_inc(qr_ready, 1)
            pipeline(pool, count, 3, step)


def cross_values(nc, x_in, x_out, ctx_in, stats, mean, rstd, ident, weights, count=NB):
    name = "xv"
    with ExitStack() as ctx:
        def sb(n, shape, dt=F32):
            return ctx.enter_context(nc.sbuf_tensor(f"{name}_{n}", shape, dt))

        def ps(n):
            return ctx.enter_context(nc.psum_tensor(f"{name}_ps_{n}", [P, 512], F32))

        sem = Semaphores(nc, ctx, name)

        w_vk, w_lk, w_vv, w_lv, b_vk, b_lk, b_vv, b_lv = (
            weights[key] for key in ("w_vk", "w_lk", "w_vv", "w_lv", "b_vk", "b_lk", "b_vv", "b_lv"))
        x_t, c_t, x_r, xn, vv, lv, x_o = (sb(n, [P, 2, D]) for n in ("x_t", "c_t", "x_r", "xn", "vv", "lv", "x_o"))
        srcT = sb("srcT", [P, 2, 2 * DC, P])
        vkT, lkT = sb("vkT", [P, 2, DC, P]), sb("lkT", [P, 2, DC, P])
        attn, attnT = sb("attn", [P, 2, P]), sb("attnT", [P, 2, P])
        neg_max, total, inv = sb("neg_max", [P, 2]), sb("total", [P, 2]), sb("inv", [P, 2])
        t_ps, vk_ps, lk_ps, vv_ps, s_ps, at_ps, l_ps, o_ps = (ps(n) for n in ("t", "vk", "lk", "vv", "s", "at", "l", "o"))
        x_loaded, c_loaded, r_loaded = ([sem(f"{n}{i}") for i in range(2)] for n in ("x_loaded", "c_loaded", "r_loaded"))
        stored = [sem.kept("stored0"), sem.kept("stored1")]
        xn_ready, t_done, srcT_ready, vk_done, vk_ready, lk_done, lk_ready, vv_done, vv_ready = (
            sem(n) for n in ("xn_ready", "t_done", "srcT_ready", "vk_done", "vk_ready", "lk_done", "lk_ready",
                             "vv_done", "vv_ready"))
        s_done, max_ready, exp_ready, inv_ready, attn_ready, at_done, attnT_ready = (
            sem(n) for n in ("s_done", "max_ready", "exp_ready", "inv_ready", "attn_ready", "at_done", "attnT_ready"))
        l_done, lv_ready, out_done, xo_ready = (sem(n) for n in ("l_done", "lv_ready", "out_done", "xo_ready"))
        ctx.callback(sem.clear)
        block = ctx.enter_context(nc.Block())

        def loaded(eng, sems, b):
            eng.wait_ge(sems[b.par], (b.n + (2 - b.par)) * 8)

        @block.sync
        def _(sp):

            def step(at):
                b = at(0)
                if b:
                    wait(sp, xn_ready, b, 1, -1)
                    sp.dma_start(x_t[:, b.par, :], x_in[b.n]).then_inc(x_loaded[b.par], 16)
                    wait(sp, t_done, b, 1, -1)
                    sp.dma_start(c_t[:, b.par, :], ctx_in[b.n]).then_inc(c_loaded[b.par], 16)
                    wait(sp, xo_ready, b, 1, -1)
                    sp.dma_start(x_r[:, b.par, :], x_in[b.n]).then_inc(r_loaded[b.par], 16)
            pipeline(sp, count, 1, step)
            for par in range(2):
                sp.wait_ge(stored[par], 16 * (count // 2))

        @block.tensor
        def _(pe):
            weights.wait(pe)

            def channels(b, bank, w, chunk0, done):
                for m in range(DC):
                    for c in range(DC):
                        last = pe.matmul(bank[:, P * m:P * m + P], w[:, c, P * m:P * m + P],
                                         srcT[:, b.par, chunk0 + c, :], start=(c == 0), stop=(c == DC - 1))
                last.then_inc(done, 1)

            def step(at):
                b0, b1, b2 = at(0), at(1), at(2)
                if b2:
                    wait(pe, lv_ready, b2, 1, 1)
                    wait(pe, attnT_ready, b2, 1, 1)
                    wait(pe, xo_ready, b2, 1, 0)
                    pe.matmul(o_ps[:, 0:D], attnT[:, b2.par, :], lv[:, b2.par, :], start=True, stop=True)\
                      .then_inc(out_done, 1)
                if b1:
                    wait(pe, vk_ready, b1, 1, 1)
                    wait(pe, lk_ready, b1, 1, 1)
                    wait(pe, exp_ready, b1, 1, 0)
                    for c in range(DC):
                        last = pe.matmul(s_ps[:, 0:P], vkT[:, b1.par, c, :], lkT[:, b1.par, c, :],
                                         start=(c == 0), stop=(c == DC - 1))
                    last.then_inc(s_done, 1)
                if b0:
                    wait(pe, xn_ready, b0, 1, 1)
                    loaded(pe, c_loaded, b0)
                    wait(pe, srcT_ready, b0, 1, 0)
                    for k in range(2 * DC):
                        src = xn if k < DC else c_t
                        last = pe.transpose(t_ps[:, P * k:P * k + P],
                                            src[:, b0.par, P * (k % DC):P * (k % DC) + P], ident[:, :])
                    last.then_inc(t_done, 1)
                if b1:
                    wait(pe, lv_ready, b1, 1, 0)
                    for c in range(DC):
                        pe.matmul(l_ps[:, 0:D], srcT[:, b1.par, DC + c, :], w_lv[:, c, :], start=(c == 0), stop=False)
                if b0:
                    wait(pe, srcT_ready, b0, 1, 1)
                    wait(pe, vk_ready, b0, 1, 0)
                    channels(b0, vk_ps, w_vk, 0, vk_done)
                if b1:
                    wait(pe, attn_ready, b1, 1, 1)
                    wait(pe, attnT_ready, b1, 1, 0)
                    pe.transpose(at_ps[:, 0:P], attn[:, b1.par, :], ident[:, :]).then_inc(at_done, 1)
                    wait(pe, vv_ready, b1, 1, 1)
                    pe.matmul(l_ps[:, 0:D], attn[:, b1.par, :], vv[:, b1.par, :], start=False, stop=True)\
                      .then_inc(l_done, 1)
                if b0:
                    wait(pe, lk_ready, b0, 1, 0)
                    channels(b0, lk_ps, w_lk, DC, lk_done)
                    wait(pe, vv_ready, b0, 1, 0)
                    for c in range(DC):
                        last = pe.matmul(vv_ps[:, 0:D], srcT[:, b0.par, c, :], w_vv[:, c, :],
                                         start=(c == 0), stop=(c == DC - 1))
                    last.then_inc(vv_done, 1)
            pipeline(pe, count, 3, step)

        @block.scalar
        def _(act):
            def step(at):
                b0, b1 = at(0), at(1)
                if b1:
                    wait(act, max_ready, b1, 1, 1)
                    wait(act, at_done, b1, 1, -1)
                    wait(act, l_done, b1, 1, -1)
                    act.activation(attn[:, b1.par, :], s_ps[:, 0:P], ACT.Exp, bias=neg_max[:, b1.par:b1.par + 1],
                                   scale=D ** -0.5, accum_out=total[:, b1.par:b1.par + 1]).then_inc(exp_ready, 1)
                if b0:
                    wait(act, t_done, b0, 1, 1)
                    wait(act, vv_done, b0, 1, -1)
                    wait(act, l_done, b0, 1, -1)
                    act.copy(srcT[:, b0.par, :, :], t_ps[:, :].rearrange("p (c t) -> p c t", c=2 * DC))\
                       .then_inc(srcT_ready, 1)
                if b1:
                    wait(act, at_done, b1, 1, 1)
                    wait(act, out_done, b1, 1, -1)
                    act.copy(attnT[:, b1.par, :], at_ps[:, 0:P]).then_inc(attnT_ready, 1)
            pipeline(act, count, 2, step)

        @block.vector
        def _(dve):
            weights.wait(dve)

            def step(at):
                b0, b1, b2 = at(0), at(1), at(2)
                if b0:
                    loaded(dve, x_loaded, b0)
                    wait(dve, t_done, b0, 1, -1)
                    dve.tensor_scalar(xn[:, b0.par, :], x_t[:, b0.par, :], mean[:, bass.ds(b0.n, 1)],
                                      rstd[:, bass.ds(b0.n, 1)], ALU.subtract, ALU.mult).then_inc(xn_ready, 1)
                if b1:
                    wait(dve, s_done, b1, 1, 1)
                    wait(dve, exp_ready, b1, 1, -1)
                    dve.tensor_reduce(neg_max[:, b1.par:b1.par + 1], s_ps[:, 0:P], AX.X, ALU.max, negate=True)\
                       .then_inc(inv_ready, 1)
                    wait(dve, inv_ready, b1, 2, 1)
                    dve.tensor_scalar(neg_max[:, b1.par:b1.par + 1], neg_max[:, b1.par:b1.par + 1], D ** -0.5, None,
                                      ALU.mult).then_inc(max_ready, 1)
                if b2:
                    wait(dve, out_done, b2, 1, 1)
                    loaded(dve, r_loaded, b2)
                    if not b2.known() or b2.n >= 2:
                        dve.wait_ge(stored[b2.par], (b2.n - b2.par) * 8)
                    dve.tensor_tensor(x_o[:, b2.par, :], o_ps[:, 0:D], x_r[:, b2.par, :], ALU.add)\
                       .then_inc(xo_ready, 1)
                    wait(dve, xo_ready, b2, 1, 1)
                    dve.bn_stats(stats[:, b2.n, :], x_o[:, b2.par, :])
                if b1:
                    wait(dve, exp_ready, b1, 1, 1)
                    dve.reciprocal(inv[:, b1.par:b1.par + 1], total[:, b1.par:b1.par + 1]).then_inc(inv_ready, 1)
                    wait(dve, inv_ready, b1, 2, 2)
                    dve.tensor_scalar(attn[:, b1.par, :], attn[:, b1.par, :], inv[:, b1.par:b1.par + 1], None,
                                      ALU.mult).then_inc(attn_ready, 1)
                if b0:
                    wait(dve, vk_done, b0, 1, 1)
                    wait(dve, s_done, b0, 1, -1)
                    dve.tensor_tensor(vkT[:, b0.par, :, :], vk_ps[:, 0:D].rearrange("p (c t) -> p c t", c=DC),
                                      b_vk[:, :].unsqueeze(2).to_broadcast([P, DC, P]), ALU.add)\
                       .then_inc(vk_ready, 1)
                if b1:
                    wait(dve, l_done, b1, 1, 1)
                    wait(dve, out_done, b1, 1, -1)
                    dve.tensor_tensor(lv[:, b1.par, :], l_ps[:, 0:D], b_lv[:, :], ALU.add).then_inc(lv_ready, 1)
                if b0:
                    wait(dve, lk_done, b0, 1, 1)
                    dve.tensor_tensor(lkT[:, b0.par, :, :], lk_ps[:, 0:D].rearrange("p (c t) -> p c t", c=DC),
                                      b_lk[:, :].unsqueeze(2).to_broadcast([P, DC, P]), ALU.add)\
                       .then_inc(lk_ready, 1)
                    wait(dve, vv_done, b0, 1, 1)
                    wait(dve, l_done, b0, 1, -1)
                    dve.tensor_tensor(vv[:, b0.par, :], vv_ps[:, 0:D], b_vv[:, :], ALU.add).then_inc(vv_ready, 1)
            pipeline(dve, count, 3, step)

        @block.gpsimd
        def _(pool):
            def step(at):
                b2 = at(2)
                if b2:
                    wait(pool, xo_ready, b2, 1, 1)
                    pool.dma_start(x_out[b2.n], x_o[:, b2.par, :]).then_inc(stored[b2.par], 16)
            pipeline(pool, count, 3, step)


MAGIC = 12582912.0
TAPS = 3


def quantised_ffn(nc, x_in, x_out, mean, rstd, ident, ident_b, weights, count=NB):
    name = "qf"
    with ExitStack() as ctx:
        def sb(n, shape, dt=F32):
            return ctx.enter_context(nc.sbuf_tensor(f"{name}_{n}", shape, dt))

        def ps(n, shape, dt=F32):
            return ctx.enter_context(nc.psum_tensor(f"{name}_ps_{n}", shape, dt))

        sem = Semaphores(nc, ctx, name)

        w1, w2, conv_w, bias = (weights[key] for key in ("w1", "w2", "conv_w", "conv_b"))
        w1_q, w2_q = sb("w1_q", [P, DC, HID], BF16), sb("w2_q", [P, HC, D], BF16)
        diag = sb("diag", [P, TAPS, HC, P])
        bias_p = sb("bias_p", [1, 3, HID], BF16)
        bias3 = sb("bias3", [3, HID], BF16)
        ones3 = sb("ones3", [3, P], BF16)
        ones = sb("ones", [P, P])
        w_sum, w_mean, w_inv, factor = sb("w_sum", [P, 2]), sb("w_mean", [P, 2]), sb("w_inv", [P, 2]), sb("factor", [P, 2])
        x_t, x_r, xn, rounded, x_o = (sb(n, [P, 2, D]) for n in ("x_t", "x_r", "xn", "rounded", "x_o"))
        q1 = sb("q1", [P, 2, D])
        q1T = sb("q1T", [P, 2, DC, P], BF16)
        peak1, step1, inv1, fac1 = (sb(n, [P, 2]) for n in ("peak1", "step1", "inv1", "fac1"))
        peak2, step2, inv2, fac2 = (sb(n, [P, 2]) for n in ("peak2", "step2", "inv2", "fac2"))
        fac_row = sb("fac_row", [P, 2, P])
        h_pad = sb("h_pad", [P, 2, HC, P + 2])
        t_h = sb("t_h", [P, 2, 512])
        sT = sb("sT", [P, HC, P])
        rounded2 = sb("rounded2", [P, HID])
        q2 = sb("q2", [P, 2, HID], BF16)
        q2T = sb("q2T", [P, HC, P], BF16)
        h_ps, z_ps, st_ps = ps("h", [P, 2, 512]), ps("z", [P, 2, 512]), ps("st", [P, 2, 512])
        q2_ps = ps("q2", [P, HC, P], BF16)
        m_ps = ps("m", [P, 512])
        f_ps, q1_ps, o_ps = m_ps[:, 0:P], m_ps[:, P:P + D], m_ps[:, 0:D]

        pool_step, inverses_ready, diag_ready, w2_ready = (
            sem(n) for n in ("pool_step", "inverses_ready", "diag_ready", "w2_ready"))
        w_step, sums_ready, sum_done, weights_ready, bias_ready, bias_stacked, pads_ready = (
            sem(n) for n in ("w_step", "sums_ready", "sum_done", "weights_ready", "bias_ready",
                             "bias_stacked", "pads_ready"))
        x_loaded, r_loaded = ([sem(f"{n}{i}") for i in range(2)] for n in ("x_loaded", "r_loaded"))
        stored = [sem.kept("stored0"), sem.kept("stored1")]
        small, xn_ready, round1_ready, q1_ready, q1t_done, q1T_ready, fac1_ready, f_ready = (
            sem(n) for n in ("small", "xn_ready", "round1_ready", "q1_ready", "q1t_done", "q1T_ready", "fac1_ready",
                             "f_ready"))
        h_done, h_ready, z_done, tanh_ready, s_ready, st_done, small2, round2_ready, q2_ready = (
            sem(n) for n in ("h_done", "h_ready", "z_done", "tanh_ready", "s_ready", "st_done", "small2",
                             "round2_ready", "q2_ready"))
        scaled1, scaled2 = sem("scaled1"), sem("scaled2")
        q2t_done, q2T_ready, o_done, xo_ready = (sem(n) for n in ("q2t_done", "q2T_ready", "o_done", "xo_ready"))
        block = ctx.enter_context(nc.Block())

        def loaded(eng, sems, b):
            eng.wait_ge(sems[b.par], (b.n + (2 - b.par)) * 8)

        @block.sync
        def _(sp):
            sp.wait_ge(bias_ready, 1)
            for part in range(3):
                sp.dma_start(bias3[part:part + 1, :], bias_p[:, part, :]).then_inc(bias_stacked, 16)

            def step(at):
                b0, b2, b3 = at(0), at(2), at(3)
                if b0:
                    wait(sp, xn_ready, b0, 1, -1)
                    sp.dma_start(x_t[:, b0.par, :], x_in[b0.n]).then_inc(x_loaded[b0.par], 16)
                if b2:
                    wait(sp, xo_ready, b2, 1, -1)
                    sp.dma_start(x_r[:, b2.par, :], x_in[b2.n]).then_inc(r_loaded[b2.par], 16)
                if b3:
                    wait(sp, xo_ready, b3, 1, 1)
                    sp.dma_start(x_out[b3.n], x_o[:, b3.par, :]).then_inc(stored[b3.par], 16)
            pipeline(sp, count, 4, step)
            for par in range(2):
                sp.wait_ge(stored[par], 16 * (count // 2))

        @block.tensor
        def _(pe):
            pe.wait_ge(sums_ready, 1)
            pe.matmul(m_ps[:, 0:2], ones[:, :], w_sum[:, :], start=True, stop=True).then_inc(sum_done, 1)
            pe.wait_ge(weights_ready, 1)

            def convolve(b, j):
                if b.known() and b.n == 0:
                    pe.wait_ge(bias_stacked, 48)
                    pe.wait_ge(diag_ready, 1)
                wait(pe, h_ready, b, 2, j + 1)
                wait(pe, s_ready, b, 2, j - 1)
                for c in range(4 * j, 4 * j + 4):
                    out = z_ps[:, j, P * (c % 4):P * (c % 4) + P]
                    for tap in range(TAPS):
                        pe.matmul(out, diag[:, tap, c, :], h_pad[:, b.par, c, tap:tap + P],
                                  start=(tap == 0), stop=False)
                    last = pe.matmul(out, bias3[:, P * c:P * c + P], ones3[:, :], start=False, stop=True)
                last.then_inc(z_done, 1)

            def silu_transpose(b, j):
                wait(pe, s_ready, b, 2, j + 1)
                if j == 0:
                    wait(pe, round2_ready, b, 1, 0)
                for c in range(4 * j, 4 * j + 4):
                    last = pe.transpose(st_ps[:, j, P * (c % 4):P * (c % 4) + P], sT[:, c, :], ident[:, :])
                if j == 1:
                    last.then_inc(st_done, 1)

            def step(at):
                b0, b1, b2 = at(0), at(1), at(2)
                if b1:
                    convolve(b1, 0)
                    convolve(b1, 1)
                if b2:
                    wait(pe, q2_ready, b2, 1, 1)
                    wait(pe, q2T_ready, b2, 1, 0)
                    for c in range(HC):
                        last = pe.transpose(q2_ps[:, c, :], q2[:, b2.par, P * c:P * c + P], ident_b[:, :])
                    last.then_inc(q2t_done, 1)
                if b1:
                    silu_transpose(b1, 0)
                if b0:
                    wait(pe, q1_ready, b0, 1, 1)
                    wait(pe, fac1_ready, b0, 1, 1)
                    wait(pe, xo_ready, b0, 1, -2)
                    for c in range(DC):
                        pe.transpose(q1_ps[:, P * c:P * c + P], q1[:, b0.par, P * c:P * c + P], ident[:, :])
                    pe.transpose(f_ps, fac1[:, b0.par:b0.par + 1].to_broadcast([P, P]), ident[:, :])\
                      .then_inc(q1t_done, 1)
                if b1:
                    silu_transpose(b1, 1)
                if b0:
                    wait(pe, q1T_ready, b0, 1, 1)
                    for j in range(2):
                        wait(pe, h_ready, b0, 2, j - 1)
                        for m in range(4 * j, 4 * j + 4):
                            for c in range(DC):
                                last = pe.matmul(h_ps[:, j, P * (m % 4):P * (m % 4) + P], w1_q[:, c, P * m:P * m + P],
                                                 q1T[:, b0.par, c, :], start=(c == 0), stop=(c == DC - 1))
                        last.then_inc(h_done, 1)
                if b2:
                    wait(pe, q2T_ready, b2, 1, 1)
                    if b2.known() and b2.n == 0:
                        pe.wait_ge(w2_ready, 1)
                    wait(pe, xo_ready, b2, 1, 0)
                    if b0:
                        wait(pe, f_ready, b0, 1, 1)
                    for c in range(HC):
                        last = pe.matmul(o_ps, q2T[:, c, :], w2_q[:, c, :], start=(c == 0), stop=(c == HC - 1))
                    last.then_inc(o_done, 1)
            pipeline(pe, count, 3, step)

        @block.scalar
        def _(act):
            def silu_tanh(b, j):
                wait(act, z_done, b, 2, j + 1)
                wait(act, s_ready, b, 2, j - 1)
                act.activation(t_h[:, j, :], z_ps[:, j, :], ACT.Tanh, scale=0.5).then_inc(tanh_ready, 1)

            def step(at):
                b0, b1, b2 = at(0), at(1), at(2)
                if b1:
                    silu_tanh(b1, 0)
                if b2:
                    wait(act, round2_ready, b2, 1, 1)
                    wait(act, q2t_done, b2, 1, -1)
                    act.activation(q2[:, b2.par, :], rounded2[:, :], ACT.Copy, bias=-MAGIC, scale=1.0)\
                       .then_inc(q2_ready, 1)
                if b1:
                    silu_tanh(b1, 1)
                if b0:
                    wait(act, round1_ready, b0, 1, 1)
                    wait(act, q1t_done, b0, 1, -1)
                    act.activation(q1[:, b0.par, :], rounded[:, b0.par, :], ACT.Copy, bias=-MAGIC, scale=1.0)\
                       .then_inc(q1_ready, 1)
                    wait(act, q1t_done, b0, 1, 1)
                    wait(act, h_done, b0, 2, -2)
                    act.copy(q1T[:, b0.par, :, :], q1_ps.rearrange("p (c t) -> p c t", c=DC)).then_inc(q1T_ready, 1)
                    wait(act, h_ready, b0, 2, -2)
                    act.copy(fac_row[:, b0.par, :], f_ps).then_inc(f_ready, 1)
                if b2:
                    wait(act, q2t_done, b2, 1, 1)
                    wait(act, o_done, b2, 1, 0)
                    act.copy(q2T[:, :, :], q2_ps[:, :, :]).then_inc(q2T_ready, 1)
            pipeline(act, count, 3, step)

        @block.vector
        def _(dve):
            done = [0]

            def link(instruction):
                done[0] += 1
                instruction.then_inc(w_step, 1)
                dve.wait_ge(w_step, done[0])

            link(dve.memset(ones[:, :], 1.0))
            weights.wait(dve)
            link(dve.tensor_reduce(w_sum[:, 0:1], w1[:, :], AX.X, ALU.add, apply_absolute_value=True))
            link(dve.tensor_reduce(w_sum[:, 1:2], w2[:, :], AX.X, ALU.add, apply_absolute_value=True))
            dve.sem_inc(sums_ready, 1)
            for part in range(3):
                link(dve.tensor_copy(bias_p[:, part, :], bias[:, :]))
                if part < 2:
                    link(dve.tensor_tensor(bias[:, :], bias[:, :], bias_p[:, part, :], ALU.subtract))
            dve.sem_inc(bias_ready, 1)
            dve.wait_ge(sum_done, 1)
            link(dve.tensor_scalar(w_mean[:, :], m_ps[:, 0:2], 1.0 / (D * HID), 1e-5, ALU.mult, ALU.max))
            link(dve.reciprocal(w_inv[:, :], w_mean[:, :]))
            dve.sem_inc(inverses_ready, 1)
            link(dve.tensor_scalar(w1[:, :], w1[:, :], w_inv[:, 0:1], None, ALU.mult))
            link(dve.tensor_scalar(w1[:, :], w1[:, :], MAGIC, MAGIC, ALU.add, ALU.subtract))
            link(dve.tensor_scalar(w1_q[:, :, :].rearrange("p a b -> p (a b)"), w1[:, :], 1.0, -1.0, ALU.min, ALU.max))
            link(dve.tensor_copy(factor[:, 0:1], w_mean[:, 0:1]))
            link(dve.tensor_scalar(factor[:, 1:2], w_mean[:, 1:2], 0.5, None, ALU.mult))
            dve.sem_inc(weights_ready, 1)

            def scales(src, par, floor, peak, stp, inv, fac, factor_col, sem_, b):
                dve.tensor_reduce(peak[:, par:par + 1], src, AX.X if len(src.shape) == 2 else AX.XY, ALU.max,
                                  apply_absolute_value=True).then_inc(sem_, 1)
                wait(dve, sem_, b, 3, 1)
                dve.tensor_scalar(stp[:, par:par + 1], peak[:, par:par + 1], floor, 1.0 / 127.0, ALU.max, ALU.mult)\
                   .then_inc(sem_, 1)
                wait(dve, sem_, b, 3, 2)
                dve.reciprocal(inv[:, par:par + 1], stp[:, par:par + 1]).then_inc(sem_, 1)
                return dve.tensor_scalar(fac[:, par:par + 1], stp[:, par:par + 1], factor[:, factor_col:factor_col + 1],
                                         None, ALU.mult)

            def silu(b, j):
                wait(dve, tanh_ready, b, 2, j + 1)
                wait(dve, st_done, b, 1, 0)
                dve.scalar_tensor_tensor(
                    out=sT[:, 4 * j:4 * j + 4, :].rearrange("p c t -> p (c t)"), in0=t_h[:, j, :],
                    scalar=1.0, in1=z_ps[:, j, :], op0=ALU.add, op1=ALU.mult).then_inc(s_ready, 1)

            def step(at):
                b0, b1, b2, b3 = at(0), at(1), at(2), at(3)
                if b1:
                    wait(dve, f_ready, b1, 1, 1)
                    if b1.known() and b1.n == 0:
                        dve.wait_ge(pads_ready, 1)
                    wait(dve, z_done, b1, 2, -2)
                    for j in range(2):
                        wait(dve, h_done, b1, 2, j + 1)
                        dve.tensor_tensor(h_pad[:, b1.par, 4 * j:4 * j + 4, 1:P + 1],
                                          h_ps[:, j, :].rearrange("p (c t) -> p c t", c=4),
                                          fac_row[:, b1.par, :].unsqueeze(1).to_broadcast([P, 4, P]),
                                          ALU.mult).then_inc(h_ready, 1)
                if b2:
                    wait(dve, st_done, b2, 1, 1)
                    scales(st_ps[:, :, :], b2.par, 2e-5, peak2, step2, inv2, fac2, 1, small2, b2)
                    wait(dve, small2, b2, 3, 3)
                    wait(dve, q2_ready, b2, 1, 0)
                    dve.tensor_scalar(rounded2[:, :], st_ps[:, :, :].rearrange("p a b -> p (a b)"),
                                      inv2[:, b2.par:b2.par + 1], MAGIC, ALU.mult, ALU.add).then_inc(scaled2, 1)
                    wait(dve, scaled2, b2, 1, 1)
                    dve.tensor_scalar(rounded2[:, :], rounded2[:, :], MAGIC + 127.0, MAGIC - 128.0,
                                      ALU.min, ALU.max).then_inc(round2_ready, 1)
                if b3:
                    wait(dve, o_done, b3, 1, 1)
                    loaded(dve, r_loaded, b3)
                    if not b3.known() or b3.n >= 2:
                        dve.wait_ge(stored[b3.par], (b3.n - b3.par) * 8)
                    dve.scalar_tensor_tensor(out=x_o[:, b3.par, :], in0=o_ps, scalar=fac2[:, b3.par:b3.par + 1],
                                             in1=x_r[:, b3.par, :], op0=ALU.mult, op1=ALU.add).then_inc(xo_ready, 1)
                if b1:
                    silu(b1, 0)
                if b0:
                    loaded(dve, x_loaded, b0)
                    dve.tensor_scalar(xn[:, b0.par, :], x_t[:, b0.par, :], mean[:, bass.ds(b0.n, 1)],
                                      rstd[:, bass.ds(b0.n, 1)], ALU.subtract, ALU.mult).then_inc(xn_ready, 1)
                    wait(dve, xn_ready, b0, 1, 1)
                    wait(dve, q1t_done, b0, 1, -1)
                    scales(xn[:, b0.par, :], b0.par, 1e-5, peak1, step1, inv1, fac1, 0, small, b0)\
                        .then_inc(fac1_ready, 1)
                    wait(dve, small, b0, 3, 3)
                    dve.tensor_scalar(xn[:, b0.par, :], xn[:, b0.par, :], inv1[:, b0.par:b0.par + 1], MAGIC,
                                      ALU.mult, ALU.add).then_inc(scaled1, 1)
                    wait(dve, scaled1, b0, 1, 1)
                    wait(dve, q1_ready, b0, 1, -1)
                    dve.tensor_scalar(rounded[:, b0.par, :], xn[:, b0.par, :], MAGIC + 127.0, MAGIC - 128.0,
                                      ALU.min, ALU.max).then_inc(round1_ready, 1)
                if b1:
                    silu(b1, 1)
            pipeline(dve, count, 4, step)

        @block.gpsimd
        def _(pool):
            link = chained(pool, pool_step)
            link(pool.memset(ones3[:, :], 1.0))
            weights.wait(pool)
            link(pool.memset(h_pad[:, :, :, :], 0.0))
            pool.sem_inc(pads_ready, 1)
            link(pool.tensor_tensor(diag[:, :, :, :].rearrange("p a c t -> p (a c) t"),
                                    ident[:, :].unsqueeze(1).to_broadcast([P, TAPS * HC, P]),
                                    conv_w[:, :, :].rearrange("p a c -> p (a c)").unsqueeze(2).to_broadcast([P, TAPS * HC, P]),
                                    ALU.mult))
            pool.sem_inc(diag_ready, 1)
            pool.wait_ge(inverses_ready, 1)
            link(pool.tensor_scalar(w2[:, :], w2[:, :], w_inv[:, 1:2], None, ALU.mult))
            link(pool.tensor_scalar(w2[:, :], w2[:, :], MAGIC, MAGIC, ALU.add, ALU.subtract))
            link(pool.tensor_scalar(w2_q[:, :, :].rearrange("p a b -> p (a b)"), w2[:, :], 1.0, -1.0, ALU.min, ALU.max))
            pool.sem_inc(w2_ready, 1)


def decoder(nc, ins, scratch, x_out):
    with ExitStack() as ctx:
        def sb(n, shape, dt=F32):
            return ctx.enter_context(nc.sbuf_tensor(n, shape, dt))

        ident, ident_b = sb("ident", [P, P]), sb("ident_b", [P, P], BF16)
        mean, rstd, rms_scale = sb("mean", [P, NB]), sb("rstd", [P, NB]), sb("rms_scale", [P, NB])
        stats = sb("stats", [P, NB, 6])
        consts_loaded = ctx.enter_context(nc.semaphore("consts_loaded"))
        with nc.Block() as block:
            @block.sync
            def _(sp):
                sp.dma_start(ident[:, :], ins["ident"]).then_inc(consts_loaded, 16)
                sp.dma_start(ident_b[:, :], ins["ident_b"]).then_inc(consts_loaded, 16)
                sp.wait_ge(consts_loaded, 32)

        def part(prefix):
            return {n[len(prefix):]: ap for n, ap in {**ins, **scratch}.items() if n.startswith(prefix)}

        x = [ins["x"]] + [scratch[f"x{i}"] for i in range(1, 5)] + [x_out]

        with ExitStack() as opening:
            block = opening.enter_context(nc.Block())
            alibi_rows(nc, opening, block, ins["q_pos"], ins["k_pos"], ins["slope_rows"],
                       scratch["alibi_q"], scratch["alibi_k"])
            latent_weights(nc, opening, block, part("latent_"), part("self_"))
            first_statistics(nc, opening, block, x[0], stats)
        with ExitStack() as early:
            self_w = Weights(nc, early, "self", part("self_"), ATTENTION_WEIGHTS)
            cross_w = Weights(nc, early, "cross", part("cross_"), ATTENTION_WEIGHTS)
            norm_scales(nc, "norm0", stats, mean, rstd, ahead=[self_w])
            attention(nc, "self", False, x[0], x[1], None, None, None, stats, mean, rstd, ident, ident_b,
                      self_w, ahead=[cross_w])
            norm_scales(nc, "norm1", stats, mean, rstd)
            attention(nc, "cross", True, x[1], x[2], ins["ctx"], ins["mask"],
                      dict(q=scratch["alibi_q"], k=scratch["alibi_k"], slopes=ins["slope_parts"]),
                      stats, mean, rstd, ident, ident_b, cross_w)
        norm_scales(nc, "norm2", stats, mean, rstd)
        mix_w = Weights(nc, ctx, "mix", part("mix_"), ("w_in", "w_out", "w_fc", "w_pr", "norm1", "norm2"))
        experts_ffn(nc, x[2], mean, rstd, ident, part("moe_"), scratch["sorted_x"], ahead=[mix_w])
        with ExitStack() as joined:
            first_statistics(nc, joined, joined.enter_context(nc.Block()), x[2], stats, name="joined")
        norm_scales(nc, "norm3", stats, mean, rstd, rms_scale=rms_scale)
        vis_w = Weights(nc, ctx, "vis", part("vis_"), ("w_vk", "w_lk", "w_vv", "w_lv", "b_vk", "b_lk", "b_vv", "b_lv"))
        q_w = Weights(nc, ctx, "q", part("q_"), ("w1", "w2", "conv_w", "conv_b"))
        mixer(nc, x[2], x[3], stats, mean, rstd, rms_scale, ident, mix_w, ahead=[vis_w, q_w])
        norm_scales(nc, "norm4", stats, mean, rstd)
        cross_values(nc, x[3], x[4], ins["ctx"], stats, mean, rstd, ident, vis_w)
        norm_scales(nc, "norm5", stats, mean, rstd)
        quantised_ffn(nc, x[4], x[5], mean, rstd, ident, ident_b, q_w)


def by_chunks(w):
    return w.reshape(w.shape[0] // P, P, w.shape[1]).transpose(1, 0, 2)


def column(v):
    return v.reshape(-1, P).T


def rows(v):
    return np.broadcast_to(v.reshape(-1), (P, v.size))


def kernel(**inputs):
    import concourse.bacc as bacc
    import ml_dtypes
    from concourse.bass_utils import run_bass_kernel_spmd

    inp = {name: np.asarray(a) for name, a in inputs.items()}
    bf16 = ml_dtypes.bfloat16

    slope = np.asarray([(2.0 ** (-8.0 / HEADS)) ** i for i in range(1, HEADS + 1)], np.float32)
    slope_parts, rest = [], slope
    for _ in range(3):
        slope_parts.append(rest.astype(bf16))
        rest = rest - slope_parts[-1].astype(np.float32)
    negated = np.stack([np.repeat(-part, P) for part in slope_parts])
    head_mask = (np.arange(P)[:, None] // HD == np.arange(P // HD)[None, :]).astype(np.float32)
    tiles = expert_tiles(NB)
    zeros = np.zeros(D, np.float32)
    padding = np.zeros((P, WIDE), np.float32)
    padding[:, D + 1] = NB * P + np.arange(P)

    lay = {
        "x": inp["x"], "ctx": inp["ctx_1024"], "mask": inp["mask_BxSxS2_if1"],
        "q_pos": inp["itok_BxS_8_8191"], "k_pos": inp["itok_BxS2_1_8191"],
        "ident": np.eye(P, dtype=np.float32), "ident_b": np.eye(P, dtype=np.float32).astype(bf16),
        "slope_rows": np.broadcast_to(slope, (NB, HEADS)), "slope_parts": np.tile(negated, (3, 1)),

        "latent_down": inp["L0_attn_Wl"].T,
        "latent_up": np.concatenate([inp["L0_attn_Wk"], inp["L0_attn_Wv"]], 1),
        "latent_bl": inp["L0_attn_bl"].reshape(LATENT, 1),
        "latent_bk": column(inp["L0_attn_bk"]), "latent_bv": rows(inp["L0_attn_bv"]),
        "self_wq": by_chunks(inp["L0_attn_Wq"]), "self_wo": by_chunks(inp["L0_attn_Wo"]),
        "self_bq": column(inp["L0_attn_bq"]), "self_bo": rows(inp["L0_attn_bo"]), "self_head_mask": head_mask,

        "cross_wq": by_chunks(inp["L0_xattn_W_q"].T), "cross_wk": by_chunks(inp["L0_xattn_W_k"].T),
        "cross_wv": by_chunks(inp["L0_xattn_W_v"].T), "cross_wo": by_chunks(inp["L0_xattn_W_o"].T),
        "cross_bq": column(zeros), "cross_bk": column(zeros), "cross_bv": rows(zeros), "cross_bo": rows(zeros),
        "cross_head_mask": head_mask,

        "moe_wr": by_chunks(inp["L0_ffn_Wr"]), "moe_br": rows(inp["L0_ffn_br"]),
        "moe_w1": inp["L0_ffn_W1"].reshape(EXPERTS, DC, P, HID).transpose(2, 0, 1, 3),
        "moe_w2": inp["L0_ffn_W2"].reshape(EXPERTS, HC, P, D).transpose(2, 0, 1, 3),
        "moe_b1": inp["L0_ffn_b1"].reshape(EXPERTS * HC, P).T, "moe_b2": rows(inp["L0_ffn_b2"]),
        "moe_falling": rows(np.arange(EXPERTS, 0, -1).astype(np.float32)),
        "moe_before": np.triu(np.ones((P, P), np.float32), 1).astype(bf16), "moe_ones": np.ones((P, P), bf16),
        "moe_tile_no": np.arange(tiles, dtype=np.float32)[None],
        "moe_base": rows(np.arange(EXPERTS, dtype=np.float32) * expert_rows(NB)),
        "moe_token_no": np.arange(NB * P, dtype=np.float32).reshape(NB, P).T, "moe_padding": padding,

        "mix_w_in": by_chunks(inp["L1_attn_in_proj_w"].T), "mix_w_out": by_chunks(inp["L1_attn_out_proj_w"].T),
        "mix_w_fc": by_chunks(inp["L1_attn_fc_w"].T), "mix_w_pr": by_chunks(inp["L1_attn_proj_w"].T),
        "mix_norm1": column(inp["L1_attn_norm1_w"]), "mix_norm2": column(inp["L1_attn_norm2_w"]),

        "vis_w_vk": by_chunks(inp["L1_xattn_W_vk"].T), "vis_w_lk": by_chunks(inp["L1_xattn_W_lk"].T),
        "vis_w_vv": by_chunks(inp["L1_xattn_W_vv"].T), "vis_w_lv": by_chunks(inp["L1_xattn_W_lv"].T),
        "vis_b_vk": column(inp["L1_xattn_b_vk"]), "vis_b_lk": column(inp["L1_xattn_b_lk"]),
        "vis_b_vv": rows(inp["L1_xattn_b_vv"]), "vis_b_lv": rows(inp["L1_xattn_b_lv"]),

        "q_w1": by_chunks(inp["L1_ffn_w1"].T).reshape(P, -1), "q_w2": by_chunks(inp["L1_ffn_w2"].T).reshape(P, -1),
        "q_conv_w": inp["L1_ffn_conv_w"].reshape(HC, P, 3).transpose(1, 2, 0),
        "q_conv_b": inp["L1_ffn_conv_b"].reshape(1, HID),
    }

    nc = bacc.Bacc("TRN2", target_bir_lowering=False, num_devices=1)
    arrays, ins = {}, {}
    for name, a in lay.items():
        arrays[f"in_{name}"] = np.ascontiguousarray(a)
        ins[name] = nc.dram_tensor(f"in_{name}", list(a.shape), mybir.dt.from_np(a.dtype), kind="ExternalInput").ap()

    def internal(name, shape, dt=F32):
        return nc.dram_tensor(f"dram_{name}", shape, dt, kind="Internal").ap()

    scratch = {f"x{i}": internal(f"x{i}", [NB + (i == 2), P, D]) for i in range(1, 5)}
    scratch["self_wk"], scratch["self_wv"] = internal("self_wk", [P, DC, D]), internal("self_wv", [P, DC, D])
    scratch["self_bk"], scratch["self_bv"] = internal("self_bk", [P, DC]), internal("self_bv", [P, D])
    scratch["alibi_q"], scratch["alibi_k"] = internal("alibi_q", [12, NB, P], BF16), internal("alibi_k", [NB, 3, HEADS * P], BF16)
    scratch["sorted_x"] = internal("sorted_x", [sorted_rows(NB), WIDE])
    x_out = nc.dram_tensor("x_out", [NB, P, D], F32, kind="ExternalOutput").ap()
    decoder(nc, ins, scratch, x_out)
    return run_bass_kernel_spmd(nc, [arrays], core_ids=[0]).results[0]["x_out"]
```
